# Optimizing a Trainium2 kernel written in Bass

```python
import numpy as np
import jax
import jax.numpy as jnp

def _softmax(x, axis=-1):
    return jax.nn.softmax(x, axis=axis)

def _gelu(x):
    return jax.nn.gelu(x, approximate=True)

def _silu(x):
    return jax.nn.silu(x)

def _sigmoid(x):
    return jax.nn.sigmoid(x)

def _layernorm(x, axis=-1, eps=1e-05):
    m = jnp.mean(x, axis=axis, keepdims=True)
    v = jnp.var(x, axis=axis, keepdims=True)
    return (x - m) / jnp.sqrt(v + eps)

def _scatter_add(tgt, idx, src, axis=0):
    return tgt.at[idx].add(src)

def _segment_sum(src, seg, n):
    return jax.ops.segment_sum(src, seg, n)
kernel_name = 'mk_prb_d1_jaxref_r4_d312bd'

def setup_inputs(seed: int=0):
    np.random.seed(seed)
    _w = jnp.asarray

    def _L0_attn_setup():
        import jax, jax.numpy as jnp
        import numpy as np
        MODEL_DIM = 256
        NUM_HEADS = 16
        HEAD_DIM = MODEL_DIM // NUM_HEADS
        ROPE_PERIOD = 10000.0

        def _rope_cos_sin(seq_len, dim, dtype):
            inv_freq = 1.0 / ROPE_PERIOD ** (jnp.arange(0, dim, 2, dtype=jnp.float32) / dim)
            t = jnp.arange(seq_len, dtype=jnp.float32)
            freqs = jnp.outer(t, inv_freq)
            emb = jnp.concatenate([freqs, freqs], axis=-1)
            return (jnp.cos(emb).astype(dtype), jnp.sin(emb).astype(dtype))

        def _rope_embed(x):
            S, D = (x.shape[-2], x.shape[-1])
            cos, sin = _rope_cos_sin(S, D, x.dtype)
            x1 = x[..., :D // 2]
            x2 = x[..., D // 2:]
            rotated = jnp.concatenate([-x2, x1], axis=-1)
            return x * cos + rotated * sin
        key = jax.random.key(seed)
        kx, kq, kk, kv, ko = jax.random.split(key, 5)
        std = 0.02
        return {'x': jax.random.normal(kx, (2, 512, MODEL_DIM), dtype=jnp.float32), 'Wq': std * jax.random.normal(kq, (MODEL_DIM, MODEL_DIM), dtype=jnp.float32), 'Wk': std * jax.random.normal(kk, (MODEL_DIM, MODEL_DIM), dtype=jnp.float32), 'Wv': std * jax.random.normal(kv, (MODEL_DIM, MODEL_DIM), dtype=jnp.float32), 'Wo': std * jax.random.normal(ko, (MODEL_DIM, MODEL_DIM), dtype=jnp.float32)}
    _L0_attn_in = _L0_attn_setup()

    def _L0_ffn_setup():
        import jax, jax.numpy as jnp
        import numpy as np
        NUM_COLUMNS = 16
        INPUT_DIM = 256
        NUM_NEURONS = 64
        SPARSITY = 0.05
        B, S = (4, 512)

        def _l2norm(v, axis=-1, eps=1e-12):
            n = jnp.sqrt(jnp.sum(v * v, axis=axis, keepdims=True))
            return v / jnp.maximum(n, eps)
        key = jax.random.key(seed)
        ks = jax.random.split(key, 12)
        D, C, N = (INPUT_DIM, NUM_COLUMNS, NUM_NEURONS)
        inp = {'x': jax.random.normal(ks[0], (B, S, D), dtype=jnp.float32), 'col_emb': jax.random.normal(ks[1], (C, D), dtype=jnp.float32) * 0.02, 'gate_w1': jax.random.normal(ks[2], (D, D // 2), dtype=jnp.float32) / np.sqrt(D), 'gate_b1': jnp.zeros((D // 2,), dtype=jnp.float32), 'gate_w2': jax.random.normal(ks[3], (D // 2, C), dtype=jnp.float32) / np.sqrt(D // 2), 'gate_b2': jnp.zeros((C,), dtype=jnp.float32), 'W_cols': jax.random.normal(ks[4], (C, D, N), dtype=jnp.float32) / np.sqrt(D), 'b_cols': jnp.zeros((C, N), dtype=jnp.float32), 'proj_w': jax.random.normal(ks[5], (C * N, D), dtype=jnp.float32) / np.sqrt(C * N), 'proj_b': jnp.zeros((D,), dtype=jnp.float32), 'ln_g': jnp.ones((D,), dtype=jnp.float32), 'ln_b': jnp.zeros((D,), dtype=jnp.float32)}
        return inp
    _L0_ffn_in = _L0_ffn_setup()
    _d = {'L0_attn_x': _L0_attn_in['x'], 'L0_attn_Wq': _L0_attn_in['Wq'], 'L0_attn_Wk': _L0_attn_in['Wk'], 'L0_attn_Wv': _L0_attn_in['Wv'], 'L0_attn_Wo': _L0_attn_in['Wo'], 'L0_ffn_col_emb': _L0_ffn_in['col_emb'], 'L0_ffn_gate_w1': _L0_ffn_in['gate_w1'], 'L0_ffn_gate_b1': _L0_ffn_in['gate_b1'], 'L0_ffn_gate_w2': _L0_ffn_in['gate_w2'], 'L0_ffn_gate_b2': _L0_ffn_in['gate_b2'], 'L0_ffn_W_cols': _L0_ffn_in['W_cols'], 'L0_ffn_b_cols': _L0_ffn_in['b_cols'], 'L0_ffn_proj_w': _L0_ffn_in['proj_w'], 'L0_ffn_proj_b': _L0_ffn_in['proj_b'], 'L0_ffn_ln_g': _L0_ffn_in['ln_g'], 'L0_ffn_ln_b': _L0_ffn_in['ln_b']}
    _x0 = _d['L0_attn_x']
    _d['L0_attn_x'] = jax.random.normal(jax.random.fold_in(jax.random.key(seed), 1), (8, 1024, 256), dtype=_x0.dtype)
    del _x0
    return _d

def reference(L0_attn_x, L0_attn_Wq, L0_attn_Wk, L0_attn_Wv, L0_attn_Wo, L0_ffn_col_emb, L0_ffn_gate_w1, L0_ffn_gate_b1, L0_ffn_gate_w2, L0_ffn_gate_b2, L0_ffn_W_cols, L0_ffn_b_cols, L0_ffn_proj_w, L0_ffn_proj_b, L0_ffn_ln_g, L0_ffn_ln_b):

    def _L0_attn_ref(x, Wq, Wk, Wv, Wo):
        import jax, jax.numpy as jnp
        import numpy as np
        MODEL_DIM = 256
        NUM_HEADS = 16
        HEAD_DIM = MODEL_DIM // NUM_HEADS
        ROPE_PERIOD = 10000.0

        def _rope_cos_sin(seq_len, dim, dtype):
            inv_freq = 1.0 / ROPE_PERIOD ** (jnp.arange(0, dim, 2, dtype=jnp.float32) / dim)
            t = jnp.arange(seq_len, dtype=jnp.float32)
            freqs = jnp.outer(t, inv_freq)
            emb = jnp.concatenate([freqs, freqs], axis=-1)
            return (jnp.cos(emb).astype(dtype), jnp.sin(emb).astype(dtype))

        def _rope_embed(x):
            S, D = (x.shape[-2], x.shape[-1])
            cos, sin = _rope_cos_sin(S, D, x.dtype)
            x1 = x[..., :D // 2]
            x2 = x[..., D // 2:]
            rotated = jnp.concatenate([-x2, x1], axis=-1)
            return x * cos + rotated * sin
        B, S, Dm = x.shape
        H, Dh = (NUM_HEADS, HEAD_DIM)
        q = (x @ Wq.T).reshape(B, S, H, Dh).transpose(0, 2, 1, 3)
        k = (x @ Wk.T).reshape(B, S, H, Dh).transpose(0, 2, 1, 3)
        v = (x @ Wv.T).reshape(B, S, H, Dh).transpose(0, 2, 1, 3)
        q = _rope_embed(q)
        k = _rope_embed(k)
        scores = jnp.einsum('bhqd,bhkd->bhqk', q, k) / jnp.sqrt(jnp.asarray(Dh, x.dtype))
        neg_inf = jnp.finfo(x.dtype).min
        causal = jnp.triu(jnp.full((S, S), neg_inf, dtype=x.dtype), k=1)
        scores = scores + causal
        attn = jax.nn.softmax(scores, axis=-1)
        out = jnp.einsum('bhqk,bhkd->bhqd', attn, v)
        out = out.transpose(0, 2, 1, 3).reshape(B, S, Dm)
        return out @ Wo.T

    def _L0_ffn_ref(x, col_emb, gate_w1, gate_b1, gate_w2, gate_b2, W_cols, b_cols, proj_w, proj_b, ln_g, ln_b):
        import jax, jax.numpy as jnp
        import numpy as np
        NUM_COLUMNS = 16
        INPUT_DIM = 256
        NUM_NEURONS = 64
        SPARSITY = 0.05
        B, S = (4, 512)

        def _l2norm(v, axis=-1, eps=1e-12):
            n = jnp.sqrt(jnp.sum(v * v, axis=axis, keepdims=True))
            return v / jnp.maximum(n, eps)
        Bq, Sq, D = x.shape
        C = col_emb.shape[0]
        similarity = jnp.einsum('bsd,cd->bsc', _l2norm(x), _l2norm(col_emb))
        h = jax.nn.gelu(x @ gate_w1 + gate_b1, approximate=False)
        gate_values = jax.nn.sigmoid(h @ gate_w2 + gate_b2)
        logits = similarity + gate_values
        k = max(1, int(C * SPARSITY))
        _, top_idx = jax.lax.top_k(logits, k)
        mask = jnp.sum(jax.nn.one_hot(top_idx, C, dtype=logits.dtype), axis=-2)
        weights = mask * jax.nn.softmax(logits, axis=-1)
        cols = jax.nn.gelu(jnp.einsum('bsd,cdn->bscn', x, W_cols) + b_cols, approximate=False)
        cols = cols * weights[..., None]
        combined = cols.reshape(Bq, Sq, -1)
        y = combined @ proj_w + proj_b + x
        mu = jnp.mean(y, axis=-1, keepdims=True)
        var = jnp.mean((y - mu) ** 2, axis=-1, keepdims=True)
        out = (y - mu) * jax.lax.rsqrt(var + 1e-05) * ln_g + ln_b
        return out
    x = L0_attn_x
    xn = _layernorm(x, axis=-1)
    x = x + _L0_attn_ref(xn, L0_attn_Wq, L0_attn_Wk, L0_attn_Wv, L0_attn_Wo) + _L0_ffn_ref(xn, L0_ffn_col_emb, L0_ffn_gate_w1, L0_ffn_gate_b1, L0_ffn_gate_w2, L0_ffn_gate_b2, L0_ffn_W_cols, L0_ffn_b_cols, L0_ffn_proj_w, L0_ffn_proj_b, L0_ffn_ln_g, L0_ffn_ln_b)
    return x

_drawn_inputs = setup_inputs


def setup_inputs(seed=0):
    import zlib

    import numpy as np

    out = dict(_drawn_inputs(seed))
    spreads = {'L0_ffn_gate_b1': (0.0, 0.8),
     'L0_ffn_gate_b2': (0.0, 2.0),
     'L0_ffn_b_cols': (0.0, 2.0),
     'L0_ffn_proj_b': (0.0, 0.644),
     'L0_ffn_ln_g': (1.0, 0.2),
     'L0_ffn_ln_b': (0.0, 0.438)}
    factors = {'L0_attn_Wq': 8.0,
     'L0_attn_Wk': 8.0,
     'L0_attn_Wv': 8.0,
     'L0_attn_Wo': 8.0,
     'L0_ffn_col_emb': 8.0,
     'L0_ffn_gate_w1': 8.0,
     'L0_ffn_gate_w2': 8.0,
     'L0_ffn_W_cols': 8.0,
     'L0_ffn_proj_w': 8.0}
    for name, (base, spread) in spreads.items():
        noise = np.random.default_rng([zlib.crc32(name.encode()), seed]).standard_normal(out[name].shape)
        drawn = base * np.exp(spread * noise) if base else spread * noise
        out[name] = jnp.asarray(drawn.astype(out[name].dtype))
    for name, factor in factors.items():
        out[name] = (out[name] * factor).astype(out[name].dtype)
    return out
```

```python
from contextlib import ExitStack

import numpy as np
import concourse.bass as bass
from concourse import mybir

FP32 = mybir.dt.float32
BF16 = mybir.dt.bfloat16
I32 = mybir.dt.int32
U32 = mybir.dt.uint32
ALU = mybir.AluOpType
ACT = mybir.ActivationFunctionType
AX = mybir.AxisListType

P = 128
BATCH, SEQ, DIM = 8, 1024, 256
HEADS = 16
HD = DIM // HEADS
TOK = BATCH * SEQ
TILES = TOK // P
COLS, NEUR, HID = 16, 64, 128
LN_EPS = 1e-5
SIGMOID_MIN = -87.0
MASKED = -3.0e38
NORM2_MIN = 1e-24

GROUP = 512
GT = GROUP // P
VA = HD + 1
QTILES = SEQ // P
UH = 4
UNITS = HEADS // UH
TERMS = ((0, 0), (0, 1), (1, 0), (0, 2), (2, 0), (1, 1))
KROWS = len(TERMS) * HD
SHIFT = KROWS
KALL = KROWS + 3
SLOTS = -(-((TOK + COLS * (P - 1)) // P) // 4) * 4


def over(eng, count, body):
    body(0, True, False)
    with eng.Fori(1, count - 1) as i:
        body(i, False, False)
    body(count - 1, False, True)


def over_batches(eng, body):
    over(eng, BATCH, body)


def wait(eng, sem, value):
    if isinstance(value, int) and value <= 0:
        return
    eng.wait_ge(sem, value)


def settle(eng, passed):
    eng.sem_inc(passed, 1)


def wait_apart(eng, sem, value, passed):
    wait(eng, sem, value)
    if not isinstance(value, int):
        settle(eng, passed)


def group_after(b, slot):
    return (b, 1) if slot == 0 else (b + 1, 0)


def group_before(b, slot):
    return (b, 0) if slot == 1 else (b - 1, 1)


def project(nc, d, keep):
    with ExitStack() as ctx:
        sb = lambda n, s, t=FP32: ctx.enter_context(nc.sbuf_tensor("p_" + n, s, t))
        pb = lambda n, s: ctx.enter_context(nc.psum_tensor("p_" + n, s, FP32))
        sem = lambda n: ctx.enter_context(nc.semaphore("p_" + n))

        ident = sb("ident", [P, P])
        w_qk = sb("w_qk", [P, 2, 2 * DIM])
        w_vs = sb("w_vs", [P, 2, DIM + COLS])
        w_g1 = sb("w_g1", [P, 2, HID])
        b_g1 = sb("b_g1", [P, 1])
        w_g2 = sb("w_g2", [P, COLS])
        rope_cos = sb("rope_cos", [P, 2, SEQ])
        rope_sin = sb("rope_sin", [P, 2, SEQ])
        zero_rows = sb("zero_rows", [P, DIM])
        x_in = sb("x_in", [P, 2, GT, DIM])
        xn = sb("xn", [P, 2, GT, DIM])
        stats = sb("stats", [P, GT, 6])
        mv = sb("mv", [P, GT, 2])
        rstd = sb("rstd", [P, GT])
        neg_half = sb("neg_half", [P, GT])
        x_t = sb("x_t", [P, 2, 2, GROUP])
        hid = sb("hid", [P, 2, GROUP])
        raw = sb("raw", [P, 2, 4, GROUP])
        rot = sb("rot", [P, 2, 4, GROUP])
        ra = sb("ra", [P, 2, 4, GROUP])
        parts = sb("parts", [P, 2, 3, 4, GROUP], BF16)
        v_st = sb("v_st", [P, 2, GT, HEADS, VA])

        ps_t = pb("ps_t", [P, 2, GROUP])
        ps_g1 = pb("ps_g1", [P, GROUP])
        ps_qk = pb("ps_qk", [P, 2, GROUP])
        ps_v = pb("ps_v", [P, 2, GROUP])
        ps_g2 = pb("ps_g2", [P, GROUP])

        weights_in = sem("weights_in")
        x_loaded = [sem(f"x_loaded{i}") for i in range(2)]
        consts_set = sem("consts_set")
        zeros_out = sem("zeros_out")
        stats_done = sem("stats_done")
        mv_done = sem("mv_done")
        mv_kept = sem("mv_kept")
        var_eps = sem("var_eps")
        rstd_done = sem("rstd_done")
        xn_ready = sem("xn_ready")
        xn_kept = [sem(f"xn_kept{i}") for i in range(2)]
        t_ready = sem("t_ready")
        xt_ready = sem("xt_ready")
        g1_ready = sem("g1_ready")
        hid_ready = sem("hid_ready")
        qk_ready = sem("qk_ready")
        raw_ready = sem("raw_ready")
        v_ready = sem("v_ready")
        v_read = sem("v_read")
        v_stored = [sem(f"v_stored{i}") for i in range(2)]
        g2_ready = sem("g2_ready")
        z_read = sem("z_read")
        rot_ready = [sem(f"rot_ready{i}") for i in range(2)]
        a_ready = sem("a_ready")
        b_ready = sem("b_ready")
        r_ready = sem("r_ready")
        high_ready = sem("high_ready")
        rest_ready = sem("rest_ready")
        mid_ready = sem("mid_ready")
        low_ready = sem("low_ready")
        passed = sem("passed")
        parts_out = [sem(f"parts_out{i}") for i in range(2)]

        block = ctx.enter_context(nc.Block())
        N_WEIGHTS = 10

        @block.sync
        def _(sp):
            def load_x(b, slot):
                g = 2 * b + slot
                src = d["x"][bass.ts(g, GROUP), :].rearrange("(t p) c -> p t c", p=P)
                sp.dma_start(x_in[:, slot, :, :], src).then_inc(x_loaded[slot], 16)

            load_x(0, 0)
            sp.dma_start(ident[:, :], d["ident"]).then_inc(weights_in, 16)
            sp.dma_start(w_g1[:, :, :], d["gate_w1"].rearrange("(k p) n -> p k n", p=P)).then_inc(weights_in, 16)
            sp.dma_start(b_g1[:, :], d["gate_b1"].unsqueeze(1)).then_inc(weights_in, 16)
            sp.dma_start(w_qk[:, :, 0:DIM], d["wq_t"].rearrange("(k p) n -> p k n", p=P)).then_inc(weights_in, 16)
            sp.dma_start(w_qk[:, :, DIM:2 * DIM], d["wk_t"].rearrange("(k p) n -> p k n", p=P)).then_inc(weights_in, 16)
            load_x(0, 1)
            sp.dma_start(w_vs[:, :, 0:DIM], d["wv_t"].rearrange("(k p) n -> p k n", p=P)).then_inc(weights_in, 16)
            sp.dma_start(w_vs[:, :, DIM:DIM + COLS], d["cemb_t"].rearrange("(k p) n -> p k n", p=P)).then_inc(weights_in, 16)
            sp.dma_start(w_g2[:, :], d["gate_w2"]).then_inc(weights_in, 16)
            sp.dma_start(rope_cos[:, :, :], d["rope_cos"]).then_inc(weights_in, 16)
            sp.dma_start(rope_sin[:, :, :], d["rope_sin"]).then_inc(weights_in, 16)
            sp.wait_ge(consts_set, 3)
            sp.dma_start(d["sorted_x"].rearrange("(t p) c -> p t c", p=P),
                         zero_rows[:, :].unsqueeze(1).to_broadcast([P, SLOTS, DIM])).then_inc(zeros_out, 16)

            def store_parts(b, slot):
                g = 2 * b + slot
                wait_apart(sp, low_ready, g + 1, passed)
                for i in range(3):
                    dst = d["qk_parts"][i, :, :, bass.ts(g, GROUP)].rearrange("m p t -> p m t")
                    sp.dma_start(dst, parts[:, slot, i, :, :]).then_inc(parts_out[slot], 16)

            def body(b, first, last):
                for slot in range(2):
                    g = 2 * b + slot
                    if not last:
                        wait_apart(sp, xn_ready, g + 1, passed)
                        load_x(b + 1, slot)
                    wait_apart(sp, xn_ready, g + 1, passed)
                    sp.dma_start(keep["xn"][:, bass.ts(g, GT), :], xn[:, slot, :, :]).then_inc(xn_kept[slot], 16)
                    wait_apart(sp, raw_ready, 4 * g + 4, passed)
                    wait_apart(sp, r_ready, g - 1, passed)
                    half = P // 2
                    sp.dma_start(rot[0:half, slot, :, :], raw[half:P, slot, :, :]).then_inc(rot_ready[slot], 16)
                    sp.dma_start(rot[half:P, slot, :, :], raw[0:half, slot, :, :]).then_inc(rot_ready[slot], 16)
                    wait_apart(sp, v_read, 8 * g + 8, passed)
                    sp.dma_start(d["v_aug"][bass.ts(g, GROUP), :].rearrange("(t p) c -> p t c", p=P),
                                 v_st[:, slot, :, :, :].rearrange("p t h e -> p t (h e)")).then_inc(v_stored[slot], 16)
                    if not (first and slot == 0):
                        store_parts(*group_before(b, slot))

            over_batches(sp, body)
            store_parts(BATCH - 1, 1)
            for slot in range(2):
                sp.wait_ge(xn_kept[slot], 16 * BATCH)
                sp.wait_ge(rot_ready[slot], 32 * BATCH)
                sp.wait_ge(v_stored[slot], 16 * BATCH)
                sp.wait_ge(parts_out[slot], 48 * BATCH)
            sp.wait_ge(zeros_out, 16)

        @block.gpsimd
        def _(pool):
            pool.memset(zero_rows[:, :], 0.0).then_inc(consts_set, 1)
            pool.memset(neg_half[:, :], -0.5).then_inc(consts_set, 1)
            pool.memset(v_st[:, :, :, :, :], 1.0).then_inc(consts_set, 1)

            def inverse_std(g):
                wait(pool, mv_done, GT * g + GT)
                wait(pool, xn_ready, g)
                settle(pool, passed)
                nc.gpsimd.tensor_scalar(rstd[:, :], mv[:, :, 1], LN_EPS, None, ALU.add).then_inc(var_eps, 1)
                wait(pool, var_eps, g + 1)
                nc.gpsimd.tensor_tensor(rstd[:, :], rstd[:, :], neg_half[:, :], ALU.pow).then_inc(rstd_done, 1)

            pool.wait_ge(consts_set, 3)
            inverse_std(0)
            pool.wait_ge(weights_in, 16 * N_WEIGHTS)

            def body(b, first, last):
                for slot in range(2):
                    g = 2 * b + slot
                    if not (last and slot == 1):
                        inverse_std(g + 1)
                    wait(pool, rot_ready[slot], 32 * b + 32)
                    sin = rope_sin[:, :, slot * GROUP:(slot + 1) * GROUP].unsqueeze(2)
                    r4 = rot[:, slot, :, :].rearrange("p (w m) t -> p w m t", w=2)
                    nc.gpsimd.tensor_tensor(r4, r4, sin.to_broadcast([P, 2, 2, GROUP]), ALU.mult).then_inc(b_ready, 1)

            over_batches(pool, body)

        @block.vector
        def _(dve):
            def norm_stats(b, slot):
                g = 2 * b + slot
                wait(dve, x_loaded[slot], 16 * b + 16)
                wait(dve, rstd_done, g)
                for t in range(GT):
                    nc.vector.bn_stats(stats[:, t, :], x_in[:, slot, t, :]).then_inc(stats_done, 1)
                for t in range(GT):
                    wait(dve, stats_done, GT * g + t + 1)
                    settle(dve, passed)
                    nc.vector.bn_aggr(mv[:, t, :], stats[:, t, :]).then_inc(mv_done, 1)
                wait(dve, mv_done, GT * g + GT)
                nc.vector.tensor_copy(keep["mv"][:, bass.ts(g, GT), :], mv[:, :, :]).then_inc(mv_kept, 1)

            def normalise(b, slot):
                g = 2 * b + slot
                wait(dve, rstd_done, g + 1)
                wait(dve, t_ready, g - 1)
                wait(dve, xn_kept[slot], 16 * b)
                for t in range(GT):
                    ins = nc.vector.tensor_scalar(xn[:, slot, t, :], x_in[:, slot, t, :], mv[:, t, 0:1],
                                                  rstd[:, t:t + 1], ALU.subtract, ALU.mult)
                ins.then_inc(xn_ready, 1)

            def rotary(b, slot):
                g = 2 * b + slot
                wait(dve, b_ready, g + 1)
                wait(dve, a_ready, g + 1)
                nc.vector.tensor_tensor(ra[:, slot, :, :], ra[:, slot, :, :], rot[:, slot, :, :],
                                        ALU.add).then_inc(r_ready, 1)

            def rest(b, slot):
                g = 2 * b + slot
                wait(dve, high_ready, g + 1)
                nc.vector.tensor_tensor(ra[:, slot, :, :], ra[:, slot, :, :], parts[:, slot, 0, :, :],
                                        ALU.subtract).then_inc(rest_ready, 1)

            def low(b, slot):
                g = 2 * b + slot
                wait(dve, mid_ready, g + 1)
                nc.vector.tensor_tensor(parts[:, slot, 2, :, :], ra[:, slot, :, :], parts[:, slot, 1, :, :],
                                        ALU.subtract).then_inc(low_ready, 1)

            norm_stats(0, 0)
            normalise(0, 0)
            dve.wait_ge(weights_in, 16 * N_WEIGHTS)

            def body(b, first, last):
                for slot in range(2):
                    g = 2 * b + slot
                    before = not (first and slot == 0)
                    after = not (last and slot == 1)
                    if after:
                        norm_stats(*group_after(b, slot))
                    if before:
                        rotary(*group_before(b, slot))
                    if after:
                        normalise(*group_after(b, slot))
                    if before:
                        rest(*group_before(b, slot))
                    wait(dve, v_stored[slot], 16 * b)
                    for t in range(GT):
                        wait(dve, v_ready, GT * g + t + 1)
                        ps = ps_v[:, t % 2, :]
                        nc.vector.tensor_copy(v_st[:, slot, t, :, 0:HD],
                                              ps[:, 0:DIM].rearrange("p (h e) -> p h e", e=HD)).then_inc(v_read, 1)
                        nc.vector.tensor_copy(keep["sim"][:, GT * g + t, :], ps[:, DIM:DIM + COLS]).then_inc(v_read, 1)
                    wait(dve, raw_ready, 4 * g + 4)
                    wait(dve, low_ready, g - 1)
                    cos = rope_cos[:, :, slot * GROUP:(slot + 1) * GROUP].unsqueeze(2)
                    four = lambda a: a[:, slot, :, :].rearrange("p (w m) t -> p w m t", w=2)
                    nc.vector.tensor_tensor(four(ra), four(raw), cos.to_broadcast([P, 2, 2, GROUP]),
                                            ALU.mult).then_inc(a_ready, 1)
                    wait(dve, g2_ready, g + 1)
                    nc.vector.tensor_copy(keep["z"][:, bass.ts(g, GT), :],
                                          ps_g2[:, 0:GT * COLS].rearrange("p (t c) -> p t c", c=COLS)).then_inc(z_read, 1)
                    if before:
                        low(*group_before(b, slot))

            over_batches(dve, body)
            rotary(BATCH - 1, 1)
            rest(BATCH - 1, 1)
            low(BATCH - 1, 1)

        @block.scalar
        def _(act):
            def evacuate_x(b, slot):
                g = 2 * b + slot
                wait(act, t_ready, g + 1)
                wait(act, v_ready, GT * (g - 1))
                wait(act, g1_ready, g - 1)
                nc.scalar.activation(x_t[:, slot, :, :], ps_t[:, :, :], ACT.Copy).then_inc(xt_ready, 1)

            def high(b, slot):
                g = 2 * b + slot
                wait(act, r_ready, g + 1)
                wait(act, parts_out[slot], 48 * b)
                nc.scalar.activation(parts[:, slot, 0, :, :], ra[:, slot, :, :], ACT.Copy).then_inc(high_ready, 1)

            def mid(b, slot):
                g = 2 * b + slot
                wait(act, rest_ready, g + 1)
                nc.scalar.activation(parts[:, slot, 1, :, :], ra[:, slot, :, :], ACT.Copy).then_inc(mid_ready, 1)

            evacuate_x(0, 0)
            act.wait_ge(weights_in, 16 * N_WEIGHTS)

            def body(b, first, last):
                for slot in range(2):
                    g = 2 * b + slot
                    before = not (first and slot == 0)
                    wait(act, g1_ready, g + 1)
                    wait(act, g2_ready, g - 1)
                    nc.scalar.activation(hid[:, slot, :], ps_g1[:, :], ACT.Gelu, bias=b_g1[:, 0:1]).then_inc(hid_ready, 1)
                    wait(act, a_ready, g - 1)
                    wait(act, rot_ready[slot], 32 * b)
                    for m in range(2):
                        wait(act, qk_ready, 4 * g + m + 1)
                        nc.scalar.activation(raw[:, slot, m, :], ps_qk[:, m % 2, :], ACT.Copy).then_inc(raw_ready, 1)
                    if before:
                        high(*group_before(b, slot))
                    for m in range(2, 4):
                        wait(act, qk_ready, 4 * g + m + 1)
                        nc.scalar.activation(raw[:, slot, m, :], ps_qk[:, m % 2, :], ACT.Copy).then_inc(raw_ready, 1)
                    if not (last and slot == 1):
                        evacuate_x(*group_after(b, slot))
                    if before:
                        mid(*group_before(b, slot))

            over_batches(act, body)
            high(BATCH - 1, 1)
            mid(BATCH - 1, 1)

        @block.tensor
        def _(pe):
            def transposes(b, slot):
                g = 2 * b + slot
                wait(pe, xn_ready, g + 1)
                wait(pe, xt_ready, g)
                for t in range(GT):
                    for k in range(2):
                        ins = nc.tensor.transpose(ps_t[:, k, t * P:(t + 1) * P],
                                                  xn[:, slot, t, k * P:(k + 1) * P], ident[:, :])
                ins.then_inc(t_ready, 1)

            pe.wait_ge(weights_in, 16 * N_WEIGHTS)
            transposes(0, 0)

            def body(b, first, last):
                for slot in range(2):
                    g = 2 * b + slot
                    wait(pe, xt_ready, g + 1)
                    wait(pe, hid_ready, g)
                    for k in range(2):
                        ins = nc.tensor.matmul(ps_g1[:, :], w_g1[:, k, :], x_t[:, slot, k, :],
                                               start=(k == 0), stop=(k == 1))
                    ins.then_inc(g1_ready, 1)
                    for m in range(4):
                        wait(pe, raw_ready, 4 * g + m - 1)
                        for k in range(2):
                            ins = nc.tensor.matmul(ps_qk[:, m % 2, :], w_qk[:, k, m * P:(m + 1) * P],
                                                   x_t[:, slot, k, :], start=(k == 0), stop=(k == 1))
                        ins.then_inc(qk_ready, 1)
                    if not (last and slot == 1):
                        transposes(*group_after(b, slot))
                    for t in range(GT):
                        wait(pe, v_read, 2 * (GT * g + t - 1))
                        for k in range(2):
                            ins = nc.tensor.matmul(ps_v[:, t % 2, 0:DIM + COLS], x_t[:, slot, k, t * P:(t + 1) * P],
                                                   w_vs[:, k, :], start=(k == 0), stop=(k == 1))
                        ins.then_inc(v_ready, 1)
                    wait(pe, hid_ready, g + 1)
                    wait(pe, z_read, g)
                    for t in range(GT):
                        ins = nc.tensor.matmul(ps_g2[:, t * COLS:(t + 1) * COLS], hid[:, slot, t * P:(t + 1) * P],
                                               w_g2[:, :], start=True, stop=True)
                    ins.then_inc(g2_ready, 1)

            over_batches(pe, body)


def route(nc, d, keep):
    with ExitStack() as ctx:
        sb = lambda n, s, t=FP32: ctx.enter_context(nc.sbuf_tensor("r_" + n, s, t))
        pb = lambda n, s: ctx.enter_context(nc.psum_tensor("r_" + n, s, FP32))
        sem = lambda n: ctx.enter_context(nc.semaphore("r_" + n))

        TC = [P, TILES, COLS]
        CT = [P, COLS, TILES]
        cemb = sb("cemb", [P, COLS, DIM])
        b_g2 = sb("b_g2", [P, COLS])
        col_rank = sb("col_rank", [P, COLS])
        tile_start = sb("tile_start", [P, SLOTS])
        before = sb("before", [P, P], BF16)
        ones = sb("ones", [P, P], BF16)
        half_neg = sb("half_neg", [P, TILES])
        c_norm = sb("c_norm", [P, COLS])
        t_norm = sb("t_norm", [P, TILES])
        rstd = sb("rstd", [P, TILES])
        lg = sb("lg", TC)
        ez = sb("ez", TC)
        top = sb("top", [P, TILES])
        pick = sb("pick", TC)
        pick_bf = sb("pick_bf", TC, BF16)
        esum = sb("esum", [P, TILES])
        total = sb("total", CT)
        seen = sb("seen", CT)
        small = sb("small", [P, 6, COLS])
        small_i = sb("small_i", [P, COLS], I32)
        place = sb("place", TC)
        place_f = sb("place_f", [P, TILES])
        tile_cmp = sb("tile_cmp", [P, SLOTS, COLS])
        tile_col = sb("tile_col", [P, SLOTS])
        ps_before = pb("ps_before", [P, TILES * COLS])
        ps_total = pb("ps_total", [P, TILES * COLS])

        loaded = sem("loaded")
        set_up = sem("set_up")
        bias_in = sem("bias_in")
        gate_exp = sem("gate_exp")
        norm_sq = sem("norm_sq")
        norms = sem("norms")
        shifted = sem("shifted")
        soft_exp = sem("soft_exp")
        picked = sem("picked")
        counted = sem("counted")
        step = sem("step")
        placed = sem("placed")
        scattered = sem("scattered")
        block = ctx.enter_context(nc.Block())

        @block.sync
        def _(sp):
            sp.dma_start(cemb[:, :, :], d["col_emb"].unsqueeze(0).to_broadcast([P, COLS, DIM])).then_inc(loaded, 16)
            sp.dma_start(b_g2[:, :], d["gate_b2"].unsqueeze(0).to_broadcast([P, COLS])).then_inc(loaded, 16)
            sp.dma_start(col_rank[:, :], d["col_rank"].unsqueeze(0).to_broadcast([P, COLS])).then_inc(loaded, 16)
            sp.dma_start(tile_start[:, :], d["tile_start"].unsqueeze(0).to_broadcast([P, SLOTS])).then_inc(loaded, 16)

        @block.gpsimd
        def _(pool):
            pool.memset(ones[:, :], 1.0).then_inc(set_up, 1)
            pool.memset(half_neg[:, :], -0.5).then_inc(set_up, 1)
            pool.memset(before[:, :], 1.0).then_inc(set_up, 1)
            pool.wait_ge(set_up, 3)
            nc.gpsimd.affine_select(out=before[:, :], in_=before[:, :], compare_op=ALU.is_gt, fill=0.0, base=0,
                                    pattern=[[1, P]], channel_multiplier=-1).then_inc(set_up, 1)
            nc.gpsimd.tensor_scalar(rstd[:, :], keep["mv"][:, :, 1], LN_EPS, None, ALU.add).then_inc(norms, 1)
            pool.wait_ge(norms, 1)
            nc.gpsimd.tensor_tensor(rstd[:, :], rstd[:, :], half_neg[:, :], ALU.pow).then_inc(norms, 1)
            pool.wait_ge(norm_sq, 1)
            nc.gpsimd.tensor_tensor(t_norm[:, :], t_norm[:, :], half_neg[:, :], ALU.pow).then_inc(norms, 1)
            nc.gpsimd.tensor_tensor(c_norm[:, :], c_norm[:, :], half_neg[:, 0:COLS], ALU.pow).then_inc(norms, 1)
            pool.wait_ge(placed, 1)
            for t in range(TILES):
                pool.indirect_dma_start(d["sorted_x"], bass.IndirectOffsetOnAxis(ap=keep["place"][:, t:t + 1], axis=0),
                                        keep["xn"][:, t, :], None).then_inc(scattered, 16)
            pool.wait_ge(scattered, 16 * TILES)

        @block.scalar
        def _(act):
            act.wait_ge(bias_in, 1)
            nc.scalar.activation(ez[:, :, :], lg[:, :, :], ACT.Exp, scale=-1.0).then_inc(gate_exp, 1)
            act.wait_ge(shifted, 1)
            nc.scalar.activation(ez[:, :, :], place[:, :, :], ACT.Exp).then_inc(soft_exp, 1)

        @block.tensor
        def _(pe):
            pe.wait_ge(set_up, 4)
            pe.wait_ge(picked, 1)
            flat = pick_bf[:, :, :].rearrange("p t c -> p (t c)")
            for weights, ps in ((before, ps_before), (ones, ps_total)):
                for i in range(2):
                    ins = nc.tensor.matmul(ps[:, i * 512:(i + 1) * 512], weights[:, :], flat[:, i * 512:(i + 1) * 512],
                                           start=True, stop=True)
            ins.then_inc(counted, 1)

        @block.vector
        def _(dve):
            chain = [0]

            def link(ins):
                chain[0] += 1
                ins.then_inc(step, 1)
                dve.wait_ge(step, chain[0])

            v = nc.vector
            per_tok = lambda a: a[:, :].unsqueeze(2).to_broadcast(TC)
            per_col = lambda a: a.unsqueeze(1).to_broadcast(TC)
            dve.wait_ge(loaded, 16 * 4)
            link(v.tensor_tensor(lg[:, :, :], keep["z"][:, :, :], per_col(b_g2[:, :]), ALU.add))
            v.tensor_scalar_max(lg[:, :, :], lg[:, :, :], SIGMOID_MIN).then_inc(bias_in, 1)
            link(v.tensor_tensor(cemb[:, :, :], cemb[:, :, :], cemb[:, :, :], ALU.mult))
            link(v.reduce_sum(c_norm[:, :], cemb[:, :, :], AX.X))
            link(v.tensor_scalar_max(c_norm[:, :], c_norm[:, :], NORM2_MIN))
            dve.wait_ge(norms, 2)
            link(v.tensor_tensor(t_norm[:, :], rstd[:, :], rstd[:, :], ALU.mult))
            link(v.tensor_tensor(t_norm[:, :], t_norm[:, :], keep["mv"][:, :, 1], ALU.mult))
            v.tensor_scalar(t_norm[:, :], t_norm[:, :], float(DIM), NORM2_MIN, ALU.mult, ALU.max).then_inc(norm_sq, 1)
            dve.wait_ge(gate_exp, 1)
            link(v.tensor_scalar_add(ez[:, :, :], ez[:, :, :], 1.0))
            link(v.reciprocal(lg[:, :, :], ez[:, :, :]))
            dve.wait_ge(norms, 4)
            link(v.tensor_tensor(place[:, :, :], keep["sim"][:, :, :], per_tok(t_norm), ALU.mult))
            link(v.tensor_tensor(place[:, :, :], place[:, :, :], per_col(c_norm[:, :]), ALU.mult))
            link(v.tensor_tensor(lg[:, :, :], lg[:, :, :], place[:, :, :], ALU.add))
            link(v.reduce_max(top[:, :], lg[:, :, :], AX.X))
            v.tensor_tensor(place[:, :, :], lg[:, :, :], per_tok(top), ALU.subtract).then_inc(shifted, 1)
            link(v.tensor_tensor(pick[:, :, :], lg[:, :, :], per_tok(top), ALU.is_equal))
            link(v.tensor_tensor(pick[:, :, :], pick[:, :, :], per_col(col_rank[:, :]), ALU.mult))
            link(v.reduce_max(top[:, :], pick[:, :, :], AX.X))
            link(v.tensor_tensor(pick[:, :, :], pick[:, :, :], per_tok(top), ALU.is_equal))
            v.tensor_copy(pick_bf[:, :, :], pick[:, :, :]).then_inc(picked, 1)
            dve.wait_ge(soft_exp, 1)
            link(v.reduce_sum(esum[:, :], ez[:, :, :], AX.X))
            link(v.reciprocal(keep["weight"][:, :], esum[:, :]))
            dve.wait_ge(counted, 1)
            link(v.tensor_copy(total[:, :, :], ps_total[:, :].rearrange("p (t c) -> p c t", c=COLS)))
            flat = lambda a: a[:, :, :].rearrange("p c t -> p (c t)")
            link(v.tensor_tensor_scan(flat(seen), flat(total), flat(total), 0.0, ALU.add, ALU.bypass))
            count, padded, base, end, zero, first = (small[:, i, :] for i in range(6))
            link(v.memset(zero, 0.0))
            link(v.tensor_tensor(first, seen[:, :, 0], total[:, :, 0], ALU.subtract))
            link(v.tensor_tensor(count, seen[:, :, TILES - 1], first, ALU.subtract))
            link(v.tensor_tensor(seen[:, :, :], seen[:, :, :], total[:, :, :], ALU.subtract))
            link(v.tensor_scalar_add(small_i[:, :], count, float(P - 1)))
            link(v.tensor_single_scalar(small_i[:, :], small_i[:, :], -P, ALU.bitwise_and))
            link(v.tensor_copy(padded, small_i[:, :]))
            link(v.tensor_tensor_scan(end, padded, padded, 0.0, ALU.add, ALU.bypass))
            link(v.tensor_tensor(base, end, padded, ALU.subtract))
            link(v.tensor_tensor(base, base, first, ALU.subtract))
            link(v.tensor_tensor(place[:, :, :], ps_before[:, :].rearrange("p (t c) -> p t c", c=COLS),
                                 seen[:, :, :].rearrange("p c t -> p t c"), ALU.add))
            link(v.tensor_tensor(place[:, :, :], place[:, :, :], per_col(base), ALU.add))
            link(v.tensor_tensor(place[:, :, :], place[:, :, :], pick[:, :, :], ALU.mult))
            link(v.reduce_sum(place_f[:, :], place[:, :, :], AX.X))
            v.tensor_copy(keep["place"][:, :], place_f[:, :]).then_inc(placed, 1)
            starts = tile_start[:, :].unsqueeze(2).to_broadcast([P, SLOTS, COLS])
            link(v.tensor_tensor(tile_cmp[:, :, :], starts, end.unsqueeze(1).to_broadcast([P, SLOTS, COLS]), ALU.is_ge))
            link(v.reduce_sum(tile_col[:, :], tile_cmp[:, :, :], AX.X))
            link(v.tensor_scalar_min(keep["tile_col"][:, :], tile_col[:, :], float(COLS - 1)))


def attend(nc, d, keep):
    with ExitStack() as ctx:
        sb = lambda n, s, t=FP32: ctx.enter_context(nc.sbuf_tensor("a_" + n, s, t))
        pb = lambda n, s: ctx.enter_context(nc.psum_tensor("a_" + n, s, FP32))
        sem = lambda n: ctx.enter_context(nc.semaphore("a_" + n))

        RING = UNITS
        BANK = 512
        q_ops = sb("q_ops", [P, RING, UH, SEQ], BF16)
        k_ops = sb("k_ops", [P, RING, UH, SEQ], BF16)
        v_ops = sb("v_ops", [P, RING, QTILES, UH * VA])
        PROBS = 4
        probs = sb("probs", [P, PROBS, UH, BANK])
        future = sb("future", [P, SEQ])
        future_t = sb("future_t", [P, P], BF16)
        ident = sb("ident", [P, P], BF16)
        sums_out = sb("sums_out", [P, 4, SEQ], BF16)
        row_max = sb("row_max", [P, 2, UH * QTILES])
        max_rest = sb("max_rest", [P, 2, UH * QTILES])
        max_parts = sb("max_parts", [P, 2, 3, UH * QTILES], BF16)
        max_rows = sb("max_rows", [P, 2, P], BF16)
        o_out = sb("o_out", [P, 2, SEQ])

        MAX_BANKS, EXP_BANKS = 4, 3
        ps_max = pb("ps_max", [P, MAX_BANKS * BANK])
        ps_exp = pb("ps_exp", [P, EXP_BANKS, BANK])
        ps_o = pb("ps_o", [P, BANK])

        passed = sem("passed")
        set_up = sem("set_up")
        o_clear = sem("o_clear")
        ops_in = [sem(f"ops_in{i}") for i in range(RING)]
        max_sent = [sem(f"max_sent{i}") for i in range(2)]
        max_in = [sem(f"max_in{i}") for i in range(RING)]
        scored = sem("scored")
        maxed = sem("maxed")
        split_step = sem("split_step")
        split_part = sem("split_part")
        split = sem("split")
        s_ready = sem("s_ready")
        exp_done = sem("exp_done")
        pv_done = sem("pv_done")
        o_read = sem("o_read")
        o_stored = [sem(f"o_stored{i}") for i in range(2)]
        block = ctx.enter_context(nc.Block())

        OPS_DMAS = 2 * len(TERMS) + 1
        GROUPS = [(0, kt) for kt in range(QTILES // 2)] + [(1, kt) for kt in range(QTILES)]
        NGROUP = len(GROUPS)
        PIECES = [(gi, j) for gi in range(NGROUP) for j in range(UH)]
        NPIECE = len(PIECES)
        CARRY = 2
        COPY_BEFORE = (UH * 6, UH * 2)

        def span(gi):
            half, kt = GROUPS[gi]
            return max(half * BANK, kt * P), (half + 1) * BANK

        MTILES = [(j, qt) for j in range(UH) for qt in range(QTILES)]
        TURN = "turn"
        TURN_AT = 8
        TILE_BANKS = [(qt,) if qt < 4 else (2 * (qt % 2), 2 * (qt % 2) + 1) for qt in range(QTILES)]
        TURN_BANKS = (0,)
        LEAD = 2 * len(MTILES) + 1
        PER_SLOT = len(MTILES) + 1

        def max_items(with_tiles, with_turn):
            items = list(MTILES) if with_tiles else []
            if with_turn:
                items.insert(min(TURN_AT, len(items)), TURN)
            return items

        def last_user():
            used, found, at = {}, [], 0
            slots = {(u, i): max_items(True, True)[i] for u in range(UNITS) for i in range(PER_SLOT)}
            for items in (dict(enumerate(MTILES + MTILES + [TURN])), slots, slots):
                found.append({})
                for key, item in items.items():
                    banks = TURN_BANKS if item == TURN else TILE_BANKS[item[1]]
                    found[-1][key] = at - max(used.get(k, -1) for k in banks)
                    used.update({k: at for k in banks})
                    at += 1
            return found

        def max_banks(item):
            banks = TURN_BANKS if item == TURN else TILE_BANKS[item[1]]
            return ps_max[:, banks[0] * BANK:(banks[-1] + 1) * BANK]

        def slot_flags(b, u, last):
            return (not (last and u >= 2)), (not (last and u == 3))

        def in_slots(eng, body):
            over_batches(eng, lambda b, first, last: [body(b, u, first, last) for u in range(UNITS)])

        @block.sync
        def _(sp):
            def load_ops(b, r):
                m, h0 = r // 2, (r % 2) * UH
                for which, ops in ((0, q_ops), (1, k_ops)):
                    for t, term in enumerate(TERMS):
                        src = d["qk_parts"][term[which], 2 * which + m, :, bass.ts(b, SEQ)]
                        src = src.rearrange("(i h) t -> i h t", h=8)[:, h0:h0 + UH, :]
                        dst = ops[t * HD:(t + 1) * HD, r, :, :]
                        sp.dma_start(dst, src).then_inc(ops_in[r], 16)
                src = d["v_aug"][bass.ts(b, SEQ), r * UH * VA:(r + 1) * UH * VA]
                sp.dma_start(v_ops[:, r, :, :], src.rearrange("(t p) e -> p t e", p=P)).then_inc(ops_in[r], 16)

            def store_o(b, r):
                n = UNITS * b + r
                wait_apart(sp, o_read, 2 * n + 2, passed)
                for j in range(UH):
                    sp.dma_start(d["heads_t"][r * UH + j, :, bass.ts(b, SEQ)],
                                 o_out[32 * j:32 * j + VA, r % 2, :]).then_inc(o_stored[r % 2], 16)

            def send_rows(r, slot, items, sent):
                wait_apart(sp, maxed, items, passed)
                sp.dma_start(d["max_rows"][slot], max_rows[0:3 * UH * QTILES, slot, :]).then_inc(max_sent[slot], 16)
                wait_apart(sp, max_sent[slot], 16 * sent, passed)
                src = d["max_rows"][slot].rearrange("(a h) q -> a (h q)", a=3)
                sp.dma_start(q_ops[SHIFT:KALL, r, :, :].rearrange("a h q -> a (h q)"), src).then_inc(max_in[r], 16)

            for r in range(3):
                load_ops(0, r)

            def body(b, u, first, last):
                n = UNITS * b + u
                if not (last and u >= 1):
                    wait_apart(sp, s_ready, NPIECE * n, passed)
                    wait_apart(sp, pv_done, NGROUP * n, passed)
                    load_ops(b if u == 0 else b + 1, (u + 3) % RING)
                if slot_flags(b, u, last)[1]:
                    r = (u + 1) % RING
                    turn = TURN_AT if slot_flags(b, u, last)[0] else 0
                    send_rows(r, (u + 1) % 2, LEAD + PER_SLOT * n + turn + 1, 2 * b + (u + 1) // 2 + 1)
                if not (first and u == 0):
                    store_o(b if u else b - 1, (u - 1) % UNITS)

            send_rows(0, 0, LEAD, 1)
            in_slots(sp, body)
            store_o(BATCH - 1, UNITS - 1)
            for i in range(2):
                sp.wait_ge(o_stored[i], 16 * UH * UNITS * BATCH // 2)

        @block.gpsimd
        def _(pool):
            pool.memset(k_ops[SHIFT:KALL, :, :, :], 1.0).then_inc(set_up, 1)
            pool.wait_ge(set_up, 1)
            pool.memset(future_t[:, :], 0.0).then_inc(set_up, 1)
            pool.memset(future[:, :], 0.0).then_inc(set_up, 1)
            pool.memset(ident[:, :], 0.0).then_inc(set_up, 1)
            pool.wait_ge(set_up, 4)
            nc.gpsimd.affine_select(out=future[:, SEQ - P:SEQ], in_=future[:, SEQ - P:SEQ], compare_op=ALU.is_ge,
                                    fill=MASKED, base=0, pattern=[[-1, P]], channel_multiplier=1).then_inc(set_up, 1)
            nc.gpsimd.affine_select(out=future_t[:, :], in_=future_t[:, :], compare_op=ALU.is_ge, fill=MASKED, base=0,
                                    pattern=[[1, P]], channel_multiplier=-1).then_inc(set_up, 1)
            nc.gpsimd.affine_select(out=ident[:, :], in_=ident[:, :], compare_op=ALU.not_equal, fill=1.0, base=0,
                                    pattern=[[1, P]], channel_multiplier=-1).then_inc(set_up, 1)

            def split_max(n, slot, items):
                STEPS = 3
                rest, mp = max_rest[:, slot, :], max_parts[:, slot, :, :]
                wait(pool, maxed, items)
                settle(pool, passed)
                nc.gpsimd.tensor_scalar(rest, row_max[:, slot, :], -1.0, None, ALU.mult).then_inc(split_step, 1)
                wait(pool, split_step, STEPS * n + 1)
                for i in range(2):
                    settle(pool, passed)
                    nc.gpsimd.tensor_copy(mp[:, i, :], rest).then_inc(split_part, 1)
                    wait(pool, split_part, 2 * n + i + 1)
                    nc.gpsimd.tensor_tensor(rest, rest, mp[:, i, :], ALU.subtract).then_inc(split_step, 1)
                    wait(pool, split_step, STEPS * n + i + 2)
                settle(pool, passed)
                nc.gpsimd.tensor_copy(mp[:, 2, :], rest).then_inc(split, 1)

            split_max(0, 0, len(MTILES))
            split_max(1, 1, 2 * len(MTILES))

            def body(b, u, first, last):
                n = UNITS * b + u
                if slot_flags(b, u, last)[0]:
                    split_max(n + 2, u % 2, LEAD + PER_SLOT * n + PER_SLOT)

            in_slots(pool, body)

        @block.vector
        def _(dve):
            nc.vector.memset(ps_o[:, :], 0.0).then_inc(o_clear, 1)
            dve.wait_ge(set_up, 7)

            def max_item(at, ring, item, slot, sent=None):
                wait(dve, scored, at + 1)
                ps = max_banks(item)
                if item == TURN:
                    if sent:
                        wait(dve, *sent)
                    nc.vector.tensor_copy(max_rows[0:3 * UH * QTILES, slot, :],
                                          ps.bitcast(BF16)[0:3 * UH * QTILES, 0:P]).then_inc(maxed, 1)
                    return
                j, qt = item
                width = (qt + 1) * P
                wait(dve, maxed, at - 3)
                settle(dve, passed)
                nc.vector.tensor_tensor_reduce(
                    out=sums_out[:, ring, 0:width], in0=ps[:, 0:width], in1=future[:, SEQ - width:SEQ],
                    scale=1.0, scalar=MASKED, op0=ALU.add, op1=ALU.max,
                    accum_out=row_max[:, slot, j * QTILES + qt:j * QTILES + qt + 1]).then_inc(maxed, 1)

            for at in range(LEAD):
                item = TURN if at == LEAD - 1 else MTILES[at % len(MTILES)]
                max_item(at, at % 4, item, 0 if item == TURN else at // len(MTILES))

            def body(b, u, first, last):
                n = UNITS * b + u
                with_tiles, with_turn = slot_flags(b, u, last)
                if with_tiles:
                    wait(dve, split, n + 1)
                for i, item in enumerate(max_items(with_tiles, with_turn)):
                    sent = (max_sent[(u + 1) % 2], 16 * (2 * b + (u + 1) // 2))
                    turn = item == TURN
                    max_item(LEAD + PER_SLOT * n + i, (LEAD + PER_SLOT * u + i) % 4, item,
                             (u + 1) % 2 if turn else u % 2, sent if turn and not (first and u == 0) else None)

            in_slots(dve, body)

        @block.scalar
        def _(act):
            def copy_o(n, u, b, half):
                wait(act, pv_done, NGROUP * n + (UH if half == 0 else NGROUP))
                if half == 0:
                    wait(act, o_stored[u % 2], 16 * UH * (2 * b + u // 2))
                nc.scalar.activation(o_out[:, u % 2, half * BANK:(half + 1) * BANK], ps_o[:, :],
                                     ACT.Copy).then_inc(o_read, 1)

            def body(b, u, first, last):
                n = UNITS * b + u
                for i, (gi, j) in enumerate(PIECES):
                    if i == COPY_BEFORE[1] and not (first and u == 0):
                        copy_o(n - 1, (u - 1) % UNITS, b if u else b - 1, 1)
                    if i == COPY_BEFORE[0]:
                        copy_o(n, u, b, 0)
                    if j == 0:
                        wait(act, pv_done, NGROUP * n + gi - PROBS + 1)
                    wait(act, s_ready, NPIECE * n + i + 1)
                    width = span(gi)[1] - span(gi)[0]
                    nc.scalar.activation(probs[:, gi % PROBS, j, 0:width], ps_exp[:, i % EXP_BANKS, 0:width],
                                         ACT.Exp).then_inc(exp_done, 1)

            in_slots(act, body)
            copy_o(UNITS * BATCH - 1, UNITS - 1, BATCH - 1, 1)

        @block.tensor
        def _(pe):
            back_ahead, back_first, back_later = last_user()

            def max_item(at, back, item, r, slot):
                wait(pe, maxed, at - back + 1)
                ps = max_banks(item)
                if item == TURN:
                    rows = 3 * UH * QTILES
                    nc.tensor.transpose(ps.bitcast(BF16)[0:rows, 0:P],
                                        max_parts[:, slot, :, :].rearrange("p a c -> p (a c)"),
                                        ident[:, :]).then_inc(scored, 1)
                    return
                j, qt = item
                width = (qt + 1) * P
                for k in range(0, width, BANK):
                    end = min(k + BANK, width)
                    ins = nc.tensor.matmul(ps[:, k:end], q_ops[0:KROWS, r, j, qt * P:width],
                                           k_ops[0:KROWS, r, j, k:end], start=True, stop=True)
                ins.then_inc(scored, 1)

            def score_piece(n, u, i):
                gi, j = PIECES[i]
                kt = GROUPS[gi][1]
                q0, q1 = span(gi)
                wait(pe, exp_done, NPIECE * n + i - EXP_BANKS + 1)
                ps = ps_exp[:, i % EXP_BANKS, :]
                diagonal = q0 == kt * P
                ins = nc.tensor.matmul(ps[:, 0:q1 - q0], k_ops[0:KALL, u, j, kt * P:(kt + 1) * P],
                                       q_ops[0:KALL, u, j, q0:q1], start=True, stop=not diagonal)
                if diagonal:
                    ins = nc.tensor.matmul(ps[:, 0:P], ident[:, :], future_t[:, :], start=False, stop=True)
                ins.then_inc(s_ready, 1)

            def value_group(n, u, gi):
                half, kt = GROUPS[gi]
                q0, q1 = span(gi)
                wait(pe, exp_done, NPIECE * n + UH * (gi + 1))
                if kt == 0:
                    wait(pe, o_read, 2 * n + half)
                for j in range(UH):
                    ins = nc.tensor.matmul(ps_o[32 * j:32 * j + VA, q0 - half * BANK:q1 - half * BANK],
                                           v_ops[:, u, kt, j * VA:(j + 1) * VA], probs[:, gi % PROBS, j, 0:q1 - q0],
                                           start=(kt == 0), stop=(q0 == q1 - P))
                ins.then_inc(pv_done, 1)

            def plan(items, carry):
                HOP = 0.2
                values = [(-1, gi) for gi in range(NGROUP - CARRY, NGROUP)] if carry else []
                values += [(0, gi) for gi in range(NGROUP - CARRY)]
                order, now, act, dve = [], 0.0, 0.0, 0.0
                exp_end, max_end, val_end = {}, {}, {}
                opened = {0: 0.0, 1: 0.0}
                i = im = iv = 0

                def score_at():
                    if i == NPIECE:
                        return None
                    if i >= COPY_BEFORE[1] and any(v[0] < 0 for v in values[iv:]):
                        return None
                    if i >= COPY_BEFORE[0] and (0, UH - 1) in values[iv:]:
                        return None
                    gi = i // UH
                    own = [v for v in values[iv:] if v[0] == 0 and v[1] <= gi - PROBS]
                    old = [v for v in values[iv:] if v[0] < 0 and v[1] - NGROUP <= gi - PROBS]
                    return None if own or old else max(now, exp_end.get(i - EXP_BANKS, 0.0) + HOP)

                def max_at():
                    if im == len(items):
                        return None
                    return max(now, max_end.get(im - 2, 0.0) + HOP)

                def value_at():
                    if iv == len(values):
                        return None
                    old, gi = values[iv]
                    if old:
                        return now
                    last = UH * gi + UH - 1
                    if last not in exp_end:
                        return None
                    if GROUPS[gi] == (0, 0) and carry and i < COPY_BEFORE[1] + 1:
                        return None
                    if GROUPS[gi] == (1, 0) and i < COPY_BEFORE[0] + 1:
                        return None
                    return max(now, exp_end[last] + HOP, opened[GROUPS[gi][0]] if GROUPS[gi][1] == 0 else 0.0)

                while i < NPIECE or im < len(items) or iv < len(values):
                    starts = [(at, rank, kind) for kind, at, rank in (
                        ("score", score_at(), act - now), ("max", max_at(), dve - now),
                        ("value", value_at(), 1.0)) if at is not None]
                    starts = [(max(at, now + 0.0), rank, kind) for at, rank, kind in starts]
                    at, _, kind = min(starts)
                    if kind == "score":
                        order.append(("score", i))
                        q0, q1 = span(i // UH)
                        now = at + (q1 - q0) / 2400 + (0.056 if q0 == GROUPS[i // UH][1] * P else 0.0)
                        if i == COPY_BEFORE[0] or (i == COPY_BEFORE[1] and carry):
                            act = max(act, val_end.get(UH - 1, 0.0) + HOP) + 0.48
                            opened[1 if i == COPY_BEFORE[0] else 0] = act + HOP
                        act = max(act, now + HOP) + (q1 - q0) / 1200 + 0.055
                        exp_end[i] = act
                        i += 1
                    elif kind == "max":
                        order.append(("max", im))
                        width = P if items[im] == TURN else (items[im][1] + 1) * P
                        now = at + width / 2400
                        dve = max(dve, now + HOP) + width / 960 + 0.12
                        max_end[im] = dve
                        im += 1
                    else:
                        order.append(("value", values[iv]))
                        q0, q1 = span(values[iv][1])
                        now = at + (q1 - q0) / 600 + 0.06
                        if values[iv][0] == 0:
                            val_end[values[iv][1]] = now
                        iv += 1
                return order

            pe.wait_ge(set_up, 7)
            pe.wait_ge(o_clear, 1)
            for at in range(LEAD):
                item = TURN if at == LEAD - 1 else MTILES[at % len(MTILES)]
                unit = at // len(MTILES)
                if item == TURN:
                    pe.wait_ge(split, 1)
                elif at % len(MTILES) == 0:
                    pe.wait_ge(ops_in[unit], 16 * OPS_DMAS)
                max_item(at, back_ahead[at], item, unit, 0)

            def body(b, u, first, last):
                n = UNITS * b + u
                with_tiles, with_turn = slot_flags(b, u, last)
                items = max_items(with_tiles, with_turn)
                for kind, what in plan(items, not (first and u == 0)):
                    if kind == "score":
                        if what == 0:
                            wait(pe, max_in[u], 16 * (b + 1))
                        score_piece(n, u, what)
                    elif kind == "value":
                        old, gi = what
                        value_group(n + old, (u + old) % UNITS, gi)
                    else:
                        if items[what] == TURN:
                            wait(pe, split, n + 2)
                        elif what == 0:
                            wait(pe, ops_in[(u + 2) % RING], 16 * OPS_DMAS * (b + 1 + (u + 2) // UNITS))
                        back = (back_first if first else back_later)[u, what] if with_tiles else 1
                        max_item(LEAD + PER_SLOT * n + what, back, items[what], (u + 2) % RING, (u + 1) % 2)

            in_slots(pe, body)
            for gi in range(NGROUP - CARRY, NGROUP):
                value_group(UNITS * BATCH - 1, UNITS - 1, gi)


def columns(nc, d, keep):
    with ExitStack() as ctx:
        sb = lambda n, s, t=FP32: ctx.enter_context(nc.sbuf_tensor("c_" + n, s, t))
        pb = lambda n, s: ctx.enter_context(nc.psum_tensor("c_" + n, s, FP32))
        sem = lambda n: ctx.enter_context(nc.semaphore("c_" + n))

        RING = 4
        ident = sb("ident", [P, P])
        sums = sb("sums", [P, HEADS * TOK // P])
        xs = sb("xs", [P, RING, DIM])
        w_up = sb("w_up", [P, RING, 2, NEUR])
        w_down = sb("w_down", [NEUR, RING, DIM + 1])
        xs_t = sb("xs_t", [P, 2, 2, P])
        act_t = sb("act_t", [NEUR, 2, P])
        y = sb("y", [P, 2, DIM])
        ps_t = pb("ps_t", [P, 2, 512])
        ps_up = pb("ps_up", [P, 2, 512])
        ps_y = pb("ps_y", [P, 2, 512])

        passed = sem("passed")
        ident_in = sem("ident_in")
        sums_in = sem("sums_in")
        inverted = sem("inverted")
        sums_out = sem("sums_out")
        tile_in = [sem(f"tile_in{i}") for i in range(RING)]
        turned = sem("turned")
        xt_ready = sem("xt_ready")
        up_ready = sem("up_ready")
        act_ready = sem("act_ready")
        y_ready = sem("y_ready")
        y_copied = sem("y_copied")
        y_out = [sem(f"y_out{i}") for i in range(2)]
        block = ctx.enter_context(nc.Block())
        QUADS = SLOTS // RING

        def over_tiles(eng, body):
            over(eng, QUADS, lambda q, first, last: [body(q, r, first, last) for r in range(RING)])

        @block.sync
        def _(sp):
            def load_tile(q, r):
                t = RING * q + r
                col = sp.value_load(keep["tile_col"][0:1, bass.ds(t, 1)], min_val=0, max_val=COLS - 1)
                sp.dma_start(xs[:, r, :], d["sorted_x"][bass.ts(t, P), :]).then_inc(tile_in[r], 16)
                sp.dma_start(w_up[:, r, :, :], d["w_up"][bass.ds(col, 1), :, :, :].rearrange("a p k n -> (a p) k n")).then_inc(tile_in[r], 16)
                sp.dma_start(w_down[:, r, :], d["w_down"][bass.ds(col, 1), :, :].rearrange("a p n -> (a p) n")).then_inc(tile_in[r], 16)

            sp.dma_start(ident[:, :], d["ident"]).then_inc(ident_in, 16)
            for r in range(RING):
                load_tile(0, r)
            sp.dma_start(sums[:, :], d["heads_t"][:, HD, :].rearrange("h (c t) -> h c t", c=P // HEADS)).then_inc(sums_in, 16)
            sp.wait_ge(inverted, 1)
            sp.dma_start(d["inv_sum"].rearrange("h (c t) -> h c t", c=P // HEADS), sums[:, :]).then_inc(sums_out, 16)

            def body(q, r, first, last):
                t = RING * q + r
                wait_apart(sp, y_copied, t + 1, passed)
                sp.dma_start(d["sorted_y"][bass.ts(t, P), :], y[:, r % 2, :]).then_inc(y_out[r % 2], 16)
                if not last:
                    load_tile(q + 1, r)

            over_tiles(sp, body)
            sp.wait_ge(y_out[0], 16 * SLOTS // 2)
            sp.wait_ge(y_out[1], 16 * SLOTS // 2)
            sp.wait_ge(sums_out, 16)

        @block.vector
        def _(dve):
            dve.wait_ge(sums_in, 16)
            nc.vector.reciprocal(sums[:, :], sums[:, :]).then_inc(inverted, 1)

            def body(q, r, first, last):
                t = RING * q + r
                wait(dve, turned, t + 1)
                wait(dve, up_ready, t - 1)
                nc.vector.tensor_copy(xs_t[:, r % 2, :, :].rearrange("p k t -> p (k t)"),
                                      ps_t[:, r % 2, 0:2 * P]).then_inc(xt_ready, 1)

            over_tiles(dve, body)

        @block.scalar
        def _(act):
            def body(q, r, first, last):
                t = RING * q + r
                wait(act, up_ready, t + 1)
                wait(act, y_ready, t - 1)
                nc.scalar.activation(act_t[:, r % 2, :], ps_up[0:NEUR, r % 2, 0:P], ACT.Gelu,
                                     bias=w_down[:, r, DIM:DIM + 1]).then_inc(act_ready, 1)
                if not (first and r == 0):
                    wait(act, y_ready, t)
                    wait(act, y_out[(r - 1) % 2], 16 * (2 * q + (r - 1) // 2))
                    nc.scalar.activation(y[:, (r - 1) % 2, :], ps_y[:, (r - 1) % 2, 0:DIM],
                                         ACT.Copy).then_inc(y_copied, 1)

            over_tiles(act, body)
            act.wait_ge(y_ready, SLOTS)
            act.wait_ge(y_out[1], 16 * (SLOTS // 2 - 1))
            nc.scalar.activation(y[:, 1, :], ps_y[:, 1, 0:DIM], ACT.Copy).then_inc(y_copied, 1)

        @block.tensor
        def _(pe):
            def turn(q, r):
                t = RING * q + r
                wait(pe, tile_in[r], 48 * q + 48)
                wait(pe, xt_ready, t - 1)
                for k in range(2):
                    ins = nc.tensor.transpose(ps_t[:, r % 2, k * P:(k + 1) * P], xs[:, r, k * P:(k + 1) * P], ident[:, :])
                ins.then_inc(turned, 1)

            def down(t, r):
                wait(pe, act_ready, t + 1)
                wait(pe, y_copied, t - 1)
                nc.tensor.matmul(ps_y[:, r % 2, 0:DIM], act_t[:, r % 2, :], w_down[:, r, 0:DIM],
                                 start=True, stop=True).then_inc(y_ready, 1)

            pe.wait_ge(ident_in, 16)
            turn(0, 0)

            def body(q, r, first, last):
                t = RING * q + r
                if not (last and r == RING - 1):
                    turn(q + (r + 1) // RING, (r + 1) % RING)
                wait(pe, xt_ready, t + 1)
                wait(pe, act_ready, t - 1)
                for k in range(2):
                    ins = nc.tensor.matmul(ps_up[0:NEUR, r % 2, 0:P], w_up[:, r, k, :], xs_t[:, r % 2, k, :],
                                           start=(k == 0), stop=(k == 1))
                ins.then_inc(up_ready, 1)
                if not (first and r == 0):
                    down(t - 1, (r - 1) % RING)

            over_tiles(pe, body)
            down(SLOTS - 1, RING - 1)


def combine(nc, d, keep):
    with ExitStack() as ctx:
        sb = lambda n, s, t=FP32: ctx.enter_context(nc.sbuf_tensor("o_" + n, s, t))
        pb = lambda n, s: ctx.enter_context(nc.psum_tensor("o_" + n, s, FP32))
        sem = lambda n: ctx.enter_context(nc.semaphore("o_" + n))

        ident = sb("ident", [P, P])
        w_o = sb("w_o", [P, 2, DIM])
        proj_b = sb("proj_b", [P, DIM])
        ln_g = sb("ln_g", [P, DIM])
        ln_b = sb("ln_b", [P, DIM])
        neg_half = sb("neg_half", [P, GT])
        x_in = sb("x_in", [P, 2, GT, DIM])
        heads = sb("heads", [P, 2, 2, GROUP])
        inv = sb("inv", [P, 2, 2, GROUP])
        rows = sb("rows", [P, 2, GT, DIM])
        yn = sb("yn", [P, 2, GT, DIM])
        res = sb("res", [P, 2, GT, DIM])
        stats = sb("stats", [P, GT, 6])
        mv = sb("mv", [P, 2, GT, 2])
        rstd = sb("rstd", [P, 2, GT])
        ps = pb("ps", [P, 2, GT * DIM])

        place = sb("place", [P, 2, GT], U32)
        passed = sem("passed")
        consts_in = sem("consts_in")
        placed = sem("placed")
        set_up = sem("set_up")
        att_in = [sem(f"att_in{i}") for i in range(2)]
        rows_in = [sem(f"rows_in{i}") for i in range(2)]
        scaled = sem("scaled")
        biased = sem("biased")
        mixed = sem("mixed")
        stats_done = sem("stats_done")
        mv_done = sem("mv_done")
        var_eps = sem("var_eps")
        rstd_done = sem("rstd_done")
        normed = sem("normed")
        gained = sem("gained")
        ps_ready = sem("ps_ready")
        summed = sem("summed")
        stored = [sem(f"stored{i}") for i in range(2)]
        block = ctx.enter_context(nc.Block())
        N_CONSTS = 5

        @block.sync
        def _(sp):
            for dst, src in ((proj_b, "proj_b"), (ln_g, "ln_g"), (ln_b, "ln_b")):
                sp.dma_start(dst[:, :], d[src].unsqueeze(0).to_broadcast([P, DIM])).then_inc(consts_in, 16)
            sp.dma_start(ident[:, :], d["ident"]).then_inc(consts_in, 16)
            sp.dma_start(w_o[:, :, :], d["wo_t"].rearrange("(k p) n -> p k n", p=P)).then_inc(consts_in, 16)

            def load(b, slot):
                g = 2 * b + slot
                toks = bass.ts(g, GROUP)
                sp.dma_start(x_in[:, slot, :, :], d["x"][toks, :].rearrange("(t p) c -> p t c", p=P)).then_inc(att_in[slot], 16)
                for k in range(2):
                    hs = slice(8 * k, 8 * k + 8)
                    sp.dma_start(heads[:, slot, k, :], d["heads_t"][hs, 0:HD, toks]).then_inc(att_in[slot], 16)
                    sp.dma_start(inv[:, slot, k, :],
                                 d["inv_sum"][hs, toks].unsqueeze(1).to_broadcast([8, HD, GROUP])).then_inc(att_in[slot], 16)

            load(0, 0)
            load(0, 1)

            def body(b, first, last):
                for slot in range(2):
                    g = 2 * b + slot
                    wait_apart(sp, summed, g + 1, passed)
                    sp.dma_start(d["out"][bass.ts(g, GROUP), :].rearrange("(t p) c -> p t c", p=P),
                                 res[:, slot, :, :]).then_inc(stored[slot], 16)
                    if not last:
                        wait_apart(sp, ps_ready, g + 1, passed)
                        load(b + 1, slot)

            over_batches(sp, body)
            sp.wait_ge(stored[0], 16 * BATCH)
            sp.wait_ge(stored[1], 16 * BATCH)

        @block.gpsimd
        def _(pool):
            pool.memset(neg_half[:, :], -0.5).then_inc(set_up, 1)
            pool.wait_ge(consts_in, 16 * N_CONSTS)

            def fetch(b, slot):
                g = 2 * b + slot
                wait(pool, mixed, GT * (g - 1))
                wait(pool, rows_in[slot], 16 * GT * b)
                settle(pool, passed)
                nc.gpsimd.tensor_copy(place[:, slot, :], keep["place"][:, bass.ts(g, GT)]).then_inc(placed, 1)
                wait(pool, placed, g + 1)
                settle(pool, passed)
                for t in range(GT):
                    at = bass.IndirectOffsetOnAxis(ap=place[:, slot, t:t + 1], axis=0)
                    nc.gpsimd.indirect_dma_start(rows[:, slot, t, :], None, d["sorted_y"], at).then_inc(rows_in[slot], 16)

            fetch(0, 0)
            pool.wait_ge(set_up, 1)

            def body(b, first, last):
                for slot in range(2):
                    g = 2 * b + slot
                    if not (last and slot == 1):
                        fetch(*group_after(b, slot))
                    wait(pool, mv_done, GT * g + GT)
                    wait(pool, normed, g - 1)
                    settle(pool, passed)
                    nc.gpsimd.tensor_scalar(rstd[:, slot, :], mv[:, slot, :, 1], LN_EPS, None, ALU.add).then_inc(var_eps, 1)
                    wait(pool, var_eps, g + 1)
                    nc.gpsimd.tensor_tensor(rstd[:, slot, :], rstd[:, slot, :], neg_half[:, :], ALU.pow).then_inc(rstd_done, 1)
                    wait(pool, normed, g + 1)
                    nc.gpsimd.tensor_tensor(yn[:, slot, :, :], yn[:, slot, :, :],
                                            ln_g[:, :].unsqueeze(1).to_broadcast([P, GT, DIM]), ALU.mult).then_inc(gained, 1)

            over_batches(pool, body)

        @block.vector
        def _(dve):
            dve.wait_ge(consts_in, 16 * N_CONSTS)

            def mix(b, slot):
                g = 2 * b + slot
                wait(dve, att_in[slot], 16 * 5 * (b + 1))
                nc.vector.tensor_tensor(heads[:, slot, :, :], heads[:, slot, :, :], inv[:, slot, :, :],
                                        ALU.mult).then_inc(scaled, 1)
                xg = keep["xn"][:, bass.ts(g, GT), :]
                wait(dve, gained, g - 1)
                wait(dve, summed, g - 1)
                nc.vector.tensor_tensor(yn[:, slot, :, :], xg, proj_b[:, :].unsqueeze(1).to_broadcast([P, GT, DIM]),
                                        ALU.add).then_inc(biased, 1)
                wait(dve, biased, g + 1)
                wait(dve, rows_in[slot], 16 * GT * (b + 1))
                for t in range(GT):
                    nc.vector.scalar_tensor_tensor(out=yn[:, slot, t, :], in0=rows[:, slot, t, :],
                                                   scalar=keep["weight"][:, bass.ds(GT * g + t, 1)],
                                                   in1=yn[:, slot, t, :], op0=ALU.mult, op1=ALU.add).then_inc(mixed, 1)
                for t in range(GT):
                    wait(dve, mixed, GT * g + t + 1)
                    wait(dve, mv_done, GT * (g - 1) + t + 1)
                    nc.vector.bn_stats(stats[:, t, :], yn[:, slot, t, :]).then_inc(stats_done, 1)
                wait(dve, rstd_done, g - 1)
                for t in range(GT):
                    wait(dve, stats_done, GT * g + t + 1)
                    settle(dve, passed)
                    nc.vector.bn_aggr(mv[:, slot, t, :], stats[:, t, :]).then_inc(mv_done, 1)

            mix(0, 0)

            def body(b, first, last):
                for slot in range(2):
                    g = 2 * b + slot
                    if not (last and slot == 1):
                        mix(*group_after(b, slot))
                    wait(dve, rstd_done, g + 1)
                    for t in range(GT):
                        ins = nc.vector.tensor_scalar(yn[:, slot, t, :], yn[:, slot, t, :], mv[:, slot, t, 0:1],
                                                      rstd[:, slot, t:t + 1], ALU.subtract, ALU.mult)
                    ins.then_inc(normed, 1)
                    wait(dve, ps_ready, g + 1)
                    wait(dve, gained, g + 1)
                    wait(dve, stored[slot], 16 * b)
                    nc.vector.tensor_tensor(res[:, slot, :, :].rearrange("p t c -> p (t c)"), ps[:, slot, :],
                                            yn[:, slot, :, :].rearrange("p t c -> p (t c)"), ALU.add).then_inc(summed, 1)

            over_batches(dve, body)

        @block.tensor
        def _(pe):
            pe.wait_ge(consts_in, 16 * N_CONSTS)

            def body(b, first, last):
                for slot in range(2):
                    g = 2 * b + slot
                    wait(pe, scaled, g + 1)
                    wait(pe, summed, g - 1)
                    for t in range(GT):
                        out = ps[:, slot, t * DIM:(t + 1) * DIM]
                        toks = slice(t * P, (t + 1) * P)
                        nc.tensor.matmul(out, ident[:, :], x_in[:, slot, t, :], start=True, stop=False)
                        nc.tensor.matmul(out, ident[:, :], ln_b[:, :], start=False, stop=False)
                        for k in range(2):
                            ins = nc.tensor.matmul(out, heads[:, slot, k, toks], w_o[:, k, :], start=False, stop=(k == 1))
                    ins.then_inc(ps_ready, 1)

            over_batches(pe, body)


def build(nc, d, phases=None):
    dram = lambda n, s, t=FP32: nc.dram_tensor(n, s, t, kind="Internal").ap()
    d = dict(d)
    d["qk_parts"] = dram("qk_parts", [3, 4, P, TOK], BF16)
    d["v_aug"] = dram("v_aug", [TOK, HEADS * VA])
    d["sorted_x"] = dram("sorted_x", [SLOTS * P, DIM])
    d["sorted_y"] = dram("sorted_y", [SLOTS * P, DIM])
    d["max_rows"] = dram("max_rows", [2, 3 * UH * QTILES, P], BF16)
    d["heads_t"] = dram("heads_t", [HEADS, VA, TOK])
    d["inv_sum"] = dram("inv_sum", [HEADS, TOK])
    with ExitStack() as ctx:
        sb = lambda n, s, t=FP32: ctx.enter_context(nc.sbuf_tensor(n, s, t))
        keep = {
            "xn": sb("keep_xn", [P, TILES, DIM]),
            "weight": sb("keep_weight", [P, TILES]),
            "place": sb("keep_place", [P, TILES], U32),
            "tile_col": sb("keep_tile_col", [P, SLOTS], I32),
        }
        with ExitStack() as early:
            sb2 = lambda n, s: early.enter_context(nc.sbuf_tensor(n, s, FP32))
            keep["mv"] = sb2("keep_mv", [P, TILES, 2])
            keep["sim"] = sb2("keep_sim", [P, TILES, COLS])
            keep["z"] = sb2("keep_z", [P, TILES, COLS])
            project(nc, d, keep)
            route(nc, d, keep)
        if phases != 1:
            attend(nc, d, keep)
        if phases is None:
            columns(nc, d, keep)
            combine(nc, d, keep)


def host_layout(x):
    f = np.float32
    order = np.array([(m * 8 + h) * HD + i for m in range(2) for i in range(HD) for h in range(8)])
    inv_freq = (f(1.0) / f(10000.0) ** (np.arange(0, HD, 2, dtype=f) / f(HD))).astype(f)
    freqs = np.outer(np.arange(SEQ, dtype=f), inv_freq).astype(f)
    rows = np.arange(P) // 8 % (HD // 2)
    cos = np.cos(freqs)[:, rows].T.astype(f)
    sin = np.sin(freqs)[:, rows].T.astype(f) * np.where(np.arange(P) < P // 2, f(-1), f(1))[:, None]
    scale = np.array([1.0 / np.sqrt(HD), 1.0], f)[None, :, None]
    c = np.ascontiguousarray
    return {
        "x": c(x["L0_attn_x"].reshape(TOK, DIM)),
        "wq_t": c(x["L0_attn_Wq"][order].T), "wk_t": c(x["L0_attn_Wk"][order].T),
        "wv_t": c(x["L0_attn_Wv"].T), "wo_t": c(x["L0_attn_Wo"].T),
        "col_emb": c(x["L0_ffn_col_emb"]), "cemb_t": c(x["L0_ffn_col_emb"].T),
        "gate_w1": c(x["L0_ffn_gate_w1"]), "gate_b1": c(x["L0_ffn_gate_b1"]),
        "gate_w2": c(x["L0_ffn_gate_w2"]), "gate_b2": c(x["L0_ffn_gate_b2"]),
        "w_up": c(x["L0_ffn_W_cols"].reshape(COLS, 2, P, NEUR).transpose(0, 2, 1, 3)),
        "w_down": c(np.concatenate([x["L0_ffn_proj_w"].reshape(COLS, NEUR, DIM),
                                    x["L0_ffn_b_cols"].reshape(COLS, NEUR, 1)], axis=2)),
        "proj_b": c(x["L0_ffn_proj_b"]),
        "ln_g": c(x["L0_ffn_ln_g"]), "ln_b": c(x["L0_ffn_ln_b"]),
        "ident": np.eye(P, dtype=f),
        "rope_cos": c((cos[:, None, :] * scale).astype(f)),
        "rope_sin": c((sin[:, None, :] * scale).astype(f)),
        "col_rank": np.arange(COLS, 0, -1).astype(f),
        "tile_start": (np.arange(SLOTS) * P).astype(f),
    }


def kernel(**inputs):
    import concourse.bacc as bacc
    from concourse.bass_utils import run_bass_kernel_spmd

    arrays = host_layout({k: np.asarray(v) for k, v in inputs.items()})
    nc = bacc.Bacc("TRN2", target_bir_lowering=False, num_devices=1)
    d = {n: nc.dram_tensor(f"in_{n}", a.shape, mybir.dt.from_np(a.dtype), kind="ExternalInput").ap()
         for n, a in arrays.items()}
    d["out"] = nc.dram_tensor("out", (TOK, DIM), FP32, kind="ExternalOutput").ap()
    build(nc, d)
    r = run_bass_kernel_spmd(nc, [{f"in_{n}": a for n, a in arrays.items()}], core_ids=[0])
    return r.results[0]["out"].reshape(BATCH, SEQ, DIM)
```

```python
from contextlib import ExitStack

import numpy as np
import concourse.bass as bass
from concourse import mybir

FP32 = mybir.dt.float32
BF16 = mybir.dt.bfloat16
I32 = mybir.dt.int32
U32 = mybir.dt.uint32
ALU = mybir.AluOpType
ACT = mybir.ActivationFunctionType
AX = mybir.AxisListType

P = 128
BATCH, SEQ, DIM = 8, 1024, 256
HEADS = 16
HD = DIM // HEADS
TOK = BATCH * SEQ
TILES = TOK // P
COLS, NEUR, HID = 16, 64, 128
LN_EPS = 1e-5
SIGMOID_MIN = -87.0
MASKED = -3.0e38
NORM2_MIN = 1e-24

GROUP = 512
GT = GROUP // P
VA = HD + 1
QTILES = SEQ // P
UH = 4
UNITS = HEADS // UH
TERMS = ((0, 0), (0, 1), (1, 0), (0, 2), (2, 0), (1, 1))
KROWS = len(TERMS) * HD
SHIFT = KROWS
KALL = KROWS + 3
SLOTS = -(-((TOK + COLS * (P - 1)) // P) // 4) * 4


def over(eng, count, body):
    body(0, True, False)
    with eng.Fori(1, count - 1) as i:
        body(i, False, False)
    body(count - 1, False, True)


def over_batches(eng, body):
    over(eng, BATCH, body)


def wait(eng, sem, value):
    if isinstance(value, int) and value <= 0:
        return
    eng.wait_ge(sem, value)


def settle(eng, passed):
    eng.sem_inc(passed, 1)


def wait_apart(eng, sem, value, passed):
    wait(eng, sem, value)
    if not isinstance(value, int):
        settle(eng, passed)


def group_after(b, slot):
    return (b, 1) if slot == 0 else (b + 1, 0)


def group_before(b, slot):
    return (b, 0) if slot == 1 else (b - 1, 1)


def project(nc, d, keep):
    with ExitStack() as ctx:
        sb = lambda n, s, t=FP32: ctx.enter_context(nc.sbuf_tensor("p_" + n, s, t))
        pb = lambda n, s: ctx.enter_context(nc.psum_tensor("p_" + n, s, FP32))
        sem = lambda n: ctx.enter_context(nc.semaphore("p_" + n))

        ident = sb("ident", [P, P])
        w_qk = sb("w_qk", [P, 2, 2 * DIM])
        w_vs = sb("w_vs", [P, 2, DIM + COLS])
        w_g1 = sb("w_g1", [P, 2, HID])
        b_g1 = sb("b_g1", [P, 1])
        w_g2 = sb("w_g2", [P, COLS])
        rope_cos = sb("rope_cos", [P, 2, SEQ])
        rope_sin = sb("rope_sin", [P, 2, SEQ])
        zero_rows = sb("zero_rows", [P, DIM])
        x_in = sb("x_in", [P, 2, GT, DIM])
        xn = sb("xn", [P, 2, GT, DIM])
        stats = sb("stats", [P, GT, 6])
        mv = sb("mv", [P, GT, 2])
        rstd = sb("rstd", [P, GT])
        neg_half = sb("neg_half", [P, GT])
        x_t = sb("x_t", [P, 2, 2, GROUP])
        hid = sb("hid", [P, 2, GROUP])
        raw = sb("raw", [P, 2, 4, GROUP])
        rot = sb("rot", [P, 2, 4, GROUP])
        ra = sb("ra", [P, 2, 4, GROUP])
        parts = sb("parts", [P, 2, 3, 4, GROUP], BF16)
        v_st = sb("v_st", [P, 2, GT, HEADS, VA])

        ps_t = pb("ps_t", [P, 2, GROUP])
        ps_g1 = pb("ps_g1", [P, GROUP])
        ps_qk = pb("ps_qk", [P, 2, GROUP])
        ps_v = pb("ps_v", [P, 2, GROUP])
        ps_g2 = pb("ps_g2", [P, GROUP])

        weights_in = sem("weights_in")
        x_loaded = [sem(f"x_loaded{i}") for i in range(2)]
        consts_set = sem("consts_set")
        zeros_out = sem("zeros_out")
        stats_done = sem("stats_done")
        mv_done = sem("mv_done")
        mv_kept = sem("mv_kept")
        var_eps = sem("var_eps")
        rstd_done = sem("rstd_done")
        xn_ready = sem("xn_ready")
        xn_kept = [sem(f"xn_kept{i}") for i in range(2)]
        t_ready = sem("t_ready")
        xt_ready = sem("xt_ready")
        g1_ready = sem("g1_ready")
        hid_ready = sem("hid_ready")
        qk_ready = sem("qk_ready")
        raw_ready = sem("raw_ready")
        v_ready = sem("v_ready")
        v_read = sem("v_read")
        v_stored = [sem(f"v_stored{i}") for i in range(2)]
        g2_ready = sem("g2_ready")
        z_read = sem("z_read")
        rot_ready = [sem(f"rot_ready{i}") for i in range(2)]
        a_ready = sem("a_ready")
        b_ready = sem("b_ready")
        r_ready = sem("r_ready")
        high_ready = sem("high_ready")
        rest_ready = sem("rest_ready")
        mid_ready = sem("mid_ready")
        low_ready = sem("low_ready")
        passed = sem("passed")
        parts_out = [sem(f"parts_out{i}") for i in range(2)]

        block = ctx.enter_context(nc.Block())
        N_WEIGHTS = 10

        @block.sync
        def _(sp):
            def load_x(b, slot):
                g = 2 * b + slot
                src = d["x"][bass.ts(g, GROUP), :].rearrange("(t p) c -> p t c", p=P)
                sp.dma_start(x_in[:, slot, :, :], src).then_inc(x_loaded[slot], 16)

            load_x(0, 0)
            sp.dma_start(ident[:, :], d["ident"]).then_inc(weights_in, 16)
            sp.dma_start(w_g1[:, :, :], d["gate_w1"].rearrange("(k p) n -> p k n", p=P)).then_inc(weights_in, 16)
            sp.dma_start(b_g1[:, :], d["gate_b1"].unsqueeze(1)).then_inc(weights_in, 16)
            sp.dma_start(w_qk[:, :, 0:DIM], d["wq_t"].rearrange("(k p) n -> p k n", p=P)).then_inc(weights_in, 16)
            sp.dma_start(w_qk[:, :, DIM:2 * DIM], d["wk_t"].rearrange("(k p) n -> p k n", p=P)).then_inc(weights_in, 16)
            load_x(0, 1)
            sp.dma_start(w_vs[:, :, 0:DIM], d["wv_t"].rearrange("(k p) n -> p k n", p=P)).then_inc(weights_in, 16)
            sp.dma_start(w_vs[:, :, DIM:DIM + COLS], d["cemb_t"].rearrange("(k p) n -> p k n", p=P)).then_inc(weights_in, 16)
            sp.dma_start(w_g2[:, :], d["gate_w2"]).then_inc(weights_in, 16)
            sp.dma_start(rope_cos[:, :, :], d["rope_cos"]).then_inc(weights_in, 16)
            sp.dma_start(rope_sin[:, :, :], d["rope_sin"]).then_inc(weights_in, 16)
            sp.wait_ge(consts_set, 3)
            sp.dma_start(d["sorted_x"].rearrange("(t p) c -> p t c", p=P),
                         zero_rows[:, :].unsqueeze(1).to_broadcast([P, SLOTS, DIM])).then_inc(zeros_out, 16)

            def store_parts(b, slot):
                g = 2 * b + slot
                wait_apart(sp, low_ready, g + 1, passed)
                for i in range(3):
                    dst = d["qk_parts"][i, :, :, bass.ts(g, GROUP)].rearrange("m p t -> p m t")
                    sp.dma_start(dst, parts[:, slot, i, :, :]).then_inc(parts_out[slot], 16)

            def body(b, first, last):
                for slot in range(2):
                    g = 2 * b + slot
                    if not last:
                        wait_apart(sp, xn_ready, g + 1, passed)
                        load_x(b + 1, slot)
                    wait_apart(sp, xn_ready, g + 1, passed)
                    sp.dma_start(keep["xn"][:, bass.ts(g, GT), :], xn[:, slot, :, :]).then_inc(xn_kept[slot], 16)
                    wait_apart(sp, raw_ready, 4 * g + 4, passed)
                    wait_apart(sp, r_ready, g - 1, passed)
                    half = P // 2
                    sp.dma_start(rot[0:half, slot, :, :], raw[half:P, slot, :, :]).then_inc(rot_ready[slot], 16)
                    sp.dma_start(rot[half:P, slot, :, :], raw[0:half, slot, :, :]).then_inc(rot_ready[slot], 16)
                    wait_apart(sp, v_read, 8 * g + 8, passed)
                    sp.dma_start(d["v_aug"][bass.ts(g, GROUP), :].rearrange("(t p) c -> p t c", p=P),
                                 v_st[:, slot, :, :, :].rearrange("p t h e -> p t (h e)")).then_inc(v_stored[slot], 16)
                    if not (first and slot == 0):
                        store_parts(*group_before(b, slot))

            over_batches(sp, body)
            store_parts(BATCH - 1, 1)
            for slot in range(2):
                sp.wait_ge(xn_kept[slot], 16 * BATCH)
                sp.wait_ge(rot_ready[slot], 32 * BATCH)
                sp.wait_ge(v_stored[slot], 16 * BATCH)
                sp.wait_ge(parts_out[slot], 48 * BATCH)
            sp.wait_ge(zeros_out, 16)

        @block.gpsimd
        def _(pool):
            pool.memset(zero_rows[:, :], 0.0).then_inc(consts_set, 1)
            pool.memset(neg_half[:, :], -0.5).then_inc(consts_set, 1)
            pool.memset(v_st[:, :, :, :, :], 1.0).then_inc(consts_set, 1)

            def inverse_std(g):
                wait(pool, mv_done, GT * g + GT)
                wait(pool, xn_ready, g)
                settle(pool, passed)
                nc.gpsimd.tensor_scalar(rstd[:, :], mv[:, :, 1], LN_EPS, None, ALU.add).then_inc(var_eps, 1)
                wait(pool, var_eps, g + 1)
                nc.gpsimd.tensor_tensor(rstd[:, :], rstd[:, :], neg_half[:, :], ALU.pow).then_inc(rstd_done, 1)

            pool.wait_ge(consts_set, 3)
            inverse_std(0)
            pool.wait_ge(weights_in, 16 * N_WEIGHTS)

            def body(b, first, last):
                for slot in range(2):
                    g = 2 * b + slot
                    if not (last and slot == 1):
                        inverse_std(g + 1)
                    wait(pool, rot_ready[slot], 32 * b + 32)
                    sin = rope_sin[:, :, slot * GROUP:(slot + 1) * GROUP].unsqueeze(2)
                    r4 = rot[:, slot, :, :].rearrange("p (w m) t -> p w m t", w=2)
                    nc.gpsimd.tensor_tensor(r4, r4, sin.to_broadcast([P, 2, 2, GROUP]), ALU.mult).then_inc(b_ready, 1)

            over_batches(pool, body)

        @block.vector
        def _(dve):
            def norm_stats(b, slot):
                g = 2 * b + slot
                wait(dve, x_loaded[slot], 16 * b + 16)
                wait(dve, rstd_done, g)
                for t in range(GT):
                    nc.vector.bn_stats(stats[:, t, :], x_in[:, slot, t, :]).then_inc(stats_done, 1)
                for t in range(GT):
                    wait(dve, stats_done, GT * g + t + 1)
                    settle(dve, passed)
                    nc.vector.bn_aggr(mv[:, t, :], stats[:, t, :]).then_inc(mv_done, 1)
                wait(dve, mv_done, GT * g + GT)
                nc.vector.tensor_copy(keep["mv"][:, bass.ts(g, GT), :], mv[:, :, :]).then_inc(mv_kept, 1)

            def normalise(b, slot):
                g = 2 * b + slot
                wait(dve, rstd_done, g + 1)
                wait(dve, t_ready, g - 1)
                wait(dve, xn_kept[slot], 16 * b)
                for t in range(GT):
                    ins = nc.vector.tensor_scalar(xn[:, slot, t, :], x_in[:, slot, t, :], mv[:, t, 0:1],
                                                  rstd[:, t:t + 1], ALU.subtract, ALU.mult)
                ins.then_inc(xn_ready, 1)

            def rotary(b, slot):
                g = 2 * b + slot
                wait(dve, b_ready, g + 1)
                wait(dve, a_ready, g + 1)
                nc.vector.tensor_tensor(ra[:, slot, :, :], ra[:, slot, :, :], rot[:, slot, :, :],
                                        ALU.add).then_inc(r_ready, 1)

            def rest(b, slot):
                g = 2 * b + slot
                wait(dve, high_ready, g + 1)
                nc.vector.tensor_tensor(ra[:, slot, :, :], ra[:, slot, :, :], parts[:, slot, 0, :, :],
                                        ALU.subtract).then_inc(rest_ready, 1)

            def low(b, slot):
                g = 2 * b + slot
                wait(dve, mid_ready, g + 1)
                nc.vector.tensor_tensor(parts[:, slot, 2, :, :], ra[:, slot, :, :], parts[:, slot, 1, :, :],
                                        ALU.subtract).then_inc(low_ready, 1)

            norm_stats(0, 0)
            normalise(0, 0)
            dve.wait_ge(weights_in, 16 * N_WEIGHTS)

            def body(b, first, last):
                for slot in range(2):
                    g = 2 * b + slot
                    before = not (first and slot == 0)
                    after = not (last and slot == 1)
                    if after:
                        norm_stats(*group_after(b, slot))
                    if before:
                        rotary(*group_before(b, slot))
                    if after:
                        normalise(*group_after(b, slot))
                    if before:
                        rest(*group_before(b, slot))
                    wait(dve, v_stored[slot], 16 * b)
                    for t in range(GT):
                        wait(dve, v_ready, GT * g + t + 1)
                        ps = ps_v[:, t % 2, :]
                        nc.vector.tensor_copy(v_st[:, slot, t, :, 0:HD],
                                              ps[:, 0:DIM].rearrange("p (h e) -> p h e", e=HD)).then_inc(v_read, 1)
                        nc.vector.tensor_copy(keep["sim"][:, GT * g + t, :], ps[:, DIM:DIM + COLS]).then_inc(v_read, 1)
                    wait(dve, raw_ready, 4 * g + 4)
                    wait(dve, low_ready, g - 1)
                    cos = rope_cos[:, :, slot * GROUP:(slot + 1) * GROUP].unsqueeze(2)
                    four = lambda a: a[:, slot, :, :].rearrange("p (w m) t -> p w m t", w=2)
                    nc.vector.tensor_tensor(four(ra), four(raw), cos.to_broadcast([P, 2, 2, GROUP]),
                                            ALU.mult).then_inc(a_ready, 1)
                    wait(dve, g2_ready, g + 1)
                    nc.vector.tensor_copy(keep["z"][:, bass.ts(g, GT), :],
                                          ps_g2[:, 0:GT * COLS].rearrange("p (t c) -> p t c", c=COLS)).then_inc(z_read, 1)
                    if before:
                        low(*group_before(b, slot))

            over_batches(dve, body)
            rotary(BATCH - 1, 1)
            rest(BATCH - 1, 1)
            low(BATCH - 1, 1)

        @block.scalar
        def _(act):
            def evacuate_x(b, slot):
                g = 2 * b + slot
                wait(act, t_ready, g + 1)
                wait(act, v_ready, GT * (g - 1))
                wait(act, g1_ready, g - 1)
                nc.scalar.activation(x_t[:, slot, :, :], ps_t[:, :, :], ACT.Copy).then_inc(xt_ready, 1)

            def high(b, slot):
                g = 2 * b + slot
                wait(act, r_ready, g + 1)
                wait(act, parts_out[slot], 48 * b)
                nc.scalar.activation(parts[:, slot, 0, :, :], ra[:, slot, :, :], ACT.Copy).then_inc(high_ready, 1)

            def mid(b, slot):
                g = 2 * b + slot
                wait(act, rest_ready, g + 1)
                nc.scalar.activation(parts[:, slot, 1, :, :], ra[:, slot, :, :], ACT.Copy).then_inc(mid_ready, 1)

            evacuate_x(0, 0)
            act.wait_ge(weights_in, 16 * N_WEIGHTS)

            def body(b, first, last):
                for slot in range(2):
                    g = 2 * b + slot
                    before = not (first and slot == 0)
                    wait(act, g1_ready, g + 1)
                    wait(act, g2_ready, g - 1)
                    nc.scalar.activation(hid[:, slot, :], ps_g1[:, :], ACT.Gelu, bias=b_g1[:, 0:1]).then_inc(hid_ready, 1)
                    wait(act, a_ready, g - 1)
                    wait(act, rot_ready[slot], 32 * b)
                    for m in range(2):
                        wait(act, qk_ready, 4 * g + m + 1)
                        nc.scalar.activation(raw[:, slot, m, :], ps_qk[:, m % 2, :], ACT.Copy).then_inc(raw_ready, 1)
                    if before:
                        high(*group_before(b, slot))
                    for m in range(2, 4):
                        wait(act, qk_ready, 4 * g + m + 1)
                        nc.scalar.activation(raw[:, slot, m, :], ps_qk[:, m % 2, :], ACT.Copy).then_inc(raw_ready, 1)
                    if not (last and slot == 1):
                        evacuate_x(*group_after(b, slot))
                    if before:
                        mid(*group_before(b, slot))

            over_batches(act, body)
            high(BATCH - 1, 1)
            mid(BATCH - 1, 1)

        @block.tensor
        def _(pe):
            def transposes(b, slot):
                g = 2 * b + slot
                wait(pe, xn_ready, g + 1)
                wait(pe, xt_ready, g)
                for t in range(GT):
                    for k in range(2):
                        ins = nc.tensor.transpose(ps_t[:, k, t * P:(t + 1) * P],
                                                  xn[:, slot, t, k * P:(k + 1) * P], ident[:, :])
                ins.then_inc(t_ready, 1)

            pe.wait_ge(weights_in, 16 * N_WEIGHTS)
            transposes(0, 0)

            def body(b, first, last):
                for slot in range(2):
                    g = 2 * b + slot
                    wait(pe, xt_ready, g + 1)
                    wait(pe, hid_ready, g)
                    for k in range(2):
                        ins = nc.tensor.matmul(ps_g1[:, :], w_g1[:, k, :], x_t[:, slot, k, :],
                                               start=(k == 0), stop=(k == 1))
                    ins.then_inc(g1_ready, 1)
                    for m in range(4):
                        wait(pe, raw_ready, 4 * g + m - 1)
                        for k in range(2):
                            ins = nc.tensor.matmul(ps_qk[:, m % 2, :], w_qk[:, k, m * P:(m + 1) * P],
                                                   x_t[:, slot, k, :], start=(k == 0), stop=(k == 1))
                        ins.then_inc(qk_ready, 1)
                    if not (last and slot == 1):
                        transposes(*group_after(b, slot))
                    for t in range(GT):
                        wait(pe, v_read, 2 * (GT * g + t - 1))
                        for k in range(2):
                            ins = nc.tensor.matmul(ps_v[:, t % 2, 0:DIM + COLS], x_t[:, slot, k, t * P:(t + 1) * P],
                                                   w_vs[:, k, :], start=(k == 0), stop=(k == 1))
                        ins.then_inc(v_ready, 1)
                    wait(pe, hid_ready, g + 1)
                    wait(pe, z_read, g)
                    for t in range(GT):
                        ins = nc.tensor.matmul(ps_g2[:, t * COLS:(t + 1) * COLS], hid[:, slot, t * P:(t + 1) * P],
                                               w_g2[:, :], start=True, stop=True)
                    ins.then_inc(g2_ready, 1)

            over_batches(pe, body)


def route(nc, d, keep):
    with ExitStack() as ctx:
        sb = lambda n, s, t=FP32: ctx.enter_context(nc.sbuf_tensor("r_" + n, s, t))
        pb = lambda n, s: ctx.enter_context(nc.psum_tensor("r_" + n, s, FP32))
        sem = lambda n: ctx.enter_context(nc.semaphore("r_" + n))

        TC = [P, TILES, COLS]
        CT = [P, COLS, TILES]
        cemb = sb("cemb", [P, COLS, DIM])
        b_g2 = sb("b_g2", [P, COLS])
        col_rank = sb("col_rank", [P, COLS])
        tile_start = sb("tile_start", [P, SLOTS])
        before = sb("before", [P, P], BF16)
        ones = sb("ones", [P, P], BF16)
        half_neg = sb("half_neg", [P, TILES])
        c_norm = sb("c_norm", [P, COLS])
        t_norm = sb("t_norm", [P, TILES])
        rstd = sb("rstd", [P, TILES])
        lg = sb("lg", TC)
        ez = sb("ez", TC)
        top = sb("top", [P, TILES])
        pick = sb("pick", TC)
        pick_bf = sb("pick_bf", TC, BF16)
        esum = sb("esum", [P, TILES])
        total = sb("total", CT)
        seen = sb("seen", CT)
        small = sb("small", [P, 6, COLS])
        small_i = sb("small_i", [P, COLS], I32)
        place = sb("place", TC)
        place_f = sb("place_f", [P, TILES])
        tile_cmp = sb("tile_cmp", [P, SLOTS, COLS])
        tile_col = sb("tile_col", [P, SLOTS])
        ps_before = pb("ps_before", [P, TILES * COLS])
        ps_total = pb("ps_total", [P, TILES * COLS])

        loaded = sem("loaded")
        set_up = sem("set_up")
        bias_in = sem("bias_in")
        gate_exp = sem("gate_exp")
        norm_sq = sem("norm_sq")
        norms = sem("norms")
        shifted = sem("shifted")
        soft_exp = sem("soft_exp")
        picked = sem("picked")
        counted = sem("counted")
        step = sem("step")
        placed = sem("placed")
        block = ctx.enter_context(nc.Block())

        @block.sync
        def _(sp):
            sp.dma_start(cemb[:, :, :], d["col_emb"].unsqueeze(0).to_broadcast([P, COLS, DIM])).then_inc(loaded, 16)
            sp.dma_start(b_g2[:, :], d["gate_b2"].unsqueeze(0).to_broadcast([P, COLS])).then_inc(loaded, 16)
            sp.dma_start(col_rank[:, :], d["col_rank"].unsqueeze(0).to_broadcast([P, COLS])).then_inc(loaded, 16)
            sp.dma_start(tile_start[:, :], d["tile_start"].unsqueeze(0).to_broadcast([P, SLOTS])).then_inc(loaded, 16)

        @block.gpsimd
        def _(pool):
            pool.memset(ones[:, :], 1.0).then_inc(set_up, 1)
            pool.memset(half_neg[:, :], -0.5).then_inc(set_up, 1)
            pool.memset(before[:, :], 1.0).then_inc(set_up, 1)
            pool.wait_ge(set_up, 3)
            nc.gpsimd.affine_select(out=before[:, :], in_=before[:, :], compare_op=ALU.is_gt, fill=0.0, base=0,
                                    pattern=[[1, P]], channel_multiplier=-1).then_inc(set_up, 1)
            nc.gpsimd.tensor_scalar(rstd[:, :], keep["mv"][:, :, 1], LN_EPS, None, ALU.add).then_inc(norms, 1)
            pool.wait_ge(norms, 1)
            nc.gpsimd.tensor_tensor(rstd[:, :], rstd[:, :], half_neg[:, :], ALU.pow).then_inc(norms, 1)
            pool.wait_ge(norm_sq, 1)
            nc.gpsimd.tensor_tensor(t_norm[:, :], t_norm[:, :], half_neg[:, :], ALU.pow).then_inc(norms, 1)
            nc.gpsimd.tensor_tensor(c_norm[:, :], c_norm[:, :], half_neg[:, 0:COLS], ALU.pow).then_inc(norms, 1)

        @block.scalar
        def _(act):
            act.wait_ge(bias_in, 1)
            nc.scalar.activation(ez[:, :, :], lg[:, :, :], ACT.Exp, scale=-1.0).then_inc(gate_exp, 1)
            act.wait_ge(shifted, 1)
            nc.scalar.activation(ez[:, :, :], place[:, :, :], ACT.Exp).then_inc(soft_exp, 1)

        @block.tensor
        def _(pe):
            pe.wait_ge(set_up, 4)
            pe.wait_ge(picked, 1)
            flat = pick_bf[:, :, :].rearrange("p t c -> p (t c)")
            for weights, ps in ((before, ps_before), (ones, ps_total)):
                for i in range(2):
                    ins = nc.tensor.matmul(ps[:, i * 512:(i + 1) * 512], weights[:, :], flat[:, i * 512:(i + 1) * 512],
                                           start=True, stop=True)
            ins.then_inc(counted, 1)

        @block.vector
        def _(dve):
            chain = [0]

            def link(ins):
                chain[0] += 1
                ins.then_inc(step, 1)
                dve.wait_ge(step, chain[0])

            v = nc.vector
            per_tok = lambda a: a[:, :].unsqueeze(2).to_broadcast(TC)
            per_col = lambda a: a.unsqueeze(1).to_broadcast(TC)
            dve.wait_ge(loaded, 16 * 4)
            link(v.tensor_tensor(lg[:, :, :], keep["z"][:, :, :], per_col(b_g2[:, :]), ALU.add))
            v.tensor_scalar_max(lg[:, :, :], lg[:, :, :], SIGMOID_MIN).then_inc(bias_in, 1)
            link(v.tensor_tensor(cemb[:, :, :], cemb[:, :, :], cemb[:, :, :], ALU.mult))
            link(v.reduce_sum(c_norm[:, :], cemb[:, :, :], AX.X))
            link(v.tensor_scalar_max(c_norm[:, :], c_norm[:, :], NORM2_MIN))
            dve.wait_ge(norms, 2)
            link(v.tensor_tensor(t_norm[:, :], rstd[:, :], rstd[:, :], ALU.mult))
            link(v.tensor_tensor(t_norm[:, :], t_norm[:, :], keep["mv"][:, :, 1], ALU.mult))
            v.tensor_scalar(t_norm[:, :], t_norm[:, :], float(DIM), NORM2_MIN, ALU.mult, ALU.max).then_inc(norm_sq, 1)
            dve.wait_ge(gate_exp, 1)
            link(v.tensor_scalar_add(ez[:, :, :], ez[:, :, :], 1.0))
            link(v.reciprocal(lg[:, :, :], ez[:, :, :]))
            dve.wait_ge(norms, 4)
            link(v.tensor_tensor(place[:, :, :], keep["sim"][:, :, :], per_tok(t_norm), ALU.mult))
            link(v.tensor_tensor(place[:, :, :], place[:, :, :], per_col(c_norm[:, :]), ALU.mult))
            link(v.tensor_tensor(lg[:, :, :], lg[:, :, :], place[:, :, :], ALU.add))
            link(v.reduce_max(top[:, :], lg[:, :, :], AX.X))
            v.tensor_tensor(place[:, :, :], lg[:, :, :], per_tok(top), ALU.subtract).then_inc(shifted, 1)
            link(v.tensor_tensor(pick[:, :, :], lg[:, :, :], per_tok(top), ALU.is_equal))
            link(v.tensor_tensor(pick[:, :, :], pick[:, :, :], per_col(col_rank[:, :]), ALU.mult))
            link(v.reduce_max(top[:, :], pick[:, :, :], AX.X))
            link(v.tensor_tensor(pick[:, :, :], pick[:, :, :], per_tok(top), ALU.is_equal))
            v.tensor_copy(pick_bf[:, :, :], pick[:, :, :]).then_inc(picked, 1)
            dve.wait_ge(soft_exp, 1)
            link(v.reduce_sum(esum[:, :], ez[:, :, :], AX.X))
            link(v.reciprocal(keep["weight"][:, :], esum[:, :]))
            dve.wait_ge(counted, 1)
            link(v.tensor_copy(total[:, :, :], ps_total[:, :].rearrange("p (t c) -> p c t", c=COLS)))
            flat = lambda a: a[:, :, :].rearrange("p c t -> p (c t)")
            link(v.tensor_tensor_scan(flat(seen), flat(total), flat(total), 0.0, ALU.add, ALU.bypass))
            count, padded, base, end, zero, first = (small[:, i, :] for i in range(6))
            link(v.memset(zero, 0.0))
            link(v.tensor_tensor(first, seen[:, :, 0], total[:, :, 0], ALU.subtract))
            link(v.tensor_tensor(count, seen[:, :, TILES - 1], first, ALU.subtract))
            link(v.tensor_tensor(seen[:, :, :], seen[:, :, :], total[:, :, :], ALU.subtract))
            link(v.tensor_scalar_add(small_i[:, :], count, float(P - 1)))
            link(v.tensor_single_scalar(small_i[:, :], small_i[:, :], -P, ALU.bitwise_and))
            link(v.tensor_copy(padded, small_i[:, :]))
            link(v.tensor_tensor_scan(end, padded, padded, 0.0, ALU.add, ALU.bypass))
            link(v.tensor_tensor(base, end, padded, ALU.subtract))
            link(v.tensor_tensor(base, base, first, ALU.subtract))
            link(v.tensor_tensor(place[:, :, :], ps_before[:, :].rearrange("p (t c) -> p t c", c=COLS),
                                 seen[:, :, :].rearrange("p c t -> p t c"), ALU.add))
            link(v.tensor_tensor(place[:, :, :], place[:, :, :], per_col(base), ALU.add))
            link(v.tensor_tensor(place[:, :, :], place[:, :, :], pick[:, :, :], ALU.mult))
            link(v.reduce_sum(place_f[:, :], place[:, :, :], AX.X))
            v.tensor_copy(keep["place"][:, :], place_f[:, :]).then_inc(placed, 1)
            starts = tile_start[:, :].unsqueeze(2).to_broadcast([P, SLOTS, COLS])
            link(v.tensor_tensor(tile_cmp[:, :, :], starts, end.unsqueeze(1).to_broadcast([P, SLOTS, COLS]), ALU.is_ge))
            link(v.reduce_sum(tile_col[:, :], tile_cmp[:, :, :], AX.X))
            link(v.tensor_scalar_min(keep["tile_col"][:, :], tile_col[:, :], float(COLS - 1)))


def attend(nc, d, keep):
    with ExitStack() as ctx:
        sb = lambda n, s, t=FP32: ctx.enter_context(nc.sbuf_tensor("a_" + n, s, t))
        pb = lambda n, s: ctx.enter_context(nc.psum_tensor("a_" + n, s, FP32))
        sem = lambda n: ctx.enter_context(nc.semaphore("a_" + n))

        RING = UNITS
        BANK = 512
        q_ops = sb("q_ops", [P, RING, UH, SEQ], BF16)
        k_ops = sb("k_ops", [P, RING, UH, SEQ], BF16)
        v_ops = sb("v_ops", [P, RING, QTILES, UH * VA])
        PROBS = 4
        probs = sb("probs", [P, PROBS, UH, BANK])
        future = sb("future", [P, SEQ])
        future_t = sb("future_t", [P, P], BF16)
        ident = sb("ident", [P, P], BF16)
        sums_out = sb("sums_out", [P, 4, SEQ], BF16)
        row_max = sb("row_max", [P, 2, UH * QTILES])
        max_rest = sb("max_rest", [P, 2, UH * QTILES])
        max_parts = sb("max_parts", [P, 2, 3, UH * QTILES], BF16)
        max_rows = sb("max_rows", [P, 2, P], BF16)
        o_out = sb("o_out", [P, 2, SEQ])
        proj_b = sb("proj_b", [P, DIM])

        MAX_BANKS, EXP_BANKS = 4, 3
        ps_max = pb("ps_max", [P, MAX_BANKS * BANK])
        ps_exp = pb("ps_exp", [P, EXP_BANKS, BANK])
        ps_o = pb("ps_o", [P, BANK])

        passed = sem("passed")
        set_up = sem("set_up")
        scattered = sem("scattered")
        bias_in = sem("bias_in")
        biased = sem("biased")
        o_clear = sem("o_clear")
        ops_in = [sem(f"ops_in{i}") for i in range(RING)]
        max_sent = [sem(f"max_sent{i}") for i in range(2)]
        max_in = [sem(f"max_in{i}") for i in range(RING)]
        scored = sem("scored")
        maxed = sem("maxed")
        split_step = sem("split_step")
        split_part = sem("split_part")
        split = sem("split")
        s_ready = sem("s_ready")
        exp_done = sem("exp_done")
        pv_done = sem("pv_done")
        o_read = sem("o_read")
        o_stored = [sem(f"o_stored{i}") for i in range(2)]
        block = ctx.enter_context(nc.Block())

        OPS_DMAS = 2 * len(TERMS) + 1
        GROUPS = [(0, kt) for kt in range(QTILES // 2)] + [(1, kt) for kt in range(QTILES)]
        NGROUP = len(GROUPS)
        PIECES = [(gi, j) for gi in range(NGROUP) for j in range(UH)]
        NPIECE = len(PIECES)
        CARRY = 2
        COPY_BEFORE = (UH * 6, UH * 2)

        def span(gi):
            half, kt = GROUPS[gi]
            return max(half * BANK, kt * P), (half + 1) * BANK

        MTILES = [(j, qt) for j in range(UH) for qt in range(QTILES)]
        TURN = "turn"
        TURN_AT = 8
        TILE_BANKS = [(qt,) if qt < 4 else (2 * (qt % 2), 2 * (qt % 2) + 1) for qt in range(QTILES)]
        TURN_BANKS = (0,)
        LEAD = 2 * len(MTILES) + 1
        PER_SLOT = len(MTILES) + 1

        def max_items(with_tiles, with_turn):
            items = list(MTILES) if with_tiles else []
            if with_turn:
                items.insert(min(TURN_AT, len(items)), TURN)
            return items

        def last_user():
            used, found, at = {}, [], 0
            slots = {(u, i): max_items(True, True)[i] for u in range(UNITS) for i in range(PER_SLOT)}
            for items in (dict(enumerate(MTILES + MTILES + [TURN])), slots, slots):
                found.append({})
                for key, item in items.items():
                    banks = TURN_BANKS if item == TURN else TILE_BANKS[item[1]]
                    found[-1][key] = at - max(used.get(k, -1) for k in banks)
                    used.update({k: at for k in banks})
                    at += 1
            return found

        def max_banks(item):
            banks = TURN_BANKS if item == TURN else TILE_BANKS[item[1]]
            return ps_max[:, banks[0] * BANK:(banks[-1] + 1) * BANK]

        def slot_flags(b, u, last):
            return (not (last and u >= 2)), (not (last and u == 3))

        def in_slots(eng, body):
            over_batches(eng, lambda b, first, last: [body(b, u, first, last) for u in range(UNITS)])

        @block.sync
        def _(sp):
            def load_ops(b, r):
                m, h0 = r // 2, (r % 2) * UH
                for which, ops in ((0, q_ops), (1, k_ops)):
                    for t, term in enumerate(TERMS):
                        src = d["qk_parts"][term[which], 2 * which + m, :, bass.ts(b, SEQ)]
                        src = src.rearrange("(i h) t -> i h t", h=8)[:, h0:h0 + UH, :]
                        dst = ops[t * HD:(t + 1) * HD, r, :, :]
                        sp.dma_start(dst, src).then_inc(ops_in[r], 16)
                src = d["v_aug"][bass.ts(b, SEQ), r * UH * VA:(r + 1) * UH * VA]
                sp.dma_start(v_ops[:, r, :, :], src.rearrange("(t p) e -> p t e", p=P)).then_inc(ops_in[r], 16)

            def store_o(b, r):
                n = UNITS * b + r
                wait_apart(sp, o_read, 2 * n + 2, passed)
                for j in range(UH):
                    sp.dma_start(d["heads_t"][r * UH + j, :, bass.ts(b, SEQ)],
                                 o_out[32 * j:32 * j + VA, r % 2, :]).then_inc(o_stored[r % 2], 16)

            def send_rows(r, slot, items, sent):
                wait_apart(sp, maxed, items, passed)
                sp.dma_start(d["max_rows"][slot], max_rows[0:3 * UH * QTILES, slot, :]).then_inc(max_sent[slot], 16)
                wait_apart(sp, max_sent[slot], 16 * sent, passed)
                src = d["max_rows"][slot].rearrange("(a h) q -> a (h q)", a=3)
                sp.dma_start(q_ops[SHIFT:KALL, r, :, :].rearrange("a h q -> a (h q)"), src).then_inc(max_in[r], 16)

            for r in range(3):
                load_ops(0, r)

            def body(b, u, first, last):
                n = UNITS * b + u
                if not (last and u >= 1):
                    wait_apart(sp, s_ready, NPIECE * n, passed)
                    wait_apart(sp, pv_done, NGROUP * n, passed)
                    load_ops(b if u == 0 else b + 1, (u + 3) % RING)
                if slot_flags(b, u, last)[1]:
                    r = (u + 1) % RING
                    turn = TURN_AT if slot_flags(b, u, last)[0] else 0
                    send_rows(r, (u + 1) % 2, LEAD + PER_SLOT * n + turn + 1, 2 * b + (u + 1) // 2 + 1)
                if not (first and u == 0):
                    store_o(b if u else b - 1, (u - 1) % UNITS)

            sp.dma_start(proj_b[:, :], d["proj_b"].unsqueeze(0).to_broadcast([P, DIM])).then_inc(bias_in, 16)
            send_rows(0, 0, LEAD, 1)
            in_slots(sp, body)
            store_o(BATCH - 1, UNITS - 1)
            for i in range(2):
                sp.wait_ge(o_stored[i], 16 * UH * UNITS * BATCH // 2)

        @block.gpsimd
        def _(pool):
            pool.memset(k_ops[SHIFT:KALL, :, :, :], 1.0).then_inc(set_up, 1)
            pool.wait_ge(set_up, 1)
            pool.memset(future_t[:, :], 0.0).then_inc(set_up, 1)
            pool.memset(future[:, :], 0.0).then_inc(set_up, 1)
            pool.memset(ident[:, :], 0.0).then_inc(set_up, 1)
            pool.wait_ge(set_up, 4)
            nc.gpsimd.affine_select(out=future[:, SEQ - P:SEQ], in_=future[:, SEQ - P:SEQ], compare_op=ALU.is_ge,
                                    fill=MASKED, base=0, pattern=[[-1, P]], channel_multiplier=1).then_inc(set_up, 1)
            nc.gpsimd.affine_select(out=future_t[:, :], in_=future_t[:, :], compare_op=ALU.is_ge, fill=MASKED, base=0,
                                    pattern=[[1, P]], channel_multiplier=-1).then_inc(set_up, 1)
            nc.gpsimd.affine_select(out=ident[:, :], in_=ident[:, :], compare_op=ALU.not_equal, fill=1.0, base=0,
                                    pattern=[[1, P]], channel_multiplier=-1).then_inc(set_up, 1)

            def split_max(n, slot, items):
                STEPS = 3
                rest, mp = max_rest[:, slot, :], max_parts[:, slot, :, :]
                wait(pool, maxed, items)
                settle(pool, passed)
                nc.gpsimd.tensor_scalar(rest, row_max[:, slot, :], -1.0, None, ALU.mult).then_inc(split_step, 1)
                wait(pool, split_step, STEPS * n + 1)
                for i in range(2):
                    settle(pool, passed)
                    nc.gpsimd.tensor_copy(mp[:, i, :], rest).then_inc(split_part, 1)
                    wait(pool, split_part, 2 * n + i + 1)
                    nc.gpsimd.tensor_tensor(rest, rest, mp[:, i, :], ALU.subtract).then_inc(split_step, 1)
                    wait(pool, split_step, STEPS * n + i + 2)
                settle(pool, passed)
                nc.gpsimd.tensor_copy(mp[:, 2, :], rest).then_inc(split, 1)

            def scatter(t0, t1):
                for t in range(t0, t1):
                    pool.indirect_dma_start(d["sorted_x"], bass.IndirectOffsetOnAxis(ap=keep["place"][:, t:t + 1], axis=0),
                                            keep["xn"][:, t, :], None).then_inc(scattered, 16)

            scatter(0, 20)
            split_max(0, 0, len(MTILES))
            scatter(20, 40)
            split_max(1, 1, 2 * len(MTILES))
            scatter(40, TILES)
            pool.wait_ge(scattered, 16 * TILES)
            pool.wait_ge(bias_in, 16)

            def body(b, u, first, last):
                n = UNITS * b + u
                if slot_flags(b, u, last)[0]:
                    split_max(n + 2, u % 2, LEAD + PER_SLOT * n + PER_SLOT)
                share = TILES // (UNITS * BATCH)
                rows = keep["xn"][:, bass.ts(n, share), :]
                nc.gpsimd.tensor_tensor(rows, rows, proj_b[:, :].unsqueeze(1).to_broadcast([P, share, DIM]),
                                        ALU.add).then_inc(biased, 1)

            in_slots(pool, body)

        @block.vector
        def _(dve):
            nc.vector.memset(ps_o[:, :], 0.0).then_inc(o_clear, 1)
            dve.wait_ge(set_up, 7)

            def max_item(at, ring, item, slot, sent=None):
                wait(dve, scored, at + 1)
                ps = max_banks(item)
                if item == TURN:
                    if sent:
                        wait(dve, *sent)
                    nc.vector.tensor_copy(max_rows[0:3 * UH * QTILES, slot, :],
                                          ps.bitcast(BF16)[0:3 * UH * QTILES, 0:P]).then_inc(maxed, 1)
                    return
                j, qt = item
                width = (qt + 1) * P
                wait(dve, maxed, at - 3)
                settle(dve, passed)
                nc.vector.tensor_tensor_reduce(
                    out=sums_out[:, ring, 0:width], in0=ps[:, 0:width], in1=future[:, SEQ - width:SEQ],
                    scale=1.0, scalar=MASKED, op0=ALU.add, op1=ALU.max,
                    accum_out=row_max[:, slot, j * QTILES + qt:j * QTILES + qt + 1]).then_inc(maxed, 1)

            for at in range(LEAD):
                item = TURN if at == LEAD - 1 else MTILES[at % len(MTILES)]
                max_item(at, at % 4, item, 0 if item == TURN else at // len(MTILES))

            def body(b, u, first, last):
                n = UNITS * b + u
                with_tiles, with_turn = slot_flags(b, u, last)
                if with_tiles:
                    wait(dve, split, n + 1)
                for i, item in enumerate(max_items(with_tiles, with_turn)):
                    sent = (max_sent[(u + 1) % 2], 16 * (2 * b + (u + 1) // 2))
                    turn = item == TURN
                    max_item(LEAD + PER_SLOT * n + i, (LEAD + PER_SLOT * u + i) % 4, item,
                             (u + 1) % 2 if turn else u % 2, sent if turn and not (first and u == 0) else None)

            in_slots(dve, body)

        @block.scalar
        def _(act):
            def copy_o(n, u, b, half):
                wait(act, pv_done, NGROUP * n + (UH if half == 0 else NGROUP))
                if half == 0:
                    wait(act, o_stored[u % 2], 16 * UH * (2 * b + u // 2))
                nc.scalar.activation(o_out[:, u % 2, half * BANK:(half + 1) * BANK], ps_o[:, :],
                                     ACT.Copy).then_inc(o_read, 1)

            def body(b, u, first, last):
                n = UNITS * b + u
                for i, (gi, j) in enumerate(PIECES):
                    if i == COPY_BEFORE[1] and not (first and u == 0):
                        copy_o(n - 1, (u - 1) % UNITS, b if u else b - 1, 1)
                    if i == COPY_BEFORE[0]:
                        copy_o(n, u, b, 0)
                    if j == 0:
                        wait(act, pv_done, NGROUP * n + gi - PROBS + 1)
                    wait(act, s_ready, NPIECE * n + i + 1)
                    width = span(gi)[1] - span(gi)[0]
                    nc.scalar.activation(probs[:, gi % PROBS, j, 0:width], ps_exp[:, i % EXP_BANKS, 0:width],
                                         ACT.Exp).then_inc(exp_done, 1)

            in_slots(act, body)
            copy_o(UNITS * BATCH - 1, UNITS - 1, BATCH - 1, 1)

        @block.tensor
        def _(pe):
            back_ahead, back_first, back_later = last_user()

            def max_item(at, back, item, r, slot):
                wait(pe, maxed, at - back + 1)
                ps = max_banks(item)
                if item == TURN:
                    rows = 3 * UH * QTILES
                    nc.tensor.transpose(ps.bitcast(BF16)[0:rows, 0:P],
                                        max_parts[:, slot, :, :].rearrange("p a c -> p (a c)"),
                                        ident[:, :]).then_inc(scored, 1)
                    return
                j, qt = item
                width = (qt + 1) * P
                for k in range(0, width, BANK):
                    end = min(k + BANK, width)
                    ins = nc.tensor.matmul(ps[:, k:end], q_ops[0:KROWS, r, j, qt * P:width],
                                           k_ops[0:KROWS, r, j, k:end], start=True, stop=True)
                ins.then_inc(scored, 1)

            def score_piece(n, u, i):
                gi, j = PIECES[i]
                kt = GROUPS[gi][1]
                q0, q1 = span(gi)
                wait(pe, exp_done, NPIECE * n + i - EXP_BANKS + 1)
                ps = ps_exp[:, i % EXP_BANKS, :]
                diagonal = q0 == kt * P
                ins = nc.tensor.matmul(ps[:, 0:q1 - q0], k_ops[0:KALL, u, j, kt * P:(kt + 1) * P],
                                       q_ops[0:KALL, u, j, q0:q1], start=True, stop=not diagonal)
                if diagonal:
                    ins = nc.tensor.matmul(ps[:, 0:P], ident[:, :], future_t[:, :], start=False, stop=True)
                ins.then_inc(s_ready, 1)

            def value_group(n, u, gi):
                half, kt = GROUPS[gi]
                q0, q1 = span(gi)
                wait(pe, exp_done, NPIECE * n + UH * (gi + 1))
                if kt == 0:
                    wait(pe, o_read, 2 * n + half)
                for j in range(UH):
                    ins = nc.tensor.matmul(ps_o[32 * j:32 * j + VA, q0 - half * BANK:q1 - half * BANK],
                                           v_ops[:, u, kt, j * VA:(j + 1) * VA], probs[:, gi % PROBS, j, 0:q1 - q0],
                                           start=(kt == 0), stop=(q0 == q1 - P))
                ins.then_inc(pv_done, 1)

            def plan(items, carry):
                HOP = 0.2
                values = [(-1, gi) for gi in range(NGROUP - CARRY, NGROUP)] if carry else []
                values += [(0, gi) for gi in range(NGROUP - CARRY)]
                order, now, act, dve = [], 0.0, 0.0, 0.0
                exp_end, max_end, val_end = {}, {}, {}
                opened = {0: 0.0, 1: 0.0}
                i = im = iv = 0

                def score_at():
                    if i == NPIECE:
                        return None
                    if i >= COPY_BEFORE[1] and any(v[0] < 0 for v in values[iv:]):
                        return None
                    if i >= COPY_BEFORE[0] and (0, UH - 1) in values[iv:]:
                        return None
                    gi = i // UH
                    own = [v for v in values[iv:] if v[0] == 0 and v[1] <= gi - PROBS]
                    old = [v for v in values[iv:] if v[0] < 0 and v[1] - NGROUP <= gi - PROBS]
                    return None if own or old else max(now, exp_end.get(i - EXP_BANKS, 0.0) + HOP)

                def max_at():
                    if im == len(items):
                        return None
                    return max(now, max_end.get(im - 2, 0.0) + HOP)

                def value_at():
                    if iv == len(values):
                        return None
                    old, gi = values[iv]
                    if old:
                        return now
                    last = UH * gi + UH - 1
                    if last not in exp_end:
                        return None
                    if GROUPS[gi] == (0, 0) and carry and i < COPY_BEFORE[1] + 1:
                        return None
                    if GROUPS[gi] == (1, 0) and i < COPY_BEFORE[0] + 1:
                        return None
                    return max(now, exp_end[last] + HOP, opened[GROUPS[gi][0]] if GROUPS[gi][1] == 0 else 0.0)

                while i < NPIECE or im < len(items) or iv < len(values):
                    starts = [(at, rank, kind) for kind, at, rank in (
                        ("score", score_at(), act - now), ("max", max_at(), dve - now),
                        ("value", value_at(), 1.0)) if at is not None]
                    starts = [(max(at, now + 0.0), rank, kind) for at, rank, kind in starts]
                    at, _, kind = min(starts)
                    if kind == "score":
                        order.append(("score", i))
                        q0, q1 = span(i // UH)
                        now = at + (q1 - q0) / 2400 + (0.056 if q0 == GROUPS[i // UH][1] * P else 0.0)
                        if i == COPY_BEFORE[0] or (i == COPY_BEFORE[1] and carry):
                            act = max(act, val_end.get(UH - 1, 0.0) + HOP) + 0.48
                            opened[1 if i == COPY_BEFORE[0] else 0] = act + HOP
                        act = max(act, now + HOP) + (q1 - q0) / 1200 + 0.055
                        exp_end[i] = act
                        i += 1
                    elif kind == "max":
                        order.append(("max", im))
                        width = P if items[im] == TURN else (items[im][1] + 1) * P
                        now = at + width / 2400
                        dve = max(dve, now + HOP) + width / 960 + 0.12
                        max_end[im] = dve
                        im += 1
                    else:
                        order.append(("value", values[iv]))
                        q0, q1 = span(values[iv][1])
                        now = at + (q1 - q0) / 600 + 0.06
                        if values[iv][0] == 0:
                            val_end[values[iv][1]] = now
                        iv += 1
                return order

            pe.wait_ge(set_up, 7)
            pe.wait_ge(o_clear, 1)
            for at in range(LEAD):
                item = TURN if at == LEAD - 1 else MTILES[at % len(MTILES)]
                unit = at // len(MTILES)
                if item == TURN:
                    pe.wait_ge(split, 1)
                elif at % len(MTILES) == 0:
                    pe.wait_ge(ops_in[unit], 16 * OPS_DMAS)
                max_item(at, back_ahead[at], item, unit, 0)

            def body(b, u, first, last):
                n = UNITS * b + u
                with_tiles, with_turn = slot_flags(b, u, last)
                items = max_items(with_tiles, with_turn)
                for kind, what in plan(items, not (first and u == 0)):
                    if kind == "score":
                        if what == 0:
                            wait(pe, max_in[u], 16 * (b + 1))
                        score_piece(n, u, what)
                    elif kind == "value":
                        old, gi = what
                        value_group(n + old, (u + old) % UNITS, gi)
                    else:
                        if items[what] == TURN:
                            wait(pe, split, n + 2)
                        elif what == 0:
                            wait(pe, ops_in[(u + 2) % RING], 16 * OPS_DMAS * (b + 1 + (u + 2) // UNITS))
                        back = (back_first if first else back_later)[u, what] if with_tiles else 1
                        max_item(LEAD + PER_SLOT * n + what, back, items[what], (u + 2) % RING, (u + 1) % 2)

            in_slots(pe, body)
            for gi in range(NGROUP - CARRY, NGROUP):
                value_group(UNITS * BATCH - 1, UNITS - 1, gi)


def columns(nc, d, keep):
    with ExitStack() as ctx:
        sb = lambda n, s, t=FP32: ctx.enter_context(nc.sbuf_tensor("c_" + n, s, t))
        pb = lambda n, s: ctx.enter_context(nc.psum_tensor("c_" + n, s, FP32))
        sem = lambda n: ctx.enter_context(nc.semaphore("c_" + n))

        QUAD = 4
        QUADS = SLOTS // QUAD
        ident = sb("ident", [P, P])
        sums = sb("sums", [P, HEADS * TOK // P])
        w_up = sb("w_up", [P, COLS, 2, NEUR])
        w_down = sb("w_down", [NEUR, COLS, DIM + 1])
        xs = sb("xs", [P, 2, QUAD, DIM])
        xs_t = sb("xs_t", [P, 2, 2, P])
        w_tile = sb("w_tile", [P, 2, 2, NEUR])
        bias = sb("bias", [NEUR, 2])
        act_t = sb("act_t", [NEUR, 2, P])
        y = sb("y", [P, 2, QUAD, DIM])
        ps_t = pb("ps_t", [P, 2, 512])
        ps_up = pb("ps_up", [P, 2, 512])
        ps_y = pb("ps_y", [P, 2, 512])

        consts_in = sem("consts_in")
        sums_in = sem("sums_in")
        inverted = sem("inverted")
        sums_out = sem("sums_out")
        passed = sem("passed")
        xs_in = [sem(f"xs_in{i}") for i in range(2)]
        turned = sem("turned")
        xt_ready = sem("xt_ready")
        chosen = sem("chosen")
        up_ready = sem("up_ready")
        act_ready = sem("act_ready")
        y_ready = sem("y_ready")
        y_copied = sem("y_copied")
        y_out = [sem(f"y_out{i}") for i in range(2)]
        block = ctx.enter_context(nc.Block())
        N_CONSTS = 3

        def over_tiles(eng, body):
            over(eng, QUADS // 2, lambda p, first, last: [body(p, r, first, last) for r in range(2 * QUAD)])

        def column_of(eng, t):
            return eng.value_load(keep["tile_col"][0:1, bass.ds(t, 1)], min_val=0, max_val=COLS - 1)

        @block.sync
        def _(sp):
            def load_quad(p, s):
                src = d["sorted_x"][bass.ts(2 * p + s, QUAD * P), :].rearrange("(t p) c -> p t c", p=P)
                sp.dma_start(xs[:, s, :, :], src).then_inc(xs_in[s], 16)

            sp.dma_start(ident[:, :], d["ident"]).then_inc(consts_in, 16)
            load_quad(0, 0)
            sp.dma_start(w_up[:, :, :, :], d["w_up"].rearrange("c p k n -> p c k n")).then_inc(consts_in, 16)
            sp.dma_start(w_down[:, :, :], d["w_down"].rearrange("c p n -> p c n")).then_inc(consts_in, 16)
            load_quad(0, 1)
            sp.dma_start(sums[:, :], d["heads_t"][:, HD, :].rearrange("h (c t) -> h c t", c=P // HEADS)).then_inc(sums_in, 16)
            sp.wait_ge(inverted, 1)
            sp.dma_start(d["inv_sum"].rearrange("h (c t) -> h c t", c=P // HEADS), sums[:, :]).then_inc(sums_out, 16)

            def body(p, first, last):
                for s in range(2):
                    if not last:
                        wait_apart(sp, turned, QUAD * (2 * p + s + 1), passed)
                        load_quad(p + 1, s)
                    wait_apart(sp, y_copied, QUAD * (2 * p + s + 1), passed)
                    sp.dma_start(d["sorted_y"][bass.ts(2 * p + s, QUAD * P), :].rearrange("(t p) c -> p t c", p=P),
                                 y[:, s, :, :]).then_inc(y_out[s], 16)

            over(sp, QUADS // 2, body)
            sp.wait_ge(y_out[0], 16 * QUADS // 2)
            sp.wait_ge(y_out[1], 16 * QUADS // 2)
            sp.wait_ge(sums_out, 16)

        @block.vector
        def _(dve):
            dve.wait_ge(consts_in, 16 * N_CONSTS)

            def body(p, r, first, last):
                t = 2 * QUAD * p + r
                col = column_of(dve, t)
                wait(dve, act_ready, t - 1)
                nc.vector.tensor_copy(w_tile[:, r % 2, :, :], w_up[:, bass.ds(col, 1), :, :].rearrange(
                    "p a k n -> p (a k) n")).then_inc(chosen, 1)
                nc.vector.tensor_copy(bias[:, r % 2:r % 2 + 1], w_down[:, bass.ds(col, 1), DIM:DIM + 1].rearrange(
                    "p a n -> p (a n)")).then_inc(chosen, 1)
                wait(dve, turned, t + 1)
                wait(dve, up_ready, t - 1)
                nc.vector.tensor_copy(xs_t[:, r % 2, :, :].rearrange("p k t -> p (k t)"),
                                      ps_t[:, r % 2, 0:2 * P]).then_inc(xt_ready, 1)
                if first and r == QUAD:
                    dve.wait_ge(sums_in, 16)
                    nc.vector.reciprocal(sums[:, :], sums[:, :]).then_inc(inverted, 1)

            over_tiles(dve, body)

        @block.scalar
        def _(act):
            def copy_y(p, r):
                t = 2 * QUAD * p + r
                wait(act, y_ready, t + 1)
                wait(act, y_out[r // QUAD], 16 * p)
                nc.scalar.activation(y[:, r // QUAD, r % QUAD, :], ps_y[:, r % 2, 0:DIM], ACT.Copy).then_inc(y_copied, 1)

            def body(p, r, first, last):
                t = 2 * QUAD * p + r
                wait(act, up_ready, t + 1)
                wait(act, chosen, 2 * t + 2)
                wait(act, y_ready, t - 1)
                nc.scalar.activation(act_t[:, r % 2, :], ps_up[0:NEUR, r % 2, 0:P], ACT.Gelu,
                                     bias=bias[:, r % 2:r % 2 + 1]).then_inc(act_ready, 1)
                if not (first and r == 0):
                    copy_y(*((p, r - 1) if r else (p - 1, 2 * QUAD - 1)))

            over_tiles(act, body)
            copy_y(QUADS // 2 - 1, 2 * QUAD - 1)

        @block.tensor
        def _(pe):
            def turn(p, r):
                t = 2 * QUAD * p + r
                wait(pe, xs_in[r // QUAD], 16 * (p + 1))
                wait(pe, xt_ready, t - 1)
                for k in range(2):
                    ins = nc.tensor.transpose(ps_t[:, r % 2, k * P:(k + 1) * P],
                                              xs[:, r // QUAD, r % QUAD, k * P:(k + 1) * P], ident[:, :])
                ins.then_inc(turned, 1)

            def down(t, r):
                col = column_of(pe, t)
                wait(pe, act_ready, t + 1)
                wait(pe, y_copied, t - 1)
                nc.tensor.matmul(ps_y[:, r % 2, 0:DIM], act_t[:, r % 2, :],
                                 w_down[:, bass.ds(col, 1), 0:DIM].rearrange("p a n -> p (a n)"),
                                 start=True, stop=True).then_inc(y_ready, 1)

            pe.wait_ge(consts_in, 16 * N_CONSTS)
            turn(0, 0)

            def body(p, r, first, last):
                t = 2 * QUAD * p + r
                if not (last and r == 2 * QUAD - 1):
                    turn(p + (r + 1) // (2 * QUAD), (r + 1) % (2 * QUAD))
                wait(pe, chosen, 2 * t + 2)
                wait(pe, xt_ready, t + 1)
                wait(pe, act_ready, t - 1)
                for k in range(2):
                    ins = nc.tensor.matmul(ps_up[0:NEUR, r % 2, 0:P],
                                           w_tile[:, r % 2, k, :], xs_t[:, r % 2, k, :], start=(k == 0), stop=(k == 1))
                ins.then_inc(up_ready, 1)
                if not (first and r == 0):
                    down(t - 1, (r - 1) % 2)

            over_tiles(pe, body)
            down(SLOTS - 1, 1)


def combine(nc, d, keep):
    with ExitStack() as ctx:
        sb = lambda n, s, t=FP32: ctx.enter_context(nc.sbuf_tensor("o_" + n, s, t))
        pb = lambda n, s: ctx.enter_context(nc.psum_tensor("o_" + n, s, FP32))
        sem = lambda n: ctx.enter_context(nc.semaphore("o_" + n))

        RING = 4
        ROUNDS = TOK // GROUP // RING
        AHEAD = 2
        SHARE = 3
        ident = sb("ident", [P, P])
        w_o = sb("w_o", [P, 2, DIM])
        ln_g = sb("ln_g", [P, DIM])
        ln_b = sb("ln_b", [P, DIM])
        b_rest = sb("b_rest", [P, DIM])
        b_parts = sb("b_parts", [P, 3, DIM], BF16)
        ones = sb("ones", [P, P], BF16)
        neg_half = sb("neg_half", [P, GT])
        x_in = sb("x_in", [P, RING, GT, DIM])
        heads = sb("heads", [P, RING, 2, GROUP])
        inv = sb("inv", [P, RING, 2, GROUP])
        rows = sb("rows", [P, RING, GT, DIM])
        cen = sb("cen", [P, 2, GT, DIM])
        res = sb("res", [P, 2, GT, DIM])
        stats = sb("stats", [P, 2, GT, 6])
        mv = sb("mv", [P, 2, GT, 2])
        neg_mean = sb("neg_mean", [P, 2, GT])
        rstd = sb("rstd", [P, 2, GT])
        ps = pb("ps", [P, 2, GT * DIM])
        place = sb("place", [P, 2, GT], U32)

        passed = sem("passed")
        consts_in = sem("consts_in")
        placed = sem("placed")
        set_up = sem("set_up")
        b_split = sem("b_split")
        att_in = [sem(f"att_in{i}") for i in range(RING)]
        rows_in = [sem(f"rows_in{i}") for i in range(RING)]
        scaled = sem("scaled")
        mixed = sem("mixed")
        stats_done = sem("stats_done")
        mv_done = sem("mv_done")
        negated = sem("negated")
        centred = sem("centred")
        var_eps = sem("var_eps")
        rstd_done = sem("rstd_done")
        gained = sem("gained")
        pool_normed = sem("pool_normed")
        pool_gained = sem("pool_gained")
        ps_ready = sem("ps_ready")
        summed = sem("summed")
        stored = [sem(f"stored{i}") for i in range(2)]
        block = ctx.enter_context(nc.Block())
        N_CONSTS = 4

        def over_groups(eng, body):
            over(eng, ROUNDS, lambda c, first, last: [body(c, r, first, last) for r in range(RING)])

        def later(c, r, by):
            return c + (r + by) // RING, (r + by) % RING

        @block.sync
        def _(sp):
            def load(c, r):
                g = RING * c + r
                toks = bass.ts(g, GROUP)
                for k in range(2):
                    hs = slice(8 * k, 8 * k + 8)
                    sp.dma_start(heads[:, r, k, :], d["heads_t"][hs, 0:HD, toks]).then_inc(att_in[r], 16)
                    sp.dma_start(inv[:, r, k, :],
                                 d["inv_sum"][hs, toks].unsqueeze(1).to_broadcast([8, HD, GROUP])).then_inc(att_in[r], 16)
                sp.dma_start(x_in[:, r, :, :], d["x"][toks, :].rearrange("(t p) c -> p t c", p=P)).then_inc(att_in[r], 16)

            load(0, 0)
            for dst, src in ((ln_g, "ln_g"), (ln_b, "ln_b")):
                sp.dma_start(dst[:, :], d[src].unsqueeze(0).to_broadcast([P, DIM])).then_inc(consts_in, 16)
            sp.dma_start(ident[:, :], d["ident"]).then_inc(consts_in, 16)
            sp.dma_start(w_o[:, :, :], d["wo_t"].rearrange("(k p) n -> p k n", p=P)).then_inc(consts_in, 16)
            for r in range(1, RING):
                load(0, r)

            def body(c, r, first, last):
                g = RING * c + r
                if not last:
                    wait_apart(sp, ps_ready, g + 1, passed)
                    load(c + 1, r)
                wait_apart(sp, summed, g + 1, passed)
                sp.dma_start(d["out"][bass.ts(g, GROUP), :].rearrange("(t p) c -> p t c", p=P),
                             res[:, r % 2, :, :]).then_inc(stored[r % 2], 16)

            over_groups(sp, body)
            sp.wait_ge(stored[0], 16 * RING * ROUNDS // 2)
            sp.wait_ge(stored[1], 16 * RING * ROUNDS // 2)

        @block.gpsimd
        def _(pool):
            pool.memset(neg_half[:, :], -0.5).then_inc(set_up, 1)
            pool.memset(ones[:, :], 1.0).then_inc(set_up, 1)

            def fetch(c, r):
                g = RING * c + r
                wait(pool, centred, g - RING + 1)
                wait(pool, rows_in[(r - 2) % RING], 16 * GT * (c if r >= 2 else c - 1) + 16 * GT)
                settle(pool, passed)
                nc.gpsimd.tensor_copy(place[:, r % 2, :], keep["place"][:, bass.ts(g, GT)]).then_inc(placed, 1)
                wait(pool, placed, g + 1)
                settle(pool, passed)
                for t in range(GT):
                    at = bass.IndirectOffsetOnAxis(ap=place[:, r % 2, t:t + 1], axis=0)
                    nc.gpsimd.indirect_dma_start(rows[:, r, t, :], None, d["sorted_y"], at).then_inc(rows_in[r], 16)

            for r in range(AHEAD):
                fetch(0, r)
            pool.wait_ge(set_up, 2)
            pool.wait_ge(consts_in, 16 * N_CONSTS)

            def body(c, r, first, last):
                g, slot = RING * c + r, r % 2
                wait(pool, mv_done, GT * g + GT)
                wait(pool, gained, g - 1)
                settle(pool, passed)
                nc.gpsimd.tensor_scalar(rstd[:, slot, :], mv[:, slot, :, 1], LN_EPS, None, ALU.add).then_inc(var_eps, 1)
                wait(pool, var_eps, g + 1)
                nc.gpsimd.tensor_tensor(rstd[:, slot, :], rstd[:, slot, :], neg_half[:, :], ALU.pow).then_inc(rstd_done, 1)
                wait(pool, centred, g + 1)
                wait(pool, rstd_done, g + 1)
                tile, shape = cen[:, slot, SHARE:GT, :], [P, GT - SHARE, DIM]
                nc.gpsimd.tensor_tensor(tile, tile, rstd[:, slot, SHARE:GT].unsqueeze(2).to_broadcast(shape),
                                        ALU.mult).then_inc(pool_normed, 1)
                wait(pool, pool_normed, g + 1)
                nc.gpsimd.tensor_tensor(tile, tile, ln_g[:, :].unsqueeze(1).to_broadcast(shape),
                                        ALU.mult).then_inc(pool_gained, 1)
                if not (last and r >= RING - AHEAD):
                    fetch(*later(c, r, AHEAD))

            over_groups(pool, body)

        @block.scalar
        def _(act):
            def body(c, r, first, last):
                g, slot = RING * c + r, r % 2
                wait(act, negated, g + 1)
                wait(act, summed, g - 1)
                for t in range(GT):
                    ins = nc.scalar.activation(cen[:, slot, t, :], rows[:, r, t, :], ACT.Identity,
                                               bias=neg_mean[:, slot, t:t + 1])
                ins.then_inc(centred, 1)

            over_groups(act, body)

        @block.vector
        def _(dve):
            dve.wait_ge(consts_in, 16 * N_CONSTS)
            nc.vector.tensor_copy(b_parts[:, 0, :], ln_b[:, :]).then_inc(b_split, 1)
            dve.wait_ge(b_split, 1)
            nc.vector.tensor_tensor(b_rest[:, :], ln_b[:, :], b_parts[:, 0, :], ALU.subtract).then_inc(b_split, 1)
            dve.wait_ge(b_split, 2)
            nc.vector.tensor_copy(b_parts[:, 1, :], b_rest[:, :]).then_inc(b_split, 1)
            dve.wait_ge(b_split, 3)
            nc.vector.tensor_tensor(b_rest[:, :], b_rest[:, :], b_parts[:, 1, :], ALU.subtract).then_inc(b_split, 1)
            dve.wait_ge(b_split, 4)
            nc.vector.tensor_copy(b_parts[:, 2, :], b_rest[:, :]).then_inc(b_split, 1)

            def mix(c, r):
                g, slot = RING * c + r, r % 2
                wait(dve, att_in[r], 16 * 5 * (c + 1))
                nc.vector.tensor_tensor(heads[:, r, :, :], heads[:, r, :, :], inv[:, r, :, :],
                                        ALU.mult).then_inc(scaled, 1)
                wait(dve, rows_in[r], 16 * GT * (c + 1))
                for t in range(GT):
                    nc.vector.scalar_tensor_tensor(out=rows[:, r, t, :], in0=rows[:, r, t, :],
                                                   scalar=keep["weight"][:, bass.ds(GT * g + t, 1)],
                                                   in1=keep["xn"][:, bass.ds(GT * g + t, 1), :].rearrange("p a c -> p (a c)"),
                                                   op0=ALU.mult, op1=ALU.add).then_inc(mixed, 1)
                for t in range(GT):
                    wait(dve, mixed, GT * g + t + 1)
                    wait(dve, mv_done, GT * (g - 2) + t + 1)
                    nc.vector.bn_stats(stats[:, slot, t, :], rows[:, r, t, :]).then_inc(stats_done, 1)
                wait(dve, rstd_done, g - 1)
                for t in range(GT):
                    wait(dve, stats_done, GT * g + t + 1)
                    settle(dve, passed)
                    nc.vector.bn_aggr(mv[:, slot, t, :], stats[:, slot, t, :]).then_inc(mv_done, 1)
                wait(dve, mv_done, GT * g + GT)
                wait(dve, centred, g - 1)
                nc.vector.tensor_scalar(neg_mean[:, slot, :], mv[:, slot, :, 0], -1.0, None, ALU.mult).then_inc(negated, 1)

            mix(0, 0)

            def body(c, r, first, last):
                g, slot = RING * c + r, r % 2
                if not (last and r == RING - 1):
                    mix(*later(c, r, 1))
                wait(dve, rstd_done, g + 1)
                wait(dve, centred, g + 1)
                for t in range(SHARE):
                    ins = nc.vector.scalar_tensor_tensor(out=cen[:, slot, t, :], in0=cen[:, slot, t, :],
                                                         scalar=rstd[:, slot, t:t + 1], in1=ln_g[:, :],
                                                         op0=ALU.mult, op1=ALU.mult)
                ins.then_inc(gained, 1)
                wait(dve, gained, g + 1)
                wait(dve, pool_gained, g + 1)
                wait(dve, ps_ready, g + 1)
                wait(dve, stored[slot], 16 * (2 * c + r // 2))
                nc.vector.tensor_tensor(res[:, slot, :, :].rearrange("p t c -> p (t c)"), ps[:, slot, :],
                                        cen[:, slot, :, :].rearrange("p t c -> p (t c)"), ALU.add).then_inc(summed, 1)

            over_groups(dve, body)

        @block.tensor
        def _(pe):
            pe.wait_ge(consts_in, 16 * N_CONSTS)
            pe.wait_ge(set_up, 2)
            pe.wait_ge(b_split, 5)

            def body(c, r, first, last):
                g, slot = RING * c + r, r % 2
                wait(pe, scaled, g + 1)
                wait(pe, summed, g - 1)
                for t in range(GT):
                    out = ps[:, slot, t * DIM:(t + 1) * DIM]
                    toks = slice(t * P, (t + 1) * P)
                    nc.tensor.matmul(out, ident[:, :], x_in[:, r, t, :], start=True, stop=False)
                    for i in range(3):
                        nc.tensor.matmul(out, ones[0:1, :], b_parts[0:1, i, :], start=False, stop=False)
                    for k in range(2):
                        ins = nc.tensor.matmul(out, heads[:, r, k, toks], w_o[:, k, :], start=False, stop=(k == 1))
                ins.then_inc(ps_ready, 1)

            over_groups(pe, body)




def build(nc, d, phases=None):
    dram = lambda n, s, t=FP32: nc.dram_tensor(n, s, t, kind="Internal").ap()
    d = dict(d)
    d["qk_parts"] = dram("qk_parts", [3, 4, P, TOK], BF16)
    d["v_aug"] = dram("v_aug", [TOK, HEADS * VA])
    d["sorted_x"] = dram("sorted_x", [SLOTS * P, DIM])
    d["sorted_y"] = dram("sorted_y", [SLOTS * P, DIM])
    d["max_rows"] = dram("max_rows", [2, 3 * UH * QTILES, P], BF16)
    d["heads_t"] = dram("heads_t", [HEADS, VA, TOK])
    d["inv_sum"] = dram("inv_sum", [HEADS, TOK])
    with ExitStack() as ctx:
        sb = lambda n, s, t=FP32: ctx.enter_context(nc.sbuf_tensor(n, s, t))
        keep = {
            "xn": sb("keep_xn", [P, TILES, DIM]),
            "weight": sb("keep_weight", [P, TILES]),
            "place": sb("keep_place", [P, TILES], U32),
            "tile_col": sb("keep_tile_col", [P, SLOTS], I32),
        }
        with ExitStack() as early:
            sb2 = lambda n, s: early.enter_context(nc.sbuf_tensor(n, s, FP32))
            keep["mv"] = sb2("keep_mv", [P, TILES, 2])
            keep["sim"] = sb2("keep_sim", [P, TILES, COLS])
            keep["z"] = sb2("keep_z", [P, TILES, COLS])
            project(nc, d, keep)
            route(nc, d, keep)
        if phases != 1:
            attend(nc, d, keep)
        if phases is None:
            columns(nc, d, keep)
            combine(nc, d, keep)


def host_layout(x):
    f = np.float32
    order = np.array([(m * 8 + h) * HD + i for m in range(2) for i in range(HD) for h in range(8)])
    inv_freq = (f(1.0) / f(10000.0) ** (np.arange(0, HD, 2, dtype=f) / f(HD))).astype(f)
    freqs = np.outer(np.arange(SEQ, dtype=f), inv_freq).astype(f)
    rows = np.arange(P) // 8 % (HD // 2)
    cos = np.cos(freqs)[:, rows].T.astype(f)
    sin = np.sin(freqs)[:, rows].T.astype(f) * np.where(np.arange(P) < P // 2, f(-1), f(1))[:, None]
    scale = np.array([1.0 / np.sqrt(HD), 1.0], f)[None, :, None]
    c = np.ascontiguousarray
    return {
        "x": c(x["L0_attn_x"].reshape(TOK, DIM)),
        "wq_t": c(x["L0_attn_Wq"][order].T), "wk_t": c(x["L0_attn_Wk"][order].T),
        "wv_t": c(x["L0_attn_Wv"].T), "wo_t": c(x["L0_attn_Wo"].T),
        "col_emb": c(x["L0_ffn_col_emb"]), "cemb_t": c(x["L0_ffn_col_emb"].T),
        "gate_w1": c(x["L0_ffn_gate_w1"]), "gate_b1": c(x["L0_ffn_gate_b1"]),
        "gate_w2": c(x["L0_ffn_gate_w2"]), "gate_b2": c(x["L0_ffn_gate_b2"]),
        "w_up": c(x["L0_ffn_W_cols"].reshape(COLS, 2, P, NEUR).transpose(0, 2, 1, 3)),
        "w_down": c(np.concatenate([x["L0_ffn_proj_w"].reshape(COLS, NEUR, DIM),
                                    x["L0_ffn_b_cols"].reshape(COLS, NEUR, 1)], axis=2)),
        "proj_b": c(x["L0_ffn_proj_b"]),
        "ln_g": c(x["L0_ffn_ln_g"]), "ln_b": c(x["L0_ffn_ln_b"]),
        "ident": np.eye(P, dtype=f),
        "rope_cos": c((cos[:, None, :] * scale).astype(f)),
        "rope_sin": c((sin[:, None, :] * scale).astype(f)),
        "col_rank": np.arange(COLS, 0, -1).astype(f),
        "tile_start": (np.arange(SLOTS) * P).astype(f),
    }


def kernel(**inputs):
    import concourse.bacc as bacc
    from concourse.bass_utils import run_bass_kernel_spmd

    arrays = host_layout({k: np.asarray(v) for k, v in inputs.items()})
    nc = bacc.Bacc("TRN2", target_bir_lowering=False, num_devices=1)
    d = {n: nc.dram_tensor(f"in_{n}", a.shape, mybir.dt.from_np(a.dtype), kind="ExternalInput").ap()
         for n, a in arrays.items()}
    d["out"] = nc.dram_tensor("out", (TOK, DIM), FP32, kind="ExternalOutput").ap()
    build(nc, d)
    r = run_bass_kernel_spmd(nc, [{f"in_{n}": a for n, a in arrays.items()}], core_ids=[0])
    return r.results[0]["out"].reshape(BATCH, SEQ, DIM)
```

```python
from contextlib import ExitStack

import numpy as np
import concourse.bass as bass
from concourse import mybir

FP32 = mybir.dt.float32
BF16 = mybir.dt.bfloat16
I32 = mybir.dt.int32
U32 = mybir.dt.uint32
ALU = mybir.AluOpType
ACT = mybir.ActivationFunctionType
AX = mybir.AxisListType

P = 128
BATCH, SEQ, DIM = 8, 1024, 256
HEADS = 16
HD = DIM // HEADS
TOK = BATCH * SEQ
TILES = TOK // P
COLS, NEUR, HID = 16, 64, 128
LN_EPS = 1e-5
SIGMOID_MIN = -87.0
MASKED = -3.0e38
NORM2_MIN = 1e-24

GROUP = 512
GT = GROUP // P
VA = HD + 1
QTILES = SEQ // P
UH = 4
UNITS = HEADS // UH
TERMS = ((0, 0), (0, 1), (1, 0), (0, 2), (2, 0), (1, 1))
KROWS = len(TERMS) * HD
SHIFT = KROWS
KALL = KROWS + 3
SLOTS = -(-((TOK + COLS * (P - 1)) // P) // 4) * 4


def over(eng, count, body):
    body(0, True, False)
    with eng.Fori(1, count - 1) as i:
        body(i, False, False)
    body(count - 1, False, True)


def over_batches(eng, body):
    over(eng, BATCH, body)


def wait(eng, sem, value):
    if isinstance(value, int) and value <= 0:
        return
    eng.wait_ge(sem, value)


def settle(eng, passed):
    eng.sem_inc(passed, 1)


def wait_apart(eng, sem, value, passed):
    wait(eng, sem, value)
    if not isinstance(value, int):
        settle(eng, passed)


OPS_DMAS = 2 * len(TERMS) + 1


def load_ops(sp, d, keep, b, r, loaded):
    m, h0 = r // 2, (r % 2) * UH
    for which, ops in ((0, keep["q_ops"]), (1, keep["k_ops"])):
        for t, term in enumerate(TERMS):
            src = d["qk_parts"][term[which], 2 * which + m, :, bass.ts(b, SEQ)]
            src = src.rearrange("(i h) t -> i h t", h=8)[:, h0:h0 + UH, :]
            sp.dma_start(ops[t * HD:(t + 1) * HD, r, :, :], src).then_inc(loaded, 16)
    src = d["v_aug"][bass.ts(b, SEQ), r * UH * VA:(r + 1) * UH * VA]
    sp.dma_start(keep["v_ops"][:, r, :, :], src.rearrange("(t p) e -> p t e", p=P)).then_inc(loaded, 16)


def group_after(b, slot):
    return (b, 1) if slot == 0 else (b + 1, 0)


def group_before(b, slot):
    return (b, 0) if slot == 1 else (b - 1, 1)


def project(nc, d, keep):
    with ExitStack() as ctx:
        sb = lambda n, s, t=FP32: ctx.enter_context(nc.sbuf_tensor("p_" + n, s, t))
        pb = lambda n, s: ctx.enter_context(nc.psum_tensor("p_" + n, s, FP32))
        sem = lambda n: ctx.enter_context(nc.semaphore("p_" + n))

        ident = sb("ident", [P, P])
        w_qk = sb("w_qk", [P, 2, 2 * DIM])
        w_vs = sb("w_vs", [P, 2, DIM + COLS])
        w_g1 = sb("w_g1", [P, 2, HID])
        b_g1 = sb("b_g1", [P, 1])
        w_g2 = sb("w_g2", [P, COLS])
        rope_cos = sb("rope_cos", [P, 2, SEQ])
        rope_sin = sb("rope_sin", [P, 2, SEQ])
        zero_rows = sb("zero_rows", [P, DIM])
        x_in = sb("x_in", [P, 2, GT, DIM])
        xn = sb("xn", [P, 2, GT, DIM])
        stats = sb("stats", [P, GT, 6])
        mv = sb("mv", [P, GT, 2])
        rstd = sb("rstd", [P, GT])
        sq = sb("sq", [P, GT])
        neg_half = sb("neg_half", [P, COLS])
        ones = sb("ones", [P, P])
        emb_sq = sb("emb_sq", [P, 2, COLS])
        x_t = sb("x_t", [P, 2, 2, GROUP])
        hid = sb("hid", [P, 2, GROUP])
        raw = sb("raw", [P, 2, 4, GROUP])
        rot = sb("rot", [P, 2, 4, GROUP])
        ra = sb("ra", [P, 2, 4, GROUP])
        parts = sb("parts", [P, 2, 3, 4, GROUP], BF16)
        v_st = sb("v_st", [P, 2, GT, HEADS, VA])

        ps_t = pb("ps_t", [P, 2, GROUP])
        ps_g1 = pb("ps_g1", [P, GROUP])
        ps_qk = pb("ps_qk", [P, 2, GROUP])
        ps_v = pb("ps_v", [P, 2, GROUP])
        ps_g2 = pb("ps_g2", [P, GROUP])

        router_in = sem("router_in")
        qk_in = sem("qk_in")
        rest_in = sem("rest_in")
        x_loaded = [sem(f"x_loaded{i}") for i in range(2)]
        consts_set = sem("consts_set")
        zeros_out = [sem(f"zeros_out{i}") for i in range(2)]
        stats_done = sem("stats_done")
        mv_done = sem("mv_done")
        var_eps = sem("var_eps")
        rstd_done = sem("rstd_done")
        xn_ready = sem("xn_ready")
        xn_kept = [sem(f"xn_kept{i}") for i in range(2)]
        t_ready = sem("t_ready")
        xt_ready = sem("xt_ready")
        g1_ready = sem("g1_ready")
        hid_ready = sem("hid_ready")
        qk_ready = sem("qk_ready")
        raw_ready = sem("raw_ready")
        v_ready = sem("v_ready")
        v_read = sem("v_read")
        v_stored = [sem(f"v_stored{i}") for i in range(2)]
        g2_ready = sem("g2_ready")
        z_read = sem("z_read")
        rot_ready = [sem(f"rot_ready{i}") for i in range(2)]
        norm_step = sem("norm_step")
        normed = sem("normed")
        emb_squared = sem("emb_squared")
        emb_ready = sem("emb_ready")
        emb_summed = sem("emb_summed")
        emb_normed = sem("emb_normed")
        a_ready = sem("a_ready")
        ak_ready = sem("ak_ready")
        b_ready = sem("b_ready")
        r_ready = sem("r_ready")
        high_ready = sem("high_ready")
        rest_ready = sem("rest_ready")
        mid_ready = sem("mid_ready")
        low_ready = sem("low_ready")
        passed = sem("passed")
        parts_out = [sem(f"parts_out{i}") for i in range(2)]

        block = ctx.enter_context(nc.Block())
        ROUTER_DMAS, QK_DMAS, REST_DMAS = 3, 2, 5
        ZERO_TILES = SLOTS // (TOK // GROUP)

        @block.sync
        def _(sp):
            def load_x(b, slot):
                g = 2 * b + slot
                src = d["x"][bass.ts(g, GROUP), :].rearrange("(t p) c -> p t c", p=P)
                sp.dma_start(x_in[:, slot, :, :], src).then_inc(x_loaded[slot], 16)

            load_x(0, 0)
            sp.dma_start(ident[:, :], d["ident"]).then_inc(router_in, 16)
            sp.dma_start(w_g1[:, :, :], d["gate_w1"].rearrange("(k p) n -> p k n", p=P)).then_inc(router_in, 16)
            sp.dma_start(b_g1[:, :], d["gate_b1"].unsqueeze(1)).then_inc(router_in, 16)
            sp.dma_start(w_qk[:, :, 0:DIM], d["wq_t"].rearrange("(k p) n -> p k n", p=P)).then_inc(qk_in, 16)
            sp.dma_start(w_qk[:, :, DIM:2 * DIM], d["wk_t"].rearrange("(k p) n -> p k n", p=P)).then_inc(qk_in, 16)
            load_x(0, 1)
            sp.dma_start(w_vs[:, :, 0:DIM], d["wv_t"].rearrange("(k p) n -> p k n", p=P)).then_inc(rest_in, 16)
            sp.dma_start(w_vs[:, :, DIM:DIM + COLS], d["cemb_t"].rearrange("(k p) n -> p k n", p=P)).then_inc(rest_in, 16)
            sp.dma_start(w_g2[:, :], d["gate_w2"]).then_inc(rest_in, 16)
            sp.dma_start(rope_cos[:, :, :], d["rope_cos"]).then_inc(rest_in, 16)
            sp.dma_start(rope_sin[:, :, :], d["rope_sin"]).then_inc(rest_in, 16)
            sp.wait_ge(consts_set, 4)

            def store_parts(b, slot):
                g = 2 * b + slot
                wait_apart(sp, low_ready, g + 1, passed)
                for i in range(3):
                    dst = d["qk_parts"][i, :, :, bass.ts(g, GROUP)].rearrange("m p t -> p m t")
                    sp.dma_start(dst, parts[:, slot, i, :, :]).then_inc(parts_out[slot], 16)

            def body(b, first, last):
                for slot in range(2):
                    g = 2 * b + slot
                    if not last:
                        wait_apart(sp, xn_ready, g + 1, passed)
                        load_x(b + 1, slot)
                    wait_apart(sp, xn_ready, g + 1, passed)
                    sp.dma_start(keep["xn"][:, bass.ts(g, GT), :], xn[:, slot, :, :]).then_inc(xn_kept[slot], 16)
                    wait_apart(sp, raw_ready, 4 * g + 4, passed)
                    wait_apart(sp, r_ready, g - 1, passed)
                    half = P // 2
                    sp.dma_start(rot[0:half, slot, :, :], raw[half:P, slot, :, :]).then_inc(rot_ready[slot], 16)
                    sp.dma_start(rot[half:P, slot, :, :], raw[0:half, slot, :, :]).then_inc(rot_ready[slot], 16)
                    wait_apart(sp, v_read, 8 * g + 8, passed)
                    sp.dma_start(d["v_aug"][bass.ts(g, GROUP), :].rearrange("(t p) c -> p t c", p=P),
                                 v_st[:, slot, :, :, :].rearrange("p t h e -> p t (h e)")).then_inc(v_stored[slot], 16)
                    if not first:
                        store_parts(b - 1, slot)
                    sp.dma_start(d["sorted_x"][bass.ts(g, ZERO_TILES * P), :].rearrange("(t p) c -> p t c", p=P),
                                 zero_rows[:, :].unsqueeze(1).to_broadcast([P, ZERO_TILES, DIM])).then_inc(zeros_out[slot], 16)

            over_batches(sp, body)
            store_parts(BATCH - 1, 0)
            store_parts(BATCH - 1, 1)
            for slot in range(2):
                sp.wait_ge(xn_kept[slot], 16 * BATCH)
                sp.wait_ge(rot_ready[slot], 32 * BATCH)
                sp.wait_ge(v_stored[slot], 16 * BATCH)
                sp.wait_ge(parts_out[slot], 48 * BATCH)
                sp.wait_ge(zeros_out[slot], 16 * BATCH)

        @block.gpsimd
        def _(pool):
            pool.memset(zero_rows[:, :], 0.0).then_inc(consts_set, 1)
            pool.memset(neg_half[:, :], -0.5).then_inc(consts_set, 1)
            pool.memset(ones[:, :], 1.0).then_inc(consts_set, 1)
            pool.memset(v_st[:, :, :, :, :], 1.0).then_inc(consts_set, 1)

            def inverse_std(g):
                wait(pool, mv_done, GT * g + GT)
                wait(pool, xn_ready, g)
                settle(pool, passed)
                nc.gpsimd.tensor_scalar(rstd[:, :], mv[:, :, 1], LN_EPS, None, ALU.add).then_inc(var_eps, 1)
                wait(pool, var_eps, g + 1)
                nc.gpsimd.tensor_tensor(rstd[:, :], rstd[:, :], neg_half[:, 0:GT], ALU.pow).then_inc(rstd_done, 1)

            def inverse_norm(g):
                STEPS = 3
                wait(pool, rstd_done, g + 1)
                wait(pool, normed, g)
                nc.gpsimd.tensor_tensor(sq[:, :], rstd[:, :], rstd[:, :], ALU.mult).then_inc(norm_step, 1)
                wait(pool, norm_step, STEPS * g + 1)
                nc.gpsimd.tensor_tensor(sq[:, :], sq[:, :], mv[:, :, 1], ALU.mult).then_inc(norm_step, 1)
                wait(pool, norm_step, STEPS * g + 2)
                settle(pool, passed)
                nc.gpsimd.tensor_scalar(sq[:, :], sq[:, :], float(DIM), NORM2_MIN, ALU.mult, ALU.max).then_inc(norm_step, 1)
                wait(pool, norm_step, STEPS * g + 3)
                nc.gpsimd.tensor_tensor(keep["t_norm"][:, bass.ts(g, GT)], sq[:, :], neg_half[:, 0:GT],
                                        ALU.pow).then_inc(normed, 1)

            pool.wait_ge(consts_set, 4)
            inverse_std(0)
            inverse_norm(0)
            inverse_std(1)
            inverse_norm(1)
            pool.wait_ge(rest_in, 16 * REST_DMAS)

            def body(b, first, last):
                for slot in range(2):
                    g = 2 * b + slot
                    if not last:
                        inverse_std(g + 2)
                    wait(pool, raw_ready, 4 * g + 4)
                    wait(pool, low_ready, g - 1)
                    cos = rope_cos[:, 1, slot * GROUP:(slot + 1) * GROUP].unsqueeze(1)
                    nc.gpsimd.tensor_tensor(ra[:, slot, 2:4, :], raw[:, slot, 2:4, :], cos.to_broadcast([P, 2, GROUP]),
                                            ALU.mult).then_inc(ak_ready, 1)
                    wait(pool, rot_ready[slot], 32 * b + 32)
                    sin = rope_sin[:, :, slot * GROUP:(slot + 1) * GROUP].unsqueeze(2)
                    r4 = rot[:, slot, :, :].rearrange("p (w m) t -> p w m t", w=2)
                    nc.gpsimd.tensor_tensor(r4, r4, sin.to_broadcast([P, 2, 2, GROUP]), ALU.mult).then_inc(b_ready, 1)
                    if not last:
                        inverse_norm(g + 2)
                    if first and slot == 0:
                        pool.wait_ge(emb_summed, 1)
                        nc.gpsimd.tensor_tensor(keep["c_norm"][:, :], keep["c_norm"][:, :], neg_half[:, :],
                                                ALU.pow).then_inc(emb_normed, 1)

            over_batches(pool, body)

        @block.vector
        def _(dve):
            def norm_stats(b, slot):
                g = 2 * b + slot
                wait(dve, x_loaded[slot], 16 * b + 16)
                wait(dve, normed, g)
                for t in range(GT):
                    nc.vector.bn_stats(stats[:, t, :], x_in[:, slot, t, :]).then_inc(stats_done, 1)
                for t in range(GT):
                    wait(dve, stats_done, GT * g + t + 1)
                    settle(dve, passed)
                    nc.vector.bn_aggr(mv[:, t, :], stats[:, t, :]).then_inc(mv_done, 1)

            def normalise(b, slot):
                g = 2 * b + slot
                wait(dve, rstd_done, g + 1)
                wait(dve, t_ready, g - 1)
                wait(dve, xn_kept[slot], 16 * b)
                for t in range(GT):
                    ins = nc.vector.tensor_scalar(xn[:, slot, t, :], x_in[:, slot, t, :], mv[:, t, 0:1],
                                                  rstd[:, t:t + 1], ALU.subtract, ALU.mult)
                ins.then_inc(xn_ready, 1)

            def rotary(b, slot):
                g = 2 * b + slot
                wait(dve, b_ready, g + 1)
                wait(dve, a_ready, g + 1)
                wait(dve, ak_ready, g + 1)
                nc.vector.tensor_tensor(ra[:, slot, :, :], ra[:, slot, :, :], rot[:, slot, :, :],
                                        ALU.add).then_inc(r_ready, 1)

            def rest(b, slot):
                g = 2 * b + slot
                wait(dve, high_ready, g + 1)
                nc.vector.tensor_tensor(ra[:, slot, :, :], ra[:, slot, :, :], parts[:, slot, 0, :, :],
                                        ALU.subtract).then_inc(rest_ready, 1)

            def low(b, slot):
                g = 2 * b + slot
                wait(dve, mid_ready, g + 1)
                nc.vector.tensor_tensor(parts[:, slot, 2, :, :], ra[:, slot, :, :], parts[:, slot, 1, :, :],
                                        ALU.subtract).then_inc(low_ready, 1)

            norm_stats(0, 0)
            normalise(0, 0)
            norm_stats(0, 1)
            dve.wait_ge(rest_in, 16 * REST_DMAS)
            emb = w_vs[:, :, DIM:DIM + COLS]
            nc.vector.tensor_tensor(emb_sq[:, :, :], emb, emb, ALU.mult).then_inc(emb_squared, 1)

            def body(b, first, last):
                for slot in range(2):
                    g = 2 * b + slot
                    before = not (first and slot == 0)
                    after = not (last and slot == 1)
                    if after:
                        normalise(*group_after(b, slot))
                    if not first:
                        low(b - 1, slot)
                    if before:
                        rotary(*group_before(b, slot))
                    if not last:
                        norm_stats(b + 1, slot)
                    if first and slot == 0:
                        dve.wait_ge(emb_ready, 1)
                        nc.vector.tensor_scalar_max(keep["c_norm"][:, :], ps_g2[:, 0:COLS],
                                                    NORM2_MIN).then_inc(emb_summed, 1)
                    wait(dve, raw_ready, 4 * g + 4)
                    wait(dve, low_ready, g - 1)
                    cos = rope_cos[:, 0, slot * GROUP:(slot + 1) * GROUP].unsqueeze(1)
                    nc.vector.tensor_tensor(ra[:, slot, 0:2, :], raw[:, slot, 0:2, :], cos.to_broadcast([P, 2, GROUP]),
                                            ALU.mult).then_inc(a_ready, 1)
                    wait(dve, g2_ready, g + 1)
                    nc.vector.tensor_copy(keep["z"][:, bass.ts(g, GT), :],
                                          ps_g2[:, 0:GT * COLS].rearrange("p (t c) -> p t c", c=COLS)).then_inc(z_read, 1)
                    if before:
                        rest(*group_before(b, slot))

            over_batches(dve, body)
            rotary(BATCH - 1, 1)
            low(BATCH - 1, 0)
            rest(BATCH - 1, 1)
            low(BATCH - 1, 1)

        @block.scalar
        def _(act):
            def evacuate_x(b, slot):
                g = 2 * b + slot
                wait(act, t_ready, g + 1)
                wait(act, v_ready, GT * (g - 1))
                wait(act, g1_ready, g - 1)
                nc.scalar.activation(x_t[:, slot, :, :], ps_t[:, :, :], ACT.Copy).then_inc(xt_ready, 1)

            def high(b, slot):
                g = 2 * b + slot
                wait(act, r_ready, g + 1)
                wait(act, parts_out[slot], 48 * b)
                nc.scalar.activation(parts[:, slot, 0, :, :], ra[:, slot, :, :], ACT.Copy).then_inc(high_ready, 1)

            def mid(b, slot):
                g = 2 * b + slot
                wait(act, rest_ready, g + 1)
                nc.scalar.activation(parts[:, slot, 1, :, :], ra[:, slot, :, :], ACT.Copy).then_inc(mid_ready, 1)

            evacuate_x(0, 0)
            act.wait_ge(router_in, 16 * ROUTER_DMAS)
            act.wait_ge(consts_set, 4)

            def body(b, first, last):
                for slot in range(2):
                    g = 2 * b + slot
                    before = not (first and slot == 0)
                    wait(act, g1_ready, g + 1)
                    wait(act, g2_ready, g - 1)
                    nc.scalar.activation(hid[:, slot, :], ps_g1[:, :], ACT.Gelu, bias=b_g1[:, 0:1]).then_inc(hid_ready, 1)
                    wait(act, a_ready, g - 1)
                    wait(act, ak_ready, g - 1)
                    wait(act, rot_ready[slot], 32 * b)
                    for m in range(2):
                        wait(act, qk_ready, 4 * g + m + 1)
                        nc.scalar.activation(raw[:, slot, m, :], ps_qk[:, m % 2, :], ACT.Copy).then_inc(raw_ready, 1)
                    if not first:
                        mid(b - 1, slot)
                    for m in range(2, 4):
                        wait(act, qk_ready, 4 * g + m + 1)
                        nc.scalar.activation(raw[:, slot, m, :], ps_qk[:, m % 2, :], ACT.Copy).then_inc(raw_ready, 1)
                    if not (last and slot == 1):
                        evacuate_x(*group_after(b, slot))
                    wait(act, v_stored[slot], 16 * b)
                    for t in range(GT):
                        wait(act, v_ready, GT * g + t + 1)
                        ps = ps_v[:, t % 2, :]
                        nc.scalar.activation(v_st[:, slot, t, :, 0:HD],
                                             ps[:, 0:DIM].rearrange("p (h e) -> p h e", e=HD), ACT.Copy).then_inc(v_read, 1)
                        nc.scalar.activation(keep["sim"][:, GT * g + t, :], ps[:, DIM:DIM + COLS],
                                             ACT.Copy).then_inc(v_read, 1)
                    if before:
                        high(*group_before(b, slot))

            over_batches(act, body)
            mid(BATCH - 1, 0)
            high(BATCH - 1, 1)
            mid(BATCH - 1, 1)

        @block.tensor
        def _(pe):
            def transposes(b, slot):
                g = 2 * b + slot
                wait(pe, xn_ready, g + 1)
                wait(pe, xt_ready, g)
                for t in range(GT):
                    for k in range(2):
                        ins = nc.tensor.transpose(ps_t[:, k, t * P:(t + 1) * P],
                                                  xn[:, slot, t, k * P:(k + 1) * P], ident[:, :])
                ins.then_inc(t_ready, 1)

            pe.wait_ge(router_in, 16 * ROUTER_DMAS)
            transposes(0, 0)

            def body(b, first, last):
                for slot in range(2):
                    g = 2 * b + slot
                    wait(pe, xt_ready, g + 1)
                    wait(pe, hid_ready, g)
                    for k in range(2):
                        ins = nc.tensor.matmul(ps_g1[:, :], w_g1[:, k, :], x_t[:, slot, k, :],
                                               start=(k == 0), stop=(k == 1))
                    ins.then_inc(g1_ready, 1)
                    if first and slot == 0:
                        pe.wait_ge(qk_in, 16 * QK_DMAS)
                    for m in range(4):
                        wait(pe, raw_ready, 4 * g + m - 1)
                        for k in range(2):
                            ins = nc.tensor.matmul(ps_qk[:, m % 2, :], w_qk[:, k, m * P:(m + 1) * P],
                                                   x_t[:, slot, k, :], start=(k == 0), stop=(k == 1))
                        ins.then_inc(qk_ready, 1)
                    if not (last and slot == 1):
                        transposes(*group_after(b, slot))
                    if first and slot == 0:
                        pe.wait_ge(rest_in, 16 * REST_DMAS)
                        pe.wait_ge(emb_squared, 1)
                        for k in range(2):
                            ins = nc.tensor.matmul(ps_g2[:, 0:COLS], ones[:, :], emb_sq[:, k, :],
                                                   start=(k == 0), stop=(k == 1))
                        ins.then_inc(emb_ready, 1)
                    for t in range(GT):
                        wait(pe, v_read, 2 * (GT * g + t - 1))
                        for k in range(2):
                            ins = nc.tensor.matmul(ps_v[:, t % 2, 0:DIM + COLS], x_t[:, slot, k, t * P:(t + 1) * P],
                                                   w_vs[:, k, :], start=(k == 0), stop=(k == 1))
                        ins.then_inc(v_ready, 1)
                    wait(pe, hid_ready, g + 1)
                    wait(pe, z_read, g)
                    if first and slot == 0:
                        pe.wait_ge(emb_summed, 1)
                    for t in range(GT):
                        ins = nc.tensor.matmul(ps_g2[:, t * COLS:(t + 1) * COLS], hid[:, slot, t * P:(t + 1) * P],
                                               w_g2[:, :], start=True, stop=True)
                    ins.then_inc(g2_ready, 1)

            over_batches(pe, body)


def route(nc, d, keep):
    with ExitStack() as ctx:
        sb = lambda n, s, t=FP32: ctx.enter_context(nc.sbuf_tensor("r_" + n, s, t))
        pb = lambda n, s: ctx.enter_context(nc.psum_tensor("r_" + n, s, FP32))
        sem = lambda n: ctx.enter_context(nc.semaphore("r_" + n))

        TC = [P, TILES, COLS]
        CT = [P, COLS, TILES]
        b_g2 = sb("b_g2", [P, COLS])
        col_rank = sb("col_rank", [P, COLS])
        before = sb("before", [P, P], BF16)
        ones = sb("ones", [P, P], BF16)
        lg = sb("lg", TC)
        ez = sb("ez", TC)
        top = sb("top", [P, TILES])
        pick = sb("pick", TC)
        pick_bf = sb("pick_bf", TC, BF16)
        esum = sb("esum", [P, TILES])
        total = sb("total", CT)
        seen = sb("seen", CT)
        small = sb("small", [P, 4, COLS])
        small_i = sb("small_i", [P, COLS], I32)
        place = sb("place", TC)
        place_f = sb("place_f", [P, TILES])
        ps_before = pb("ps_before", [P, TILES * COLS])
        ps_total = pb("ps_total", [P, TILES * COLS])

        loaded = sem("loaded")
        ops_in = sem("ops_in")
        set_up = sem("set_up")
        bias_in = sem("bias_in")
        gate_exp = sem("gate_exp")
        cosine = sem("cosine")
        shifted = sem("shifted")
        soft_exp = sem("soft_exp")
        picked = sem("picked")
        counted = sem("counted")
        step = sem("step")
        placed = sem("placed")
        block = ctx.enter_context(nc.Block())

        @block.sync
        def _(sp):
            sp.dma_start(b_g2[:, :], d["gate_b2"].unsqueeze(0).to_broadcast([P, COLS])).then_inc(loaded, 16)
            sp.dma_start(col_rank[:, :], d["col_rank"].unsqueeze(0).to_broadcast([P, COLS])).then_inc(loaded, 16)
            for r in range(3):
                load_ops(sp, d, keep, 0, r, ops_in)
            sp.wait_ge(ops_in, 16 * 3 * OPS_DMAS)

        @block.gpsimd
        def _(pool):
            nc.gpsimd.tensor_tensor(place[:, :, :], keep["sim"][:, :, :], keep["t_norm"][:, :].unsqueeze(2).to_broadcast(TC),
                                    ALU.mult).then_inc(cosine, 1)
            pool.wait_ge(cosine, 1)
            nc.gpsimd.tensor_tensor(place[:, :, :], place[:, :, :], keep["c_norm"][:, :].unsqueeze(1).to_broadcast(TC),
                                    ALU.mult).then_inc(cosine, 1)
            pool.memset(ones[:, :], 1.0).then_inc(set_up, 1)
            pool.memset(before[:, :], 1.0).then_inc(set_up, 1)
            pool.wait_ge(set_up, 2)
            nc.gpsimd.affine_select(out=before[:, :], in_=before[:, :], compare_op=ALU.is_gt, fill=0.0, base=0,
                                    pattern=[[1, P]], channel_multiplier=-1).then_inc(set_up, 1)
            pool.wait_ge(set_up, 3)
            pool.memset(keep["k_ops"][SHIFT:KALL, :, :, :], 1.0).then_inc(set_up, 1)

        @block.scalar
        def _(act):
            act.wait_ge(bias_in, 1)
            nc.scalar.activation(ez[:, :, :], lg[:, :, :], ACT.Exp, scale=-1.0).then_inc(gate_exp, 1)
            act.wait_ge(shifted, 1)
            nc.scalar.activation(ez[:, :, :], place[:, :, :], ACT.Exp).then_inc(soft_exp, 1)

        @block.tensor
        def _(pe):
            pe.wait_ge(set_up, 3)
            pe.wait_ge(picked, 1)
            flat = pick_bf[:, :, :].rearrange("p t c -> p (t c)")
            for weights, ps in ((before, ps_before), (ones, ps_total)):
                for i in range(2):
                    ins = nc.tensor.matmul(ps[:, i * 512:(i + 1) * 512], weights[:, :], flat[:, i * 512:(i + 1) * 512],
                                           start=True, stop=True)
            ins.then_inc(counted, 1)

        @block.vector
        def _(dve):
            chain = [0]

            def link(ins):
                chain[0] += 1
                ins.then_inc(step, 1)
                dve.wait_ge(step, chain[0])

            v = nc.vector
            per_tok = lambda a: a[:, :].unsqueeze(2).to_broadcast(TC)
            per_col = lambda a: a.unsqueeze(1).to_broadcast(TC)
            dve.wait_ge(loaded, 16 * 2)
            link(v.tensor_tensor(lg[:, :, :], keep["z"][:, :, :], per_col(b_g2[:, :]), ALU.add))
            v.tensor_scalar_max(lg[:, :, :], lg[:, :, :], SIGMOID_MIN).then_inc(bias_in, 1)
            dve.wait_ge(gate_exp, 1)
            link(v.tensor_scalar_add(ez[:, :, :], ez[:, :, :], 1.0))
            link(v.reciprocal(lg[:, :, :], ez[:, :, :]))
            dve.wait_ge(cosine, 2)
            link(v.tensor_tensor(lg[:, :, :], lg[:, :, :], place[:, :, :], ALU.add))
            link(v.reduce_max(top[:, :], lg[:, :, :], AX.X))
            v.tensor_tensor(place[:, :, :], lg[:, :, :], per_tok(top), ALU.subtract).then_inc(shifted, 1)
            link(v.tensor_tensor(pick[:, :, :], lg[:, :, :], per_tok(top), ALU.is_equal))
            link(v.tensor_tensor(pick[:, :, :], pick[:, :, :], per_col(col_rank[:, :]), ALU.mult))
            link(v.reduce_max(top[:, :], pick[:, :, :], AX.X))
            link(v.tensor_tensor(pick[:, :, :], pick[:, :, :], per_tok(top), ALU.is_equal))
            v.tensor_copy(pick_bf[:, :, :], pick[:, :, :]).then_inc(picked, 1)
            dve.wait_ge(soft_exp, 1)
            link(v.reduce_sum(esum[:, :], ez[:, :, :], AX.X))
            link(v.reciprocal(keep["weight"][:, :], esum[:, :]))
            dve.wait_ge(counted, 1)
            link(v.tensor_copy(total[:, :, :], ps_total[:, :].rearrange("p (t c) -> p c t", c=COLS)))
            flat = lambda a: a[:, :, :].rearrange("p c t -> p (c t)")
            link(v.tensor_tensor_scan(flat(seen), flat(total), flat(total), 0.0, ALU.add, ALU.bypass))
            count, padded, base, first = (small[:, i, :] for i in range(4))
            end = keep["col_end"][:, :]
            link(v.tensor_tensor(first, seen[:, :, 0], total[:, :, 0], ALU.subtract))
            link(v.tensor_tensor(count, seen[:, :, TILES - 1], first, ALU.subtract))
            link(v.tensor_tensor(seen[:, :, :], seen[:, :, :], total[:, :, :], ALU.subtract))
            link(v.tensor_scalar_add(small_i[:, :], count, float(P - 1)))
            link(v.tensor_single_scalar(small_i[:, :], small_i[:, :], -P, ALU.bitwise_and))
            link(v.tensor_copy(padded, small_i[:, :]))
            link(v.tensor_tensor_scan(end, padded, padded, 0.0, ALU.add, ALU.bypass))
            link(v.tensor_tensor(base, end, padded, ALU.subtract))
            link(v.tensor_tensor(base, base, first, ALU.subtract))
            link(v.tensor_tensor(place[:, :, :], ps_before[:, :].rearrange("p (t c) -> p t c", c=COLS),
                                 seen[:, :, :].rearrange("p c t -> p t c"), ALU.add))
            link(v.tensor_tensor(place[:, :, :], place[:, :, :], per_col(base), ALU.add))
            link(v.tensor_tensor(place[:, :, :], place[:, :, :], pick[:, :, :], ALU.mult))
            link(v.reduce_sum(place_f[:, :], place[:, :, :], AX.X))
            v.tensor_copy(keep["place"][:, :], place_f[:, :]).then_inc(placed, 1)


def attend(nc, d, keep):
    with ExitStack() as ctx:
        sb = lambda n, s, t=FP32: ctx.enter_context(nc.sbuf_tensor("a_" + n, s, t))
        pb = lambda n, s: ctx.enter_context(nc.psum_tensor("a_" + n, s, FP32))
        sem = lambda n: ctx.enter_context(nc.semaphore("a_" + n))

        RING = UNITS
        BANK = 512
        q_ops, k_ops, v_ops = keep["q_ops"], keep["k_ops"], keep["v_ops"]
        PROBS = 4
        probs = sb("probs", [P, PROBS, UH, BANK])
        future = sb("future", [P, SEQ])
        future_t = sb("future_t", [P, P], BF16)
        ident = sb("ident", [P, P], BF16)
        sums_out = sb("sums_out", [P, 4, SEQ], BF16)
        row_max = sb("row_max", [P, 2, UH * QTILES])
        max_rest = sb("max_rest", [P, 2, UH * QTILES])
        max_parts = sb("max_parts", [P, 2, 3, UH * QTILES], BF16)
        max_rows = sb("max_rows", [P, 2, P], BF16)
        o_out = sb("o_out", [P, 2, SEQ])
        proj_b = sb("proj_b", [P, DIM])

        MAX_BANKS, EXP_BANKS = 4, 3
        ps_max = pb("ps_max", [P, MAX_BANKS * BANK])
        ps_exp = pb("ps_exp", [P, EXP_BANKS, BANK])
        ps_o = pb("ps_o", [P, BANK])

        passed = sem("passed")
        set_up = sem("set_up")
        scattered = sem("scattered")
        bias_in = sem("bias_in")
        biased = sem("biased")
        o_clear = sem("o_clear")
        ops_in = [sem(f"ops_in{i}") for i in range(RING)]
        max_sent = [sem(f"max_sent{i}") for i in range(2)]
        max_in = [sem(f"max_in{i}") for i in range(RING)]
        scored = sem("scored")
        maxed = sem("maxed")
        split_step = sem("split_step")
        split_part = sem("split_part")
        split = sem("split")
        s_ready = sem("s_ready")
        exp_done = sem("exp_done")
        pv_done = sem("pv_done")
        o_read = sem("o_read")
        o_stored = [sem(f"o_stored{i}") for i in range(2)]
        block = ctx.enter_context(nc.Block())

        GROUPS = [(0, kt) for kt in range(QTILES // 2)] + [(1, kt) for kt in range(QTILES)]
        NGROUP = len(GROUPS)
        PIECES = [(gi, j) for gi in range(NGROUP) for j in range(UH)]
        NPIECE = len(PIECES)
        CARRY = 2
        COPY_BEFORE = (UH * 6, UH * 2)

        def span(gi):
            half, kt = GROUPS[gi]
            return max(half * BANK, kt * P), (half + 1) * BANK

        MTILES = [(j, qt) for j in range(UH) for qt in range(QTILES)]
        TURN = "turn"
        TURN_AT = 8
        TILE_BANKS = [(qt,) if qt < 4 else (2 * (qt % 2), 2 * (qt % 2) + 1) for qt in range(QTILES)]
        TURN_BANKS = (0,)
        LEAD = 2 * len(MTILES) + 1
        PER_SLOT = len(MTILES) + 1

        def max_items(with_tiles, with_turn):
            items = list(MTILES) if with_tiles else []
            if with_turn:
                items.insert(min(TURN_AT, len(items)), TURN)
            return items

        def last_user():
            used, found, at = {}, [], 0
            slots = {(u, i): max_items(True, True)[i] for u in range(UNITS) for i in range(PER_SLOT)}
            for items in (dict(enumerate(MTILES + MTILES + [TURN])), slots, slots):
                found.append({})
                for key, item in items.items():
                    banks = TURN_BANKS if item == TURN else TILE_BANKS[item[1]]
                    found[-1][key] = at - max(used.get(k, -1) for k in banks)
                    used.update({k: at for k in banks})
                    at += 1
            return found

        def max_banks(item):
            banks = TURN_BANKS if item == TURN else TILE_BANKS[item[1]]
            return ps_max[:, banks[0] * BANK:(banks[-1] + 1) * BANK]

        def slot_flags(b, u, last):
            return (not (last and u >= 2)), (not (last and u == 3))

        def in_slots(eng, body):
            over_batches(eng, lambda b, first, last: [body(b, u, first, last) for u in range(UNITS)])

        @block.sync
        def _(sp):
            def store_o(b, r):
                n = UNITS * b + r
                wait_apart(sp, o_read, 2 * n + 2, passed)
                for j in range(UH):
                    sp.dma_start(d["heads_t"][r * UH + j, :, bass.ts(b, SEQ)],
                                 o_out[32 * j:32 * j + VA, r % 2, :]).then_inc(o_stored[r % 2], 16)

            def send_rows(r, slot, items, sent):
                wait_apart(sp, maxed, items, passed)
                sp.dma_start(d["max_rows"][slot], max_rows[0:3 * UH * QTILES, slot, :]).then_inc(max_sent[slot], 16)
                wait_apart(sp, max_sent[slot], 16 * sent, passed)
                src = d["max_rows"][slot].rearrange("(a h) q -> a (h q)", a=3)
                sp.dma_start(q_ops[SHIFT:KALL, r, :, :].rearrange("a h q -> a (h q)"), src).then_inc(max_in[r], 16)

            def body(b, u, first, last):
                n = UNITS * b + u
                if not (last and u >= 1):
                    wait_apart(sp, s_ready, NPIECE * n, passed)
                    wait_apart(sp, pv_done, NGROUP * n, passed)
                    r = (u + 3) % RING
                    load_ops(sp, d, keep, b if u == 0 else b + 1, r, ops_in[r])
                if slot_flags(b, u, last)[1]:
                    r = (u + 1) % RING
                    turn = TURN_AT if slot_flags(b, u, last)[0] else 0
                    send_rows(r, (u + 1) % 2, LEAD + PER_SLOT * n + turn + 1, 2 * b + (u + 1) // 2 + 1)
                if not (first and u == 0):
                    store_o(b if u else b - 1, (u - 1) % UNITS)

            sp.dma_start(proj_b[:, :], d["proj_b"].unsqueeze(0).to_broadcast([P, DIM])).then_inc(bias_in, 16)
            send_rows(0, 0, LEAD, 1)
            in_slots(sp, body)
            store_o(BATCH - 1, UNITS - 1)
            for i in range(2):
                sp.wait_ge(o_stored[i], 16 * UH * UNITS * BATCH // 2)

        @block.gpsimd
        def _(pool):
            pool.memset(future_t[:, :], 0.0).then_inc(set_up, 1)
            pool.memset(future[:, :], 0.0).then_inc(set_up, 1)
            pool.memset(ident[:, :], 0.0).then_inc(set_up, 1)
            pool.wait_ge(set_up, 3)
            nc.gpsimd.affine_select(out=future[:, SEQ - P:SEQ], in_=future[:, SEQ - P:SEQ], compare_op=ALU.is_ge,
                                    fill=MASKED, base=0, pattern=[[-1, P]], channel_multiplier=1).then_inc(set_up, 1)
            nc.gpsimd.affine_select(out=future_t[:, :], in_=future_t[:, :], compare_op=ALU.is_ge, fill=MASKED, base=0,
                                    pattern=[[1, P]], channel_multiplier=-1).then_inc(set_up, 1)
            nc.gpsimd.affine_select(out=ident[:, :], in_=ident[:, :], compare_op=ALU.not_equal, fill=1.0, base=0,
                                    pattern=[[1, P]], channel_multiplier=-1).then_inc(set_up, 1)

            def split_max(n, slot, items):
                STEPS = 3
                rest, mp = max_rest[:, slot, :], max_parts[:, slot, :, :]
                wait(pool, maxed, items)
                settle(pool, passed)
                nc.gpsimd.tensor_scalar(rest, row_max[:, slot, :], -1.0, None, ALU.mult).then_inc(split_step, 1)
                wait(pool, split_step, STEPS * n + 1)
                for i in range(2):
                    settle(pool, passed)
                    nc.gpsimd.tensor_copy(mp[:, i, :], rest).then_inc(split_part, 1)
                    wait(pool, split_part, 2 * n + i + 1)
                    nc.gpsimd.tensor_tensor(rest, rest, mp[:, i, :], ALU.subtract).then_inc(split_step, 1)
                    wait(pool, split_step, STEPS * n + i + 2)
                settle(pool, passed)
                nc.gpsimd.tensor_copy(mp[:, 2, :], rest).then_inc(split, 1)

            def scatter(t0, t1):
                for t in range(t0, t1):
                    pool.indirect_dma_start(d["sorted_x"], bass.IndirectOffsetOnAxis(ap=keep["place"][:, t:t + 1], axis=0),
                                            keep["xn"][:, t, :], None).then_inc(scattered, 16)

            scatter(0, 10)
            split_max(0, 0, len(MTILES))
            scatter(10, 30)
            split_max(1, 1, 2 * len(MTILES))
            scatter(30, TILES)
            pool.wait_ge(scattered, 16 * TILES)
            pool.wait_ge(bias_in, 16)

            def body(b, u, first, last):
                n = UNITS * b + u
                if slot_flags(b, u, last)[0]:
                    split_max(n + 2, u % 2, LEAD + PER_SLOT * n + PER_SLOT)
                share = TILES // (UNITS * BATCH)
                rows = keep["xn"][:, bass.ts(n, share), :]
                nc.gpsimd.tensor_tensor(rows, rows, proj_b[:, :].unsqueeze(1).to_broadcast([P, share, DIM]),
                                        ALU.add).then_inc(biased, 1)

            in_slots(pool, body)

        @block.vector
        def _(dve):
            nc.vector.memset(ps_o[:, :], 0.0).then_inc(o_clear, 1)
            dve.wait_ge(set_up, 6)

            def max_item(at, ring, item, slot, sent=None):
                wait(dve, scored, at + 1)
                ps = max_banks(item)
                if item == TURN:
                    if sent:
                        wait(dve, *sent)
                    nc.vector.tensor_copy(max_rows[0:3 * UH * QTILES, slot, :],
                                          ps.bitcast(BF16)[0:3 * UH * QTILES, 0:P]).then_inc(maxed, 1)
                    return
                j, qt = item
                width = (qt + 1) * P
                wait(dve, maxed, at - 3)
                settle(dve, passed)
                nc.vector.tensor_tensor_reduce(
                    out=sums_out[:, ring, 0:width], in0=ps[:, 0:width], in1=future[:, SEQ - width:SEQ],
                    scale=1.0, scalar=MASKED, op0=ALU.add, op1=ALU.max,
                    accum_out=row_max[:, slot, j * QTILES + qt:j * QTILES + qt + 1]).then_inc(maxed, 1)

            for at in range(LEAD):
                item = TURN if at == LEAD - 1 else MTILES[at % len(MTILES)]
                max_item(at, at % 4, item, 0 if item == TURN else at // len(MTILES))

            def body(b, u, first, last):
                n = UNITS * b + u
                with_tiles, with_turn = slot_flags(b, u, last)
                if with_tiles:
                    wait(dve, split, n + 1)
                for i, item in enumerate(max_items(with_tiles, with_turn)):
                    sent = (max_sent[(u + 1) % 2], 16 * (2 * b + (u + 1) // 2))
                    turn = item == TURN
                    max_item(LEAD + PER_SLOT * n + i, (LEAD + PER_SLOT * u + i) % 4, item,
                             (u + 1) % 2 if turn else u % 2, sent if turn and not (first and u == 0) else None)

            in_slots(dve, body)

        @block.scalar
        def _(act):
            def copy_o(n, u, b, half):
                wait(act, pv_done, NGROUP * n + (UH if half == 0 else NGROUP))
                if half == 0:
                    wait(act, o_stored[u % 2], 16 * UH * (2 * b + u // 2))
                nc.scalar.activation(o_out[:, u % 2, half * BANK:(half + 1) * BANK], ps_o[:, :],
                                     ACT.Copy).then_inc(o_read, 1)

            def body(b, u, first, last):
                n = UNITS * b + u
                for i, (gi, j) in enumerate(PIECES):
                    if i == COPY_BEFORE[1] and not (first and u == 0):
                        copy_o(n - 1, (u - 1) % UNITS, b if u else b - 1, 1)
                    if i == COPY_BEFORE[0]:
                        copy_o(n, u, b, 0)
                    if j == 0:
                        wait(act, pv_done, NGROUP * n + gi - PROBS + 1)
                    wait(act, s_ready, NPIECE * n + i + 1)
                    width = span(gi)[1] - span(gi)[0]
                    nc.scalar.activation(probs[:, gi % PROBS, j, 0:width], ps_exp[:, i % EXP_BANKS, 0:width],
                                         ACT.Exp).then_inc(exp_done, 1)

            in_slots(act, body)
            copy_o(UNITS * BATCH - 1, UNITS - 1, BATCH - 1, 1)

        @block.tensor
        def _(pe):
            back_ahead, back_first, back_later = last_user()

            def max_item(at, back, item, r, slot):
                wait(pe, maxed, at - back + 1)
                ps = max_banks(item)
                if item == TURN:
                    rows = 3 * UH * QTILES
                    nc.tensor.transpose(ps.bitcast(BF16)[0:rows, 0:P],
                                        max_parts[:, slot, :, :].rearrange("p a c -> p (a c)"),
                                        ident[:, :]).then_inc(scored, 1)
                    return
                j, qt = item
                width = (qt + 1) * P
                for k in range(0, width, BANK):
                    end = min(k + BANK, width)
                    ins = nc.tensor.matmul(ps[:, k:end], q_ops[0:KROWS, r, j, qt * P:width],
                                           k_ops[0:KROWS, r, j, k:end], start=True, stop=True)
                ins.then_inc(scored, 1)

            def score_piece(n, u, i):
                gi, j = PIECES[i]
                kt = GROUPS[gi][1]
                q0, q1 = span(gi)
                wait(pe, exp_done, NPIECE * n + i - EXP_BANKS + 1)
                ps = ps_exp[:, i % EXP_BANKS, :]
                diagonal = q0 == kt * P
                ins = nc.tensor.matmul(ps[:, 0:q1 - q0], k_ops[0:KALL, u, j, kt * P:(kt + 1) * P],
                                       q_ops[0:KALL, u, j, q0:q1], start=True, stop=not diagonal)
                if diagonal:
                    ins = nc.tensor.matmul(ps[:, 0:P], ident[:, :], future_t[:, :], start=False, stop=True)
                ins.then_inc(s_ready, 1)

            def value_group(n, u, gi):
                half, kt = GROUPS[gi]
                q0, q1 = span(gi)
                wait(pe, exp_done, NPIECE * n + UH * (gi + 1))
                if kt == 0:
                    wait(pe, o_read, 2 * n + half)
                for j in range(UH):
                    ins = nc.tensor.matmul(ps_o[32 * j:32 * j + VA, q0 - half * BANK:q1 - half * BANK],
                                           v_ops[:, u, kt, j * VA:(j + 1) * VA], probs[:, gi % PROBS, j, 0:q1 - q0],
                                           start=(kt == 0), stop=(q0 == q1 - P))
                ins.then_inc(pv_done, 1)

            plans = {}

            def plan(items, carry):
                key = (len(items), carry)
                if key not in plans:
                    tries = [greedy(items, carry, near, weight, value)
                             for near in (0.0, 0.03, 0.08, 0.15) for weight in (0.5, 1.0, 2.0) for value in (0.0, 0.5, 1.0, 2.0)]
                    plans[key] = min(tries, key=lambda t: t[1])[0]
                return plans[key]

            def greedy(items, carry, near, weight, value):
                HOP = 0.2
                values = [(-1, gi) for gi in range(NGROUP - CARRY, NGROUP)] if carry else []
                values += [(0, gi) for gi in range(NGROUP - CARRY)]
                order, now, act, dve = [], 0.0, 0.0, 0.0
                exp_end, max_end, val_end = {}, {}, {}
                opened = {0: 0.0, 1: 0.0}
                i = im = iv = 0
                banks_used = {}
                banks_of = [TURN_BANKS if item == TURN else TILE_BANKS[item[1]] for item in items]

                def score_at():
                    if i == NPIECE:
                        return None
                    if i >= COPY_BEFORE[1] and any(v[0] < 0 for v in values[iv:]):
                        return None
                    if i >= COPY_BEFORE[0] and (0, UH - 1) in values[iv:]:
                        return None
                    gi = i // UH
                    own = [v for v in values[iv:] if v[0] == 0 and v[1] <= gi - PROBS]
                    old = [v for v in values[iv:] if v[0] < 0 and v[1] - NGROUP <= gi - PROBS]
                    return None if own or old else max(now, exp_end.get(i - EXP_BANKS, 0.0) + HOP)

                def max_at():
                    if im == len(items):
                        return None
                    return max([now] + [max_end[banks_used[k]] + HOP for k in banks_of[im] if k in banks_used])

                def value_at():
                    if iv == len(values):
                        return None
                    old, gi = values[iv]
                    if old:
                        return now
                    last = UH * gi + UH - 1
                    if last not in exp_end:
                        return None
                    if GROUPS[gi] == (0, 0) and carry and i < COPY_BEFORE[1] + 1:
                        return None
                    if GROUPS[gi] == (1, 0) and i < COPY_BEFORE[0] + 1:
                        return None
                    return max(now, exp_end[last] + HOP, opened[GROUPS[gi][0]] if GROUPS[gi][1] == 0 else 0.0)

                while i < NPIECE or im < len(items) or iv < len(values):
                    starts = [(at, rank, kind) for kind, at, rank in (
                        ("score", score_at(), act - now), ("max", max_at(), (dve - now) * weight),
                        ("value", value_at(), value)) if at is not None]
                    soon = min(starts)[0] + near
                    _, at, kind = min((rank, at, kind) for at, rank, kind in starts if at <= soon)
                    if kind == "score":
                        order.append(("score", i))
                        q0, q1 = span(i // UH)
                        now = at + (q1 - q0) / 2400 + (0.056 if q0 == GROUPS[i // UH][1] * P else 0.0)
                        if i == COPY_BEFORE[0] or (i == COPY_BEFORE[1] and carry):
                            act = max(act, val_end.get(UH - 1, 0.0) + HOP) + 0.48
                            opened[1 if i == COPY_BEFORE[0] else 0] = act + HOP
                        act = max(act, now + HOP) + (q1 - q0) / 1200 + 0.055
                        exp_end[i] = act
                        i += 1
                    elif kind == "max":
                        order.append(("max", im))
                        width = P if items[im] == TURN else (items[im][1] + 1) * P
                        now = at + width / 2400
                        dve = max(dve, now + HOP) + width / 960 + 0.09
                        max_end[im] = dve
                        banks_used.update({k: im for k in banks_of[im]})
                        im += 1
                    else:
                        order.append(("value", values[iv]))
                        q0, q1 = span(values[iv][1])
                        now = at + (q1 - q0) / 600 + 0.06
                        if values[iv][0] == 0:
                            val_end[values[iv][1]] = now
                        iv += 1
                return order, max(now, act, dve)

            pe.wait_ge(set_up, 6)
            pe.wait_ge(o_clear, 1)
            for at in range(LEAD):
                item = TURN if at == LEAD - 1 else MTILES[at % len(MTILES)]
                unit = at // len(MTILES)
                if item == TURN:
                    pe.wait_ge(split, 1)
                max_item(at, back_ahead[at], item, unit, 0)

            def body(b, u, first, last):
                n = UNITS * b + u
                with_tiles, with_turn = slot_flags(b, u, last)
                items = max_items(with_tiles, with_turn)
                for kind, what in plan(items, not (first and u == 0)):
                    if kind == "score":
                        if what == 0:
                            wait(pe, max_in[u], 16 * (b + 1))
                        score_piece(n, u, what)
                    elif kind == "value":
                        old, gi = what
                        value_group(n + old, (u + old) % UNITS, gi)
                    else:
                        if items[what] == TURN:
                            wait(pe, split, n + 2)
                        elif what == 0:
                            wait(pe, ops_in[(u + 2) % RING], 16 * OPS_DMAS * ((b + 1 if u == 1 else b) + (u + 2) // UNITS))
                        back = (back_first if first else back_later)[u, what] if with_tiles else 1
                        max_item(LEAD + PER_SLOT * n + what, back, items[what], (u + 2) % RING, (u + 1) % 2)

            in_slots(pe, body)
            for gi in range(NGROUP - CARRY, NGROUP):
                value_group(UNITS * BATCH - 1, UNITS - 1, gi)


RING = 4


def load_group(sp, d, keep, g, r, loaded):
    toks = bass.ts(g, GROUP)
    for k in range(2):
        hs = slice(8 * k, 8 * k + 8)
        sp.dma_start(keep["heads"][:, r, k, :], d["heads_t"][hs, 0:HD, toks]).then_inc(loaded, 16)
        sp.dma_start(keep["inv"][:, r, k, :],
                     d["inv_sum"][hs, toks].unsqueeze(1).to_broadcast([8, HD, GROUP])).then_inc(loaded, 16)
    sp.dma_start(keep["x_in"][:, r, :, :], d["x"][toks, :].rearrange("(t p) c -> p t c", p=P)).then_inc(loaded, 16)


def columns(nc, d, keep):
    with ExitStack() as ctx:
        sb = lambda n, s, t=FP32: ctx.enter_context(nc.sbuf_tensor("c_" + n, s, t))
        pb = lambda n, s: ctx.enter_context(nc.psum_tensor("c_" + n, s, FP32))
        sem = lambda n: ctx.enter_context(nc.semaphore("c_" + n))

        QUAD = 4
        QUADS = SLOTS // QUAD
        sums = sb("sums", [P, HEADS * TOK // P])
        w_up = sb("w_up", [P, COLS, 2, NEUR])
        w_down = sb("w_down", [NEUR, COLS, DIM + 1])
        xs = sb("xs", [P, 2, QUAD, DIM])
        xs_t = sb("xs_t", [P, 2, 2, P])
        w_tile = sb("w_tile", [P, QUAD, 2, NEUR])
        w_out = sb("w_out", [NEUR, QUAD, DIM + 1])
        act_t = sb("act_t", [NEUR, 2, P])
        y = sb("y", [P, 2, QUAD, DIM])
        ps_t = pb("ps_t", [P, 2, 512])
        ps_up = pb("ps_up", [P, 2, 512])
        ps_y = pb("ps_y", [P, 2, 512])

        ident = keep["ident"]
        tile_start = sb("tile_start", [P, SLOTS])
        tile_cmp = sb("tile_cmp", [P, SLOTS, COLS])
        tile_col = sb("tile_col", [P, SLOTS])
        starts_in = sem("starts_in")
        col_step = sem("col_step")
        consts_in = sem("consts_in")
        weights_in = sem("weights_in")
        combine_in = sem("combine_in")
        sums_in = sem("sums_in")
        inverted = sem("inverted")
        sums_out = sem("sums_out")
        passed = sem("passed")
        xs_in = [sem(f"xs_in{i}") for i in range(2)]
        turned = sem("turned")
        xt_ready = sem("xt_ready")
        chosen = sem("chosen")
        up_ready = sem("up_ready")
        act_ready = sem("act_ready")
        y_ready = sem("y_ready")
        y_copied = sem("y_copied")
        y_out = [sem(f"y_out{i}") for i in range(2)]
        block = ctx.enter_context(nc.Block())

        def over_tiles(eng, body):
            over(eng, QUADS // 2, lambda p, first, last: [body(p, r, first, last) for r in range(2 * QUAD)])

        def column_of(eng, t):
            return eng.value_load(keep["tile_col"][0:1, bass.ds(t, 1)], min_val=0, max_val=COLS - 1)

        @block.sync
        def _(sp):
            def load_quad(p, s):
                src = d["sorted_x"][bass.ts(2 * p + s, QUAD * P), :].rearrange("(t p) c -> p t c", p=P)
                sp.dma_start(xs[:, s, :, :], src).then_inc(xs_in[s], 16)

            sp.dma_start(tile_start[:, :], d["tile_start"].unsqueeze(0).to_broadcast([P, SLOTS])).then_inc(starts_in, 16)
            sp.dma_start(ident[:, :], d["ident"]).then_inc(consts_in, 16)
            sp.dma_start(w_up[:, :, :, :], d["w_up"].rearrange("c p k n -> p c k n")).then_inc(weights_in, 16)
            load_quad(0, 0)
            sp.dma_start(w_down[:, :, :], d["w_down"].rearrange("c p n -> p c n")).then_inc(weights_in, 16)
            load_quad(0, 1)
            sp.dma_start(sums[:, :], d["heads_t"][:, HD, :].rearrange("h (c t) -> h c t", c=P // HEADS)).then_inc(sums_in, 16)
            sp.wait_ge(inverted, 1)
            sp.dma_start(d["inv_sum"].rearrange("h (c t) -> h c t", c=P // HEADS), sums[:, :]).then_inc(sums_out, 16)

            def load_for_combine():
                for name in ("ln_b", "ln_g"):
                    sp.dma_start(keep[name][:, :], d[name].unsqueeze(0).to_broadcast([P, DIM])).then_inc(combine_in, 16)
                sp.dma_start(keep["w_o"][:, :, :], d["wo_t"].rearrange("(k p) n -> p k n", p=P)).then_inc(combine_in, 16)
                sp.wait_ge(sums_out, 16)
                for r in range(2):
                    load_group(sp, d, keep, r, r, combine_in)

            def body(p, first, last):
                if last:
                    load_for_combine()
                for s in range(2):
                    if not last:
                        wait_apart(sp, turned, QUAD * (2 * p + s + 1), passed)
                        load_quad(p + 1, s)
                    wait_apart(sp, y_copied, QUAD * (2 * p + s + 1), passed)
                    sp.dma_start(d["sorted_y"][bass.ts(2 * p + s, QUAD * P), :].rearrange("(t p) c -> p t c", p=P),
                                 y[:, s, :, :]).then_inc(y_out[s], 16)

            over(sp, QUADS // 2, body)
            sp.wait_ge(combine_in, 16 * (3 + 2 * 5))
            sp.wait_ge(y_out[0], 16 * QUADS // 2)
            sp.wait_ge(y_out[1], 16 * QUADS // 2)

        @block.vector
        def _(dve):
            dve.wait_ge(starts_in, 16)
            shape = [P, SLOTS, COLS]
            nc.vector.tensor_tensor(tile_cmp[:, :, :], tile_start[:, :].unsqueeze(2).to_broadcast(shape),
                                    keep["col_end"][:, :].unsqueeze(1).to_broadcast(shape), ALU.is_ge).then_inc(col_step, 1)
            dve.wait_ge(col_step, 1)
            nc.vector.reduce_sum(tile_col[:, :], tile_cmp[:, :, :], AX.X).then_inc(col_step, 1)
            dve.wait_ge(col_step, 2)
            nc.vector.tensor_scalar_min(keep["tile_col"][:, :], tile_col[:, :], float(COLS - 1)).then_inc(col_step, 1)
            dve.wait_ge(col_step, 3)
            dve.wait_ge(weights_in, 16 * 2)

            def body(p, r, first, last):
                t, slot = 2 * QUAD * p + r, r % QUAD
                col = column_of(dve, t)
                wait(dve, y_ready, t - QUAD + 1)
                nc.vector.tensor_copy(w_tile[:, slot, :, :], w_up[:, bass.ds(col, 1), :, :].rearrange(
                    "p a k n -> p (a k) n")).then_inc(chosen, 1)
                nc.vector.tensor_copy(w_out[:, slot, :], w_down[:, bass.ds(col, 1), :].rearrange(
                    "p a n -> p (a n)")).then_inc(chosen, 1)
                if first and r == QUAD:
                    dve.wait_ge(sums_in, 16)
                    nc.vector.reciprocal(sums[:, :], sums[:, :]).then_inc(inverted, 1)

            over_tiles(dve, body)

        @block.scalar
        def _(act):
            def copy_y(p, r):
                t = 2 * QUAD * p + r
                wait(act, y_ready, t + 1)
                wait(act, y_out[r // QUAD], 16 * p)
                nc.scalar.activation(y[:, r // QUAD, r % QUAD, :], ps_y[:, r % 2, 0:DIM], ACT.Copy).then_inc(y_copied, 1)

            def take_rows(p, r):
                t = 2 * QUAD * p + r
                wait(act, turned, t + 1)
                wait(act, up_ready, t - 1)
                nc.scalar.activation(xs_t[:, r % 2, :, :].rearrange("p k t -> p (k t)"), ps_t[:, r % 2, 0:2 * P],
                                     ACT.Copy).then_inc(xt_ready, 1)

            take_rows(0, 0)

            def body(p, r, first, last):
                t = 2 * QUAD * p + r
                if not (last and r == 2 * QUAD - 1):
                    take_rows(p + (r + 1) // (2 * QUAD), (r + 1) % (2 * QUAD))
                wait(act, up_ready, t + 1)
                wait(act, chosen, 2 * t + 2)
                wait(act, y_ready, t - 1)
                nc.scalar.activation(act_t[:, r % 2, :], ps_up[0:NEUR, r % 2, 0:P], ACT.Gelu,
                                     bias=w_out[:, r % QUAD, DIM:DIM + 1]).then_inc(act_ready, 1)
                if not (first and r == 0):
                    copy_y(*((p, r - 1) if r else (p - 1, 2 * QUAD - 1)))

            over_tiles(act, body)
            copy_y(QUADS // 2 - 1, 2 * QUAD - 1)

        @block.tensor
        def _(pe):
            def turn(p, r):
                t = 2 * QUAD * p + r
                wait(pe, xs_in[r // QUAD], 16 * (p + 1))
                wait(pe, xt_ready, t - 1)
                for k in range(2):
                    ins = nc.tensor.transpose(ps_t[:, r % 2, k * P:(k + 1) * P],
                                              xs[:, r // QUAD, r % QUAD, k * P:(k + 1) * P], ident[:, :])
                ins.then_inc(turned, 1)

            def down(t, r):
                wait(pe, act_ready, t + 1)
                wait(pe, y_copied, t - 1)
                nc.tensor.matmul(ps_y[:, r % 2, 0:DIM], act_t[:, r % 2, :],
                                 w_out[:, r % QUAD, 0:DIM],
                                 start=True, stop=True).then_inc(y_ready, 1)

            pe.wait_ge(consts_in, 16)
            turn(0, 0)

            def body(p, r, first, last):
                t = 2 * QUAD * p + r
                if not (last and r == 2 * QUAD - 1):
                    turn(p + (r + 1) // (2 * QUAD), (r + 1) % (2 * QUAD))
                wait(pe, chosen, 2 * t + 2)
                wait(pe, xt_ready, t + 1)
                wait(pe, act_ready, t - 1)
                for k in range(2):
                    ins = nc.tensor.matmul(ps_up[0:NEUR, r % 2, 0:P],
                                           w_tile[:, r % QUAD, k, :], xs_t[:, r % 2, k, :], start=(k == 0), stop=(k == 1))
                ins.then_inc(up_ready, 1)
                if not (first and r == 0):
                    down(t - 1, (r - 1) % QUAD)

            over_tiles(pe, body)
            down(SLOTS - 1, QUAD - 1)


def combine(nc, d, keep):
    with ExitStack() as ctx:
        sb = lambda n, s, t=FP32: ctx.enter_context(nc.sbuf_tensor("o_" + n, s, t))
        pb = lambda n, s: ctx.enter_context(nc.psum_tensor("o_" + n, s, FP32))
        sem = lambda n: ctx.enter_context(nc.semaphore("o_" + n))

        ROUNDS = TOK // GROUP // RING
        AHEAD = 2
        SHARE = 3
        ident, w_o, ln_g, ln_b = (keep[name] for name in ("ident", "w_o", "ln_g", "ln_b"))
        heads, inv, x_in = (keep[name] for name in ("heads", "inv", "x_in"))
        b_rest = sb("b_rest", [P, DIM])
        b_parts = sb("b_parts", [P, 3, DIM], BF16)
        ones = sb("ones", [P, P], BF16)
        neg_half = sb("neg_half", [P, GT])
        rows = sb("rows", [P, RING, GT, DIM])
        cen = sb("cen", [P, 2, GT, DIM])
        res = sb("res", [P, 2, GT, DIM])
        stats = sb("stats", [P, 2, GT, 6])
        mv = sb("mv", [P, 2, GT, 2])
        neg_mean = sb("neg_mean", [P, 2, GT])
        rstd = sb("rstd", [P, 2, GT])
        ps = pb("ps", [P, 2, GT * DIM])
        place = sb("place", [P, 2, GT], U32)

        passed = sem("passed")
        placed = sem("placed")
        set_up = sem("set_up")
        b_split = sem("b_split")
        att_in = [sem(f"att_in{i}") for i in range(RING)]
        rows_in = [sem(f"rows_in{i}") for i in range(RING)]
        scaled = sem("scaled")
        mixed = sem("mixed")
        stats_done = sem("stats_done")
        mv_done = sem("mv_done")
        negated = sem("negated")
        centred = sem("centred")
        var_eps = sem("var_eps")
        rstd_done = sem("rstd_done")
        gained = sem("gained")
        pool_normed = sem("pool_normed")
        pool_gained = sem("pool_gained")
        ps_ready = sem("ps_ready")
        summed = sem("summed")
        stored = [sem(f"stored{i}") for i in range(2)]
        block = ctx.enter_context(nc.Block())

        def over_groups(eng, body):
            over(eng, ROUNDS, lambda c, first, last: [body(c, r, first, last) for r in range(RING)])

        def later(c, r, by):
            return c + (r + by) // RING, (r + by) % RING

        @block.sync
        def _(sp):
            for r in range(2, RING):
                load_group(sp, d, keep, r, r, att_in[r])

            def body(c, r, first, last):
                g = RING * c + r
                if not last:
                    wait_apart(sp, ps_ready, g + 1, passed)
                    load_group(sp, d, keep, g + RING, r, att_in[r])
                wait_apart(sp, summed, g + 1, passed)
                sp.dma_start(d["out"][bass.ts(g, GROUP), :].rearrange("(t p) c -> p t c", p=P),
                             res[:, r % 2, :, :]).then_inc(stored[r % 2], 16)

            over_groups(sp, body)
            sp.wait_ge(stored[0], 16 * RING * ROUNDS // 2)
            sp.wait_ge(stored[1], 16 * RING * ROUNDS // 2)

        @block.gpsimd
        def _(pool):
            pool.memset(neg_half[:, :], -0.5).then_inc(set_up, 1)
            pool.memset(ones[:, :], 1.0).then_inc(set_up, 1)

            def fetch(c, r):
                g = RING * c + r
                wait(pool, centred, g - RING + 1)
                wait(pool, rows_in[(r - 2) % RING], 16 * GT * (c if r >= 2 else c - 1) + 16 * GT)
                settle(pool, passed)
                nc.gpsimd.tensor_copy(place[:, r % 2, :], keep["place"][:, bass.ts(g, GT)]).then_inc(placed, 1)
                wait(pool, placed, g + 1)
                settle(pool, passed)
                for t in range(GT):
                    at = bass.IndirectOffsetOnAxis(ap=place[:, r % 2, t:t + 1], axis=0)
                    nc.gpsimd.indirect_dma_start(rows[:, r, t, :], None, d["sorted_y"], at).then_inc(rows_in[r], 16)

            for r in range(AHEAD):
                fetch(0, r)
            pool.wait_ge(set_up, 2)

            def body(c, r, first, last):
                g, slot = RING * c + r, r % 2
                wait(pool, mv_done, GT * g + GT)
                wait(pool, gained, g - 1)
                settle(pool, passed)
                nc.gpsimd.tensor_scalar(rstd[:, slot, :], mv[:, slot, :, 1], LN_EPS, None, ALU.add).then_inc(var_eps, 1)
                wait(pool, var_eps, g + 1)
                nc.gpsimd.tensor_tensor(rstd[:, slot, :], rstd[:, slot, :], neg_half[:, :], ALU.pow).then_inc(rstd_done, 1)
                wait(pool, centred, g + 1)
                wait(pool, rstd_done, g + 1)
                tile, shape = cen[:, slot, SHARE:GT, :], [P, GT - SHARE, DIM]
                nc.gpsimd.tensor_tensor(tile, tile, rstd[:, slot, SHARE:GT].unsqueeze(2).to_broadcast(shape),
                                        ALU.mult).then_inc(pool_normed, 1)
                wait(pool, pool_normed, g + 1)
                nc.gpsimd.tensor_tensor(tile, tile, ln_g[:, :].unsqueeze(1).to_broadcast(shape),
                                        ALU.mult).then_inc(pool_gained, 1)
                if not (last and r >= RING - AHEAD):
                    fetch(*later(c, r, AHEAD))

            over_groups(pool, body)

        @block.scalar
        def _(act):
            def body(c, r, first, last):
                g, slot = RING * c + r, r % 2
                wait(act, negated, g + 1)
                wait(act, summed, g - 1)
                for t in range(GT):
                    ins = nc.scalar.activation(cen[:, slot, t, :], rows[:, r, t, :], ACT.Identity,
                                               bias=neg_mean[:, slot, t:t + 1])
                ins.then_inc(centred, 1)

            over_groups(act, body)

        @block.vector
        def _(dve):
            nc.vector.tensor_copy(b_parts[:, 0, :], ln_b[:, :]).then_inc(b_split, 1)
            dve.wait_ge(b_split, 1)
            nc.vector.tensor_tensor(b_rest[:, :], ln_b[:, :], b_parts[:, 0, :], ALU.subtract).then_inc(b_split, 1)
            dve.wait_ge(b_split, 2)
            nc.vector.tensor_copy(b_parts[:, 1, :], b_rest[:, :]).then_inc(b_split, 1)
            dve.wait_ge(b_split, 3)
            nc.vector.tensor_tensor(b_rest[:, :], b_rest[:, :], b_parts[:, 1, :], ALU.subtract).then_inc(b_split, 1)
            dve.wait_ge(b_split, 4)
            nc.vector.tensor_copy(b_parts[:, 2, :], b_rest[:, :]).then_inc(b_split, 1)

            def mix(c, r):
                g, slot = RING * c + r, r % 2
                wait(dve, att_in[r], 16 * 5 * (c if r < 2 else c + 1))
                nc.vector.tensor_tensor(heads[:, r, :, :], heads[:, r, :, :], inv[:, r, :, :],
                                        ALU.mult).then_inc(scaled, 1)
                wait(dve, rows_in[r], 16 * GT * (c + 1))
                for t in range(GT):
                    nc.vector.scalar_tensor_tensor(out=rows[:, r, t, :], in0=rows[:, r, t, :],
                                                   scalar=keep["weight"][:, bass.ds(GT * g + t, 1)],
                                                   in1=keep["xn"][:, bass.ds(GT * g + t, 1), :].rearrange("p a c -> p (a c)"),
                                                   op0=ALU.mult, op1=ALU.add).then_inc(mixed, 1)
                for t in range(GT):
                    wait(dve, mixed, GT * g + t + 1)
                    wait(dve, mv_done, GT * (g - 2) + t + 1)
                    nc.vector.bn_stats(stats[:, slot, t, :], rows[:, r, t, :]).then_inc(stats_done, 1)
                wait(dve, rstd_done, g - 1)
                for t in range(GT):
                    wait(dve, stats_done, GT * g + t + 1)
                    settle(dve, passed)
                    nc.vector.bn_aggr(mv[:, slot, t, :], stats[:, slot, t, :]).then_inc(mv_done, 1)
                wait(dve, mv_done, GT * g + GT)
                wait(dve, centred, g - 1)
                nc.vector.tensor_scalar(neg_mean[:, slot, :], mv[:, slot, :, 0], -1.0, None, ALU.mult).then_inc(negated, 1)

            mix(0, 0)

            def body(c, r, first, last):
                g, slot = RING * c + r, r % 2
                if not (last and r == RING - 1):
                    mix(*later(c, r, 1))
                wait(dve, rstd_done, g + 1)
                wait(dve, centred, g + 1)
                for t in range(SHARE):
                    ins = nc.vector.scalar_tensor_tensor(out=cen[:, slot, t, :], in0=cen[:, slot, t, :],
                                                         scalar=rstd[:, slot, t:t + 1], in1=ln_g[:, :],
                                                         op0=ALU.mult, op1=ALU.mult)
                ins.then_inc(gained, 1)
                wait(dve, gained, g + 1)
                wait(dve, pool_gained, g + 1)
                wait(dve, ps_ready, g + 1)
                wait(dve, stored[slot], 16 * (2 * c + r // 2))
                nc.vector.tensor_tensor(res[:, slot, :, :].rearrange("p t c -> p (t c)"), ps[:, slot, :],
                                        cen[:, slot, :, :].rearrange("p t c -> p (t c)"), ALU.add).then_inc(summed, 1)

            over_groups(dve, body)

        @block.tensor
        def _(pe):
            pe.wait_ge(set_up, 2)
            pe.wait_ge(b_split, 5)

            def body(c, r, first, last):
                g, slot = RING * c + r, r % 2
                wait(pe, scaled, g + 1)
                wait(pe, summed, g - 1)
                for t in range(GT):
                    out = ps[:, slot, t * DIM:(t + 1) * DIM]
                    toks = slice(t * P, (t + 1) * P)
                    nc.tensor.matmul(out, ident[:, :], x_in[:, r, t, :], start=True, stop=False)
                    for i in range(3):
                        nc.tensor.matmul(out, ones[0:1, :], b_parts[0:1, i, :], start=False, stop=False)
                    for k in range(2):
                        ins = nc.tensor.matmul(out, heads[:, r, k, toks], w_o[:, k, :], start=False, stop=(k == 1))
                ins.then_inc(ps_ready, 1)

            over_groups(pe, body)




def build(nc, d, phases=None):
    dram = lambda n, s, t=FP32: nc.dram_tensor(n, s, t, kind="Internal").ap()
    d = dict(d)
    d["qk_parts"] = dram("qk_parts", [3, 4, P, TOK], BF16)
    d["v_aug"] = dram("v_aug", [TOK, HEADS * VA])
    d["sorted_x"] = dram("sorted_x", [SLOTS * P, DIM])
    d["sorted_y"] = dram("sorted_y", [SLOTS * P, DIM])
    d["max_rows"] = dram("max_rows", [2, 3 * UH * QTILES, P], BF16)
    d["heads_t"] = dram("heads_t", [HEADS, VA, TOK])
    d["inv_sum"] = dram("inv_sum", [HEADS, TOK])
    with ExitStack() as ctx:
        sb = lambda n, s, t=FP32: ctx.enter_context(nc.sbuf_tensor(n, s, t))
        keep = {
            "xn": sb("keep_xn", [P, TILES, DIM]),
            "weight": sb("keep_weight", [P, TILES]),
            "place": sb("keep_place", [P, TILES], U32),
            "tile_col": sb("keep_tile_col", [P, SLOTS], I32),
        }
        keep["t_norm"] = sb("keep_t_norm", [P, TILES])
        keep["c_norm"] = sb("keep_c_norm", [P, COLS])
        keep["sim"] = sb("keep_sim", [P, TILES, COLS])
        keep["col_end"] = sb("keep_col_end", [P, COLS])
        keep["z"] = sb("keep_z", [P, TILES, COLS])
        project(nc, d, keep)
        with ExitStack() as middle:
            sb2 = lambda n, s, t=FP32: middle.enter_context(nc.sbuf_tensor(n, s, t))
            keep["q_ops"] = sb2("q_ops", [P, UNITS, UH, SEQ], BF16)
            keep["k_ops"] = sb2("k_ops", [P, UNITS, UH, SEQ], BF16)
            keep["v_ops"] = sb2("v_ops", [P, UNITS, QTILES, UH * VA])
            route(nc, d, keep)
            if phases != 1:
                attend(nc, d, keep)
        if phases is None:
            keep["ident"] = sb("keep_ident", [P, P])
            keep["w_o"] = sb("keep_w_o", [P, 2, DIM])
            keep["ln_g"] = sb("keep_ln_g", [P, DIM])
            keep["ln_b"] = sb("keep_ln_b", [P, DIM])
            keep["heads"] = sb("keep_heads", [P, RING, 2, GROUP])
            keep["inv"] = sb("keep_inv", [P, RING, 2, GROUP])
            keep["x_in"] = sb("keep_x_in", [P, RING, GT, DIM])
            columns(nc, d, keep)
            combine(nc, d, keep)


def host_layout(x):
    f = np.float32
    order = np.array([(m * 8 + h) * HD + i for m in range(2) for i in range(HD) for h in range(8)])
    inv_freq = (f(1.0) / f(10000.0) ** (np.arange(0, HD, 2, dtype=f) / f(HD))).astype(f)
    freqs = np.outer(np.arange(SEQ, dtype=f), inv_freq).astype(f)
    rows = np.arange(P) // 8 % (HD // 2)
    cos = np.cos(freqs)[:, rows].T.astype(f)
    sin = np.sin(freqs)[:, rows].T.astype(f) * np.where(np.arange(P) < P // 2, f(-1), f(1))[:, None]
    scale = np.array([1.0 / np.sqrt(HD), 1.0], f)[None, :, None]
    c = np.ascontiguousarray
    return {
        "x": c(x["L0_attn_x"].reshape(TOK, DIM)),
        "wq_t": c(x["L0_attn_Wq"][order].T), "wk_t": c(x["L0_attn_Wk"][order].T),
        "wv_t": c(x["L0_attn_Wv"].T), "wo_t": c(x["L0_attn_Wo"].T),
        "cemb_t": c(x["L0_ffn_col_emb"].T),
        "gate_w1": c(x["L0_ffn_gate_w1"]), "gate_b1": c(x["L0_ffn_gate_b1"]),
        "gate_w2": c(x["L0_ffn_gate_w2"]), "gate_b2": c(x["L0_ffn_gate_b2"]),
        "w_up": c(x["L0_ffn_W_cols"].reshape(COLS, 2, P, NEUR).transpose(0, 2, 1, 3)),
        "w_down": c(np.concatenate([x["L0_ffn_proj_w"].reshape(COLS, NEUR, DIM),
                                    x["L0_ffn_b_cols"].reshape(COLS, NEUR, 1)], axis=2)),
        "proj_b": c(x["L0_ffn_proj_b"]),
        "ln_g": c(x["L0_ffn_ln_g"]), "ln_b": c(x["L0_ffn_ln_b"]),
        "ident": np.eye(P, dtype=f),
        "rope_cos": c((cos[:, None, :] * scale).astype(f)),
        "rope_sin": c((sin[:, None, :] * scale).astype(f)),
        "col_rank": np.arange(COLS, 0, -1).astype(f),
        "tile_start": (np.arange(SLOTS) * P).astype(f),
    }


def kernel(**inputs):
    import concourse.bacc as bacc
    from concourse.bass_utils import run_bass_kernel_spmd

    arrays = host_layout({k: np.asarray(v) for k, v in inputs.items()})
    nc = bacc.Bacc("TRN2", target_bir_lowering=False, num_devices=1)
    d = {n: nc.dram_tensor(f"in_{n}", a.shape, mybir.dt.from_np(a.dtype), kind="ExternalInput").ap()
         for n, a in arrays.items()}
    d["out"] = nc.dram_tensor("out", (TOK, DIM), FP32, kind="ExternalOutput").ap()
    build(nc, d)
    r = run_bass_kernel_spmd(nc, [{f"in_{n}": a for n, a in arrays.items()}], core_ids=[0])
    return r.results[0]["out"].reshape(BATCH, SEQ, DIM)
```
